# Optimizing a Trainium2 kernel written in Bass

```python
import numpy as np
import jax
import jax.numpy as jnp

def _softmax(x, axis=-1):
    return jax.nn.softmax(x, axis=axis)

def _gelu(x):
    return jax.nn.gelu(x, approximate=True)

def _silu(x):
    return jax.nn.silu(x)

def _sigmoid(x):
    return jax.nn.sigmoid(x)

def _layernorm(x, axis=-1, eps=1e-05):
    m = jnp.mean(x, axis=axis, keepdims=True)
    v = jnp.var(x, axis=axis, keepdims=True)
    return (x - m) / jnp.sqrt(v + eps)

def _scatter_add(tgt, idx, src, axis=0):
    return tgt.at[idx].add(src)

def _segment_sum(src, seg, n):
    return jax.ops.segment_sum(src, seg, n)
kernel_name = 'mk_decoder_preln_d1_seqx_r4_3774bc'

def setup_inputs(seed: int=0):
    np.random.seed(seed)
    _w = jnp.asarray

    def _rec_inputs():
        import jax
        import jax.numpy as jnp
        _rk = jax.random.key(seed)
        x = 4.136e-05 + 0.9999 * jax.random.normal(jax.random.fold_in(_rk, 1), (4, 512, 512), jnp.float32)
        _lenS = 512 - jax.random.randint(jax.random.fold_in(_rk, 7), (4,), 0, max(1, 512 // 4) + 1, jnp.int32)
        _lenS2 = 512 - jax.random.randint(jax.random.fold_in(_rk, 8), (4,), 0, max(1, 512 // 4) + 1, jnp.int32)
        _ctx_1024P = jax.random.normal(jax.random.fold_in(_rk, 11), (4, 16, 256), jnp.float32)
        _ctx_1024c = jax.random.dirichlet(jax.random.fold_in(_rk, 511), 0.3 * jnp.ones((16,), jnp.float32), (4, 512))
        _ctx_1024t = jnp.einsum('bsk,bkd->bsd', _ctx_1024c, _ctx_1024P)
        _ctx_1024t = _ctx_1024t * jax.lax.rsqrt(jnp.mean(jnp.square(_ctx_1024t)) + 1e-12) * 0.953939
        ctx_1024 = -0.000292821 + 1.00034 * (_ctx_1024t + 0.3 * jax.random.normal(jax.random.fold_in(_rk, 611), (4, 512, 256), jnp.float32))
        return (x, ctx_1024)
    x, ctx_1024 = _rec_inputs()

    def _L0_attn_setup():
        import jax, jax.numpy as jnp
        import numpy as np
        import math
        D = 512
        NH = 16
        HD = D // NH

        def rotary_apply(x, cos, sin):
            d = x.shape[-1]
            x1, x2 = (x[..., :d // 2], x[..., d // 2:])
            c, s = (cos[..., :d // 2], sin[..., :d // 2])
            return jnp.concatenate([x1 * c - x2 * s, x2 * c + x1 * s], axis=-1)
        key = jax.random.key(seed)
        k1, k2, k3 = jax.random.split(key, 3)
        x = jax.random.normal(k1, (2, 512, D), dtype=jnp.float32)
        w_qkv = jax.random.normal(k2, (D, 3 * D), dtype=jnp.float32) * (1.0 / math.sqrt(D))
        w_o = jax.random.normal(k3, (D, D), dtype=jnp.float32) * (1.0 / math.sqrt(D))
        return {'x': x, 'w_qkv': w_qkv, 'w_o': w_o}
    _L0_attn_all = _L0_attn_setup()
    _L0_attn_in = {k: v for k, v in _L0_attn_all.items() if k in ('w_qkv', 'w_o')}
    del _L0_attn_all

    def _L0_xattn_setup():
        import jax, jax.numpy as jnp
        import numpy as np
        import math
        B, L, DM = (2, 512, 256)
        DS, DC, EXP = (16, 4, 2)
        DI = EXP * DM
        DR = math.ceil(DM / 16)
        DT_MIN, DT_MAX, DT_FLOOR = (0.001, 0.1, 0.0001)

        def _ssm_forward(hidden_states, z, in_proj_w, conv_w, conv_b, x_proj_w, dt_proj_w, dt_proj_b, A_log, D):
            b = hidden_states.shape[0]
            x = jnp.einsum('ed,bld->bel', in_proj_w, hidden_states)
            xp = jnp.pad(x, ((0, 0), (0, 0), (DC - 1, 0)))
            xc = jax.lax.conv_general_dilated(xp, conv_w[:, None, :], window_strides=(1,), padding='VALID', dimension_numbers=('NCH', 'OIH', 'NCH'), feature_group_count=DI)
            u = jax.nn.silu(xc + conv_b[None, :, None])
            x_dbl = jnp.einsum('ke,bel->bkl', x_proj_w, u)
            dt_lo = x_dbl[:, :DR]
            Bm = x_dbl[:, DR:DR + DS]
            Cm = x_dbl[:, DR + DS:]
            delta = jax.nn.softplus(jnp.einsum('er,brl->bel', dt_proj_w, dt_lo) + dt_proj_b[None, :, None])
            A = -jnp.exp(A_log)

            def step(state, xs):
                d_t, B_t, C_t, u_t = xs
                dA = jnp.exp(d_t[..., None] * A)
                state = state * dA + (d_t * u_t)[..., None] * B_t[:, None, :]
                y_t = jnp.einsum('ben,bn->be', state, C_t)
                return (state, y_t)
            xs = (jnp.moveaxis(delta, -1, 0), jnp.moveaxis(Bm, -1, 0), jnp.moveaxis(Cm, -1, 0), jnp.moveaxis(u, -1, 0))
            state0 = jnp.zeros((b, DI, DS), delta.dtype)
            _, ys = jax.lax.scan(step, state0, xs)
            y = jnp.moveaxis(ys, 0, -1)
            y = y + D[None, :, None] * u
            y = y * jax.nn.silu(z)
            return jnp.swapaxes(y, 1, 2)
        key = jax.random.key(seed)
        ks = jax.random.split(key, 8)
        hidden_states = jax.random.normal(ks[0], (B, L, DM), jnp.float32)
        z = jax.random.normal(ks[1], (B, DI, L), jnp.float32)
        in_proj_w = jax.random.normal(ks[2], (DI, DM), jnp.float32) * DM ** (-0.5)
        conv_w = jax.random.normal(ks[3], (DI, DC), jnp.float32) * DC ** (-0.5)
        conv_b = jnp.zeros((DI,), jnp.float32)
        x_proj_w = jax.random.normal(ks[4], (DR + 2 * DS, DI), jnp.float32) * DI ** (-0.5)
        dt_std = DR ** (-0.5)
        dt_proj_w = jax.random.uniform(ks[5], (DI, DR), jnp.float32, -dt_std, dt_std)
        dt = jnp.exp(jax.random.uniform(ks[6], (DI,), jnp.float32) * (math.log(DT_MAX) - math.log(DT_MIN)) + math.log(DT_MIN))
        dt = jnp.clip(dt, DT_FLOOR)
        dt_proj_b = dt + jnp.log(-jnp.expm1(-dt))
        A_log = jnp.log(jnp.broadcast_to(jnp.arange(1, DS + 1, dtype=jnp.float32), (DI, DS)))
        D = jnp.ones((DI,), jnp.float32)
        return dict(hidden_states=hidden_states, z=z, in_proj_w=in_proj_w, conv_w=conv_w, conv_b=conv_b, x_proj_w=x_proj_w, dt_proj_w=dt_proj_w, dt_proj_b=dt_proj_b, A_log=A_log, D=D)
    _L0_xattn_all = _L0_xattn_setup()
    _L0_xattn_in = {k: v for k, v in _L0_xattn_all.items() if k in ('in_proj_w', 'conv_w', 'conv_b', 'x_proj_w', 'dt_proj_w', 'dt_proj_b', 'A_log', 'D')}
    del _L0_xattn_all

    def _L0_ffn_setup():
        import jax, jax.numpy as jnp
        import numpy as np
        EPS = 1e-06
        Q_B = 128.0

        def layer_norm(x):
            mean = jnp.mean(x, axis=-1, keepdims=True)
            var = jnp.var(x, axis=-1, keepdims=True)
            return (x - mean) / jnp.sqrt(var + EPS)

        def absmax_quant(x):
            gamma = jnp.max(jnp.abs(x), axis=-1, keepdims=True)
            x_hat = jnp.clip(x * Q_B / gamma, -Q_B + EPS, Q_B - EPS)
            return x_hat * gamma / Q_B

        def ternarize_weights(w):
            gamma = jnp.mean(jnp.abs(w))
            return jnp.sign(jnp.round(w / (gamma + EPS))) * gamma

        def bitlinear(x, w):
            xn = layer_norm(x)
            x_hat = xn + jax.lax.stop_gradient(absmax_quant(xn) - xn)
            w_hat = w + jax.lax.stop_gradient(ternarize_weights(w) - w)
            return jnp.einsum('bsd,od->bso', x_hat, w_hat)
        key = jax.random.key(seed)
        k1, k2, k3 = jax.random.split(key, 3)
        B, S, D = (4, 512, 512)
        x = jax.random.normal(k1, (B, S, D), dtype=jnp.float32)
        w_fc = jax.random.normal(k2, (4 * D, D), dtype=jnp.float32) / np.sqrt(D)
        w_proj = jax.random.normal(k3, (D, 4 * D), dtype=jnp.float32) / np.sqrt(4 * D)
        return {'x': x, 'w_fc': w_fc, 'w_proj': w_proj}
    _L0_ffn_all = _L0_ffn_setup()
    _L0_ffn_in = {k: v for k, v in _L0_ffn_all.items() if k in ('w_fc', 'w_proj')}
    del _L0_ffn_all
    return {'x': x, 'ctx_1024': ctx_1024, 'L0_attn_w_qkv': _L0_attn_in['w_qkv'], 'L0_attn_w_o': _L0_attn_in['w_o'], 'L0_xattn_in_proj_w': _L0_xattn_in['in_proj_w'], 'L0_xattn_conv_w': _L0_xattn_in['conv_w'], 'L0_xattn_conv_b': _L0_xattn_in['conv_b'], 'L0_xattn_x_proj_w': _L0_xattn_in['x_proj_w'], 'L0_xattn_dt_proj_w': _L0_xattn_in['dt_proj_w'], 'L0_xattn_dt_proj_b': _L0_xattn_in['dt_proj_b'], 'L0_xattn_A_log': _L0_xattn_in['A_log'], 'L0_xattn_D': _L0_xattn_in['D'], 'L0_ffn_w_fc': _L0_ffn_in['w_fc'], 'L0_ffn_w_proj': _L0_ffn_in['w_proj']}

def reference(x, ctx_1024, L0_attn_w_qkv, L0_attn_w_o, L0_xattn_in_proj_w, L0_xattn_conv_w, L0_xattn_conv_b, L0_xattn_x_proj_w, L0_xattn_dt_proj_w, L0_xattn_dt_proj_b, L0_xattn_A_log, L0_xattn_D, L0_ffn_w_fc, L0_ffn_w_proj):
    import jax
    import jax.numpy as jnp

    def _L0_attn_ref(x, w_qkv, w_o):
        import jax, jax.numpy as jnp
        import numpy as np
        import math
        D = 512
        NH = 16
        HD = D // NH

        def rotary_apply(x, cos, sin):
            d = x.shape[-1]
            x1, x2 = (x[..., :d // 2], x[..., d // 2:])
            c, s = (cos[..., :d // 2], sin[..., :d // 2])
            return jnp.concatenate([x1 * c - x2 * s, x2 * c + x1 * s], axis=-1)
        B, T, _ = x.shape
        qkv = (x @ w_qkv).reshape(B, T, 3, NH, HD)
        q, k, v = (qkv[:, :, 0], qkv[:, :, 1], qkv[:, :, 2])
        inv_freq = 1.0 / 10000.0 ** (jnp.arange(0, HD, 2, dtype=jnp.float32) / HD)
        t = jnp.arange(T, dtype=jnp.float32)
        freqs = jnp.outer(t, inv_freq)
        emb = jnp.concatenate([freqs, freqs], axis=-1)
        cos = jnp.cos(emb)[None, None]
        sin = jnp.sin(emb)[None, None]
        q = rotary_apply(jnp.transpose(q, (0, 2, 1, 3)), cos, sin)
        k = rotary_apply(jnp.transpose(k, (0, 2, 1, 3)), cos, sin)
        v = jnp.transpose(v, (0, 2, 1, 3))
        scores = jnp.einsum('bhqd,bhkd->bhqk', q, k) / math.sqrt(HD)
        causal = jnp.tril(jnp.ones((T, T), dtype=bool))
        scores = jnp.where(causal, scores, -jnp.inf)
        attn = jax.nn.softmax(scores, axis=-1)
        out = jnp.einsum('bhqk,bhkd->bhqd', attn, v)
        out = jnp.transpose(out, (0, 2, 1, 3)).reshape(B, T, D)
        return out @ w_o

    def _L0_xattn_ref(hidden_states, z, in_proj_w, conv_w, conv_b, x_proj_w, dt_proj_w, dt_proj_b, A_log, D):
        import jax, jax.numpy as jnp
        import numpy as np
        import math
        B, L, DM = (2, 512, 256)
        DS, DC, EXP = (16, 4, 2)
        DI = EXP * DM
        DR = math.ceil(DM / 16)
        DT_MIN, DT_MAX, DT_FLOOR = (0.001, 0.1, 0.0001)

        def _ssm_forward(hidden_states, z, in_proj_w, conv_w, conv_b, x_proj_w, dt_proj_w, dt_proj_b, A_log, D):
            b = hidden_states.shape[0]
            x = jnp.einsum('ed,bld->bel', in_proj_w, hidden_states)
            xp = jnp.pad(x, ((0, 0), (0, 0), (DC - 1, 0)))
            xc = jax.lax.conv_general_dilated(xp, conv_w[:, None, :], window_strides=(1,), padding='VALID', dimension_numbers=('NCH', 'OIH', 'NCH'), feature_group_count=DI)
            u = jax.nn.silu(xc + conv_b[None, :, None])
            x_dbl = jnp.einsum('ke,bel->bkl', x_proj_w, u)
            dt_lo = x_dbl[:, :DR]
            Bm = x_dbl[:, DR:DR + DS]
            Cm = x_dbl[:, DR + DS:]
            delta = jax.nn.softplus(jnp.einsum('er,brl->bel', dt_proj_w, dt_lo) + dt_proj_b[None, :, None])
            A = -jnp.exp(A_log)

            def step(state, xs):
                d_t, B_t, C_t, u_t = xs
                dA = jnp.exp(d_t[..., None] * A)
                state = state * dA + (d_t * u_t)[..., None] * B_t[:, None, :]
                y_t = jnp.einsum('ben,bn->be', state, C_t)
                return (state, y_t)
            xs = (jnp.moveaxis(delta, -1, 0), jnp.moveaxis(Bm, -1, 0), jnp.moveaxis(Cm, -1, 0), jnp.moveaxis(u, -1, 0))
            state0 = jnp.zeros((b, DI, DS), delta.dtype)
            _, ys = jax.lax.scan(step, state0, xs)
            y = jnp.moveaxis(ys, 0, -1)
            y = y + D[None, :, None] * u
            y = y * jax.nn.silu(z)
            return jnp.swapaxes(y, 1, 2)
        return _ssm_forward(hidden_states, z, in_proj_w, conv_w, conv_b, x_proj_w, dt_proj_w, dt_proj_b, A_log, D)

    def _L0_ffn_ref(x, w_fc, w_proj):
        import jax, jax.numpy as jnp
        import numpy as np
        EPS = 1e-06
        Q_B = 128.0

        def layer_norm(x):
            mean = jnp.mean(x, axis=-1, keepdims=True)
            var = jnp.var(x, axis=-1, keepdims=True)
            return (x - mean) / jnp.sqrt(var + EPS)

        def absmax_quant(x):
            gamma = jnp.max(jnp.abs(x), axis=-1, keepdims=True)
            x_hat = jnp.clip(x * Q_B / gamma, -Q_B + EPS, Q_B - EPS)
            return x_hat * gamma / Q_B

        def ternarize_weights(w):
            gamma = jnp.mean(jnp.abs(w))
            return jnp.sign(jnp.round(w / (gamma + EPS))) * gamma

        def bitlinear(x, w):
            xn = layer_norm(x)
            x_hat = xn + jax.lax.stop_gradient(absmax_quant(xn) - xn)
            w_hat = w + jax.lax.stop_gradient(ternarize_weights(w) - w)
            return jnp.einsum('bsd,od->bso', x_hat, w_hat)
        h = bitlinear(x, w_fc)
        h = jax.nn.gelu(h, approximate=False)
        return bitlinear(h, w_proj)
    x = x + _L0_attn_ref(_layernorm(x, axis=-1), L0_attn_w_qkv, L0_attn_w_o)
    x = x + _L0_xattn_ref(ctx_1024, _layernorm(x, axis=-1), L0_xattn_in_proj_w, L0_xattn_conv_w, L0_xattn_conv_b, L0_xattn_x_proj_w, L0_xattn_dt_proj_w, L0_xattn_dt_proj_b, L0_xattn_A_log, L0_xattn_D)
    x = x + _L0_ffn_ref(_layernorm(x, axis=-1), L0_ffn_w_fc, L0_ffn_w_proj)
    return x

_drawn_inputs = setup_inputs


def setup_inputs(seed=0):
    import zlib

    import numpy as np

    out = dict(_drawn_inputs(seed))
    spreads = {'L0_xattn_conv_b': (0.0, 0.1), 'L0_xattn_D': (1.0, 0.2)}
    factors = {'L0_xattn_dt_proj_w': 5.392}
    for name, (base, spread) in spreads.items():
        noise = np.random.default_rng([zlib.crc32(name.encode()), seed]).standard_normal(out[name].shape)
        drawn = base * np.exp(spread * noise) if base else spread * noise
        out[name] = jnp.asarray(drawn.astype(out[name].dtype))
    for name, factor in factors.items():
        out[name] = (out[name] * factor).astype(out[name].dtype)
    return out
```

```python
from contextlib import ExitStack

import concourse.bass as bass
from concourse import mybir

F32 = mybir.dt.float32
F32R = mybir.dt.float32r
BF16 = mybir.dt.bfloat16
ALU = mybir.AluOpType
ACT = mybir.ActivationFunctionType
AX = mybir.AxisListType

P = 128
B, L, DM = 4, 512, 512
NH, HD = 16, 32
HALF = HD // 2
DC, DS, DR, TAPS = 256, 16, 16, 4
FF = 4 * DM
LT = L // P
ET = DM // P
KD = DM // P
KC = DC // P
FT = FF // P
SCALE = float(HD) ** -0.5
EPS = 1e-5
EPS_Q = 1e-6
Q_B = 128.0
MASKED = -1e30

SLOTS = B * 8
SUBS = 4
CH = 256
XF = 5

P_AT = [0, 512, 1024, 896]
P_W = 1280


def schedule():
    chunk = [0]

    def used():
        chunk[0] += 1
        return chunk[0] - 1

    def release(c):
        return ("wload", c + 2)

    def qk(b, n):
        c = used()
        yield ("rot", b, n, c)
        yield release(c)

    out = [("wload", 0), ("wload", 1), ("xload", 0, 0), ("xload", 0, 1), ("cload", 0)]
    for t in (0, 1):
        out += [("ln1a", 0, t)]
    for et in range(ET):
        out += [("inproj", 0, et)]
    out += [("ln1b", 0, 0), ("ln1b", 0, 1), ("xload", 0, 2), ("xload", 0, 3), ("xproj", 0)]
    out += [("bcload", 0, 0, k) for k in range(SUBS)]
    out += [("ln1a", 0, 2), ("ln1a", 0, 3), ("ln1b", 0, 2), ("ln1b", 0, 3)]
    out += [("dt", 0, 0), ("delta", 0, 0)]
    for n in range(4):
        out += list(qk(0, n))
        out += [("lo", 0, n)]
        if n == 1:
            out += [("stack", 0)]
    out += [("dt", 0, 1), ("delta", 0, 1), ("dt", 0, 2), ("delta", 0, 2)]
    c = used()
    out += [("v", 0, 0, 0, c), ("v", 0, 0, 1, c), release(c)]
    out += [("exp", 0), ("dbu", 0)]

    for s in range(SLOTS + 1):
        b, sb = divmod(s, 8)
        main, more, post = s < SLOTS, b + 1 < B and s < SLOTS, b > 0
        nb, pb = b + 1, b - 1
        for k in range(SUBS):
            j = SUBS * s + k
            if main:
                if j + 1 < SUBS * SLOTS:
                    out += [("exp", j + 1), ("dbu", j + 1)]
                out += [("scan", j)]
            if k == 0:
                if s + 1 < SLOTS:
                    out += [("stack", s + 1)]
                if s > 0:
                    out += [("pv", s - 1)]
                if main:
                    out += [("s", s, 0)]
            if main and k == 1:
                out += [("s", s, 1), ("s", s, 2)]
            if main and k == 2:
                out += [("s", s, 3), ("s", s, 4)]
            if main and k == 3:
                out += [("mt", s)] + [("t", s, u) for u in range(5)]
            if main:
                out += [("ch", j)]
                if j > 0:
                    out += [("y", j - 1)]
                    if k == 0:
                        out += [("yacc", s - 1)]
                if sb % 4 == 3:
                    half = sb // 4
                    if half == 0:
                        out += [("bcload", b, 1, k)]
                    elif nb < B:
                        out += [("bcload", nb, 0, k)]
            elif k == 0:
                out += [("y", j - 1), ("yacc", s - 1)]
            if k == 1 and s > 0 and s % 2 == 0:
                out += [("norm", s // 2 - 1)]
            at = (sb, k)
            if main:
                if at == (0, 0):
                    out += [("dt", b, 3), ("delta", b, 3)]
                    vc = used()
                    out += [("v", b, 1, 0, vc)]
                if at == (0, 1):
                    out += [("v", b, 1, 1, vc), release(vc)]
            if post and s <= SLOTS:
                if at == (0, 0):
                    out += [("resid", pb)]
                if at == (0, 2):
                    wc = used(), used()
                    out += [("wo", pb, 0, *wc), ("wo", pb, 1, *wc)]
                if at == (0, 3):
                    out += [("wo", pb, 2, *wc), ("wo", pb, 3, *wc), release(wc[0]), release(wc[1]), ("ln2a", pb)]
            steps = {}
            if post:
                steps[1, 1] = [("ln2b", pb)]
                steps[1, 2] = [("gate", pb, et) for et in range(ET)]
                steps[3, 2] = [("yt", pb, 0)]
                steps[4, 0] = [("yt", pb, 1)]
                steps[4, 3] = [("yt", pb, 2)]
                steps[5, 2] = [("yt", pb, 3), ("x2store", pb)]
            if s == SLOTS and k == 3:
                for at in sorted(steps):
                    out += steps[at]
            elif main:
                out += steps.get(at, [])
            if more:
                out += {
                    (0, 3): [("xload", nb, 0), ("xload", nb, 1), ("cload", nb)],
                    (1, 3): [("ln1a", nb, 0), ("ln1a", nb, 1)],
                    (2, 0): [("ln1b", nb, 0), ("xload", nb, 2)],
                    (2, 1): [("ln1b", nb, 1), ("xload", nb, 3)],
                    (2, 2): [("ln1a", nb, 2)],
                    (2, 3): [("ln1a", nb, 3)],
                    (3, 0): [("ln1b", nb, 2), ("inproj", nb, 0)],
                    (3, 1): [("ln1b", nb, 3)],
                    (3, 3): list(qk(nb, 0)) if at == (3, 3) else [],
                    (4, 0): [("lo", nb, 0), ("inproj", nb, 1)],
                    (4, 1): list(qk(nb, 1)) if at == (4, 1) else [],
                    (4, 2): [("lo", nb, 1), ("inproj", nb, 2)],
                    (5, 0): [("inproj", nb, 3)],
                    (5, 1): list(qk(nb, 2)) if at == (5, 1) else [],
                    (5, 2): [("lo", nb, 2)],
                    (5, 3): [("xproj", nb)],
                    (6, 0): list(qk(nb, 3)) if at == (6, 0) else [],
                    (6, 1): [("lo", nb, 3)],
                    (6, 2): [("dt", nb, 0), ("delta", nb, 0)],
                    (7, 0): [("dt", nb, 1), ("delta", nb, 1)],
                    (7, 1): [("dt", nb, 2), ("delta", nb, 2)],
                }.get(at, [])
                if at == (6, 1):
                    vc = used()
                    out += [("v", nb, 0, 0, vc)]
                if at == (6, 3):
                    out += [("v", nb, 0, 1, vc), release(vc)]
    chunks = chunk[0]
    return [x for x in out if not (x[0] == "wload" and x[1] >= chunks)]


SCHEDULE = schedule()


def chunk_contents():
    found = {}
    for kind, *a in SCHEDULE:
        if kind == "rot":
            found[a[2]] = a[1]
        if kind == "v":
            found[a[3]] = 4 + a[1]
        if kind == "wo":
            found[a[2]], found[a[3]] = 6, 7
    return found


CHUNK = chunk_contents()


def bank_tasks():
    emptied_by = {"ln1b": "act", "inproj": "act", "xproj": "act", "dt": "act", "v": "act",
                  "rot": "dve", "wo": "dve", "yt": "dve"}
    tasks, freed, count = {}, [], {"act": 0, "dve": 0}
    for item in SCHEDULE:
        who = emptied_by.get(item[0])
        if who:
            tasks[item[:3] if item[0] != "v" else item[:4]] = len(freed)
            for _ in range(2 if item[0] == "rot" else 1):
                count[who] += 1
                freed.append((who, count[who]))
    return tasks, freed


TASK, FREED = bank_tasks()
SCRATCH = {x[:3]: n for n, x in enumerate(x for x in SCHEDULE if x[0] in ("rot", "dt"))}


def scratch_after(item):
    return SCRATCH[item] + 1


def layer_kernel(nc, t_in, out):
    sems = {}
    with ExitStack() as ctx:
        base = [(nc.sbuf_base + 31) // 32 * 32]

        def sb(name, shape, dt=F32):
            size = 4 if dt in (F32, F32R) else 2
            n = size
            for d in shape[1:]:
                n *= d
            at = base[0]
            base[0] += (n + 31) // 32 * 32
            assert base[0] <= nc.sbuf_usable_end, (name, base[0], nc.sbuf_usable_end)
            return nc.alloc_sbuf_tensor_at(name, shape, dt, offset=at)

        def sem(name):
            sems[name] = ctx.enter_context(nc.semaphore(name))
            return sems[name]

        ident = sb("ident", [P, P])
        ones = sb("ones", [P, P])
        neg_half = sb("neg_half", [P, 4])
        phase_base = base[0]

        ident_b = sb("ident_b", [P, P], BF16)
        mask_qk = sb("mask_qk", [P, P], BF16)
        mask_kq = sb("mask_kq", [P, P], BF16)
        pick = sb("pick", [2, 2, P], F32R)
        pick_f = sb("pick_f", [2, 2, P])
        cos = sb("cos", [P, L])
        sin = sb("sin", [P, L])
        in_w = sb("in_w", [P, KC, DM])
        xp_w = sb("xp_w", [P, ET, DR + 2 * DS])
        dt_w = sb("dt_w", [DR, DM])
        small = sb("small", [P, ET, TAPS + 3 + DS])
        conv_w = small[:, :, 0:TAPS]
        conv_b = small[:, :, TAPS:TAPS + 1]
        dt_b = small[:, :, TAPS + 1:TAPS + 2]
        d_skip = small[:, :, TAPS + 2:TAPS + 3]
        a_log = small[:, :, TAPS + 3:]
        a_neg = sb("a_neg", [P, ET, DS])
        x_in = sb("x_in", [P, 2, DM])
        stats = sb("stats", [P, 2, 6])
        mv = sb("mv", [P, 2, 2])
        rstd = sb("rstd", [P, 2, 1])
        xn_t = sb("xn_t", [P, KD, L])
        w_ring = sb("w_ring", [P, 2, KD, CH])
        ctx_in = sb("ctx_in", [P, KC, L])
        x_pad = sb("x_pad", [P, 520])
        u = sb("u", [P, ET, L])
        delta = sb("delta", [P, ET, L])
        du = sb("du", [P, ET, L])
        b_bc = sb("b_bc", [P, 8, L])
        c_bc = sb("c_bc", [P, 8, L])
        da = sb("da", [P, 2, 2, L])
        hb = sb("hb", [P, 3, 2, L])
        y_acc = sb("y_acc", [P, 2, ET, L])
        x_dbl = sb("x_dbl", [DR + 2 * DS, L])
        tmp = sb("tmp", [P, 3, L])
        hl = sb("hl", [P, 4, L], F32R)
        v_sb = sb("v_sb", [P, LT, DM])
        q_st = sb("q_st", [P, 2, 2, L], F32R)
        k_st = sb("k_st", [P, 2, 2, L], F32R)
        p_t = sb("p_t", [P, 2, P_W])
        m_col = sb("m_col", [P, LT, 2])
        m_row = sb("m_row", [2, L], F32R)
        o_t = sb("o_t", [P, ET, L])
        xr = sb("xr", [P, LT, DM])
        stats2 = sb("stats2", [P, LT, 6])
        mv2 = sb("mv2", [P, LT, 2])
        ve2 = sb("ve2", [P, LT])
        rstd2 = sb("rstd2", [P, LT])
        nmr2 = sb("nmr2", [P, LT])
        gate = sb("gate", [P, L])

        base[0] = phase_base
        stage = sb("stage", [P, 2, KD * FF])
        low = sb("low", [P, 2, FF], BF16)
        t_fc = sb("t_fc", [P, KD, FF], F32R)
        t_pr = sb("t_pr", [P, FT, DM], F32R)
        w_sum = sb("w_sum", [P, 2])
        gam = sb("gam", [P, 2])
        thr = sb("thr", [P, 2])
        nthr = sb("nthr", [P, 2])
        base[0] -= 0
        act_base = phase_base
        end = base[0]
        base[0] = act_base
        xf = sb("xf", [P, XF, DM])
        xq = sb("xq", [P, 2, DM])
        fx = sb("fx", [P, 2, 16])
        st_x = sb("st_x", [P, 2, 6])
        xq_hi = sb("xq_hi", [P, 2, KD, P], F32R)
        xq_lo = sb("xq_lo", [P, 2, KD, P], F32R)
        h_sb = sb("h_sb", [P, 2, FF])
        fh = sb("fh", [P, 2, 16])
        st_h = sb("st_h", [P, 2, 4, 6])
        hq_hi = sb("hq_hi", [P, FT, P], F32R)
        hq_lo = sb("hq_lo", [P, FT, P], F32R)
        y_out = sb("y_out", [P, 2, DM])
        assert base[0] <= phase_base + 2 * KD * FF * 4

        ps = ctx.enter_context(nc.psum_tensor("ps", [P, 8, 512], F32))
        M = [ps[:, 0, :], ps[:, 1, :]]
        S_B = ps[:, 2, :]
        T_B = [ps[:, 3, :], ps[:, 4, :]]
        O_B, Z_B = ps[:, 5, :], ps[:, 6, :]
        Y_B = ps[:, 7, :]

        qk_d = nc.dram_tensor("qk_d", [B, 2, NH, 4, HALF, L], F32, kind="Internal").ap()
        bc_d = nc.dram_tensor("bc_d", [B, 2 * DS, L], F32, kind="Internal").ap()
        x2_d = nc.dram_tensor("x2_d", [B, LT, P, DM], F32, kind="Internal").ap()

        consts_in = sem("consts_in")
        w_in = [sem(f"w_in{i}") for i in range(2)]
        x_in_s = [sem(f"x_in{i}") for i in range(2)]
        ctx_in_s = sem("ctx_in_s")
        stack_in = [sem(f"stack_in{i}") for i in range(2)]
        bc_in = [sem(f"bc_in{i}") for i in range(SUBS)]
        resid_in = sem("resid_in")
        hl_stored = sem("hl_stored")
        bc_stored = sem("bc_stored")
        x2_stored = sem("x2_stored")
        pool_set = sem("pool_set")
        a_exp = sem("a_exp")
        a_ready = sem("a_ready")
        pick_ready = sem("pick_ready")
        m_full = sem("m_full")
        m_free = {"act": sem("m_free_act"), "dve": sem("m_free_dve")}
        ln1_var = sem("ln1_var")
        ln1_rstd = sem("ln1_rstd")
        ln1_done = sem("ln1_done")
        conv_done = sem("conv_done")
        u_ready = sem("u_ready")
        sp_ready = sem("sp_ready")
        delta_ready = sem("delta_ready")
        du_ready = sem("du_ready")
        scratch_free = sem("scratch_free")
        rot_done = sem("rot_done")
        hi_ready = sem("hi_ready")
        da_ready = sem("da_ready")
        dbu_ready = sem("dbu_ready")
        scan_done = sem("scan_done")
        ch_done = sem("ch_done")
        y_done = sem("y_done")
        yacc_done = sem("yacc_done")
        s_full = sem("s_full")
        max_done = sem("max_done")
        m_row_ready = sem("m_row_ready")
        t_full = sem("t_full")
        p_ready = sem("p_ready")
        pv_done = sem("pv_done")
        norm_done = sem("norm_done")
        ln2_var = sem("ln2_var")
        ln2_rstd = sem("ln2_rstd")
        ln2_ready = sem("ln2_ready")
        gate_ready = sem("gate_ready")
        gated = sem("gated")
        act_own = sem("act_own")
        dve_own = sem("dve_own")
        fw_in = [sem("fw_in0"), sem("fw_in1")]
        wsum_ready = sem("wsum_ready")
        wsum_act = sem("wsum_act")
        wtot_full = sem("wtot_full")
        tern_done = sem("tern_done")
        xf_in = [sem(f"xf_in{i}") for i in range(XF)]
        fx_var = sem("fx_var")
        fx_pow = sem("fx_pow")
        xq_done = sem("xq_done")
        tr_full = sem("tr_full")
        tr_hi = sem("tr_hi")
        tr_free = sem("tr_free")
        fc_full = sem("fc_full")
        gelu_done = sem("gelu_done")
        fh_var = sem("fh_var")
        fh_pow = sem("fh_pow")
        fh_nmr = sem("fh_nmr")
        hn_done = sem("hn_done")
        hq_done = sem("hq_done")
        proj_full = sem("proj_full")
        y_ready = sem("y_ready")
        y_stored = [sem("y_stored0"), sem("y_stored1")]

        CONSTS = [
            (ident, t_in["ident"]), (pick_f, t_in["pick"]), (in_w, t_in["in_w"]), (small, t_in["small"]),
            (xp_w, t_in["xp_w"]), (dt_w, t_in["dt_w"]), (cos, t_in["cos"]), (sin, t_in["sin"]),
        ]
        ALL_CONSTS = 16 * len(CONSTS)

        def sub(j):
            return j // 32, j // 16 % 2, j // 4 % 4, j % 4

        def freed(eng, n):
            if n >= 2:
                who, count = FREED[n - 2]
                eng.wait_ge(m_free[who], count)

        def emptied(eng, n):
            who, count = FREED[n]
            eng.wait_ge(m_free[who], count)

        class Own:

            def __init__(self, eng, s):
                self.eng, self.s, self.n = eng, s, 0

            def done(self, ins):
                ins.then_inc(self.s, 1)
                self.n += 1

            def settle(self):
                self.eng.wait_ge(self.s, self.n)

        S_UNITS = [[(0, 3, 0)], [(0, 2, 0), (0, 0, 384)], [(1, 3, 0)], [(1, 2, 0), (1, 0, 384)],
                   [(0, 1, 0), (1, 1, 256)]]
        T_UNITS = [[(0, 0, 0)], [(0, 1, 0), (0, 3, 384)], [(1, 0, 0)], [(1, 1, 0), (1, 3, 384)],
                   [(0, 2, 0), (1, 2, 256)]]

        block = ctx.enter_context(nc.Block())

        @block.sync
        def _(sp):
            for dst, src in CONSTS:
                sp.dma_start(dst[:], src).then_inc(consts_in, 16)

            for kind, *a in SCHEDULE:
                if kind == "wload":
                    c, = a
                    if c >= 2:
                        user = max(TASK[x[:4] if x[0] == "v" else x[:3]] + (x[0] == "rot")
                                   for x in SCHEDULE
                                   if (x[0] == "rot" and x[3] == c - 2) or (x[0] == "v" and x[4] == c - 2)
                                   or (x[0] == "wo" and c - 2 in x[3:]))
                        sp.wait_ge(m_full, user + 1)
                    sp.dma_start(w_ring[:, c % 2], t_in["w_attn"][CHUNK[c]]).then_inc(w_in[c % 2], 16)
                elif kind == "xload":
                    b, t = a
                    i = LT * b + t
                    if i >= 2:
                        sp.wait_ge(m_full, TASK["ln1b", (i - 2) // LT, (i - 2) % LT] + 1)
                    sp.dma_start(x_in[:, i % 2], t_in["x"][b, t]).then_inc(x_in_s[i % 2], 16)
                elif kind == "cload":
                    b, = a
                    if b:
                        sp.wait_ge(m_full, TASK["inproj", b - 1, ET - 1] + 1)
                    sp.dma_start(ctx_in[:], t_in["ctx"][b]).then_inc(ctx_in_s, 16)
                elif kind == "lo":
                    b, n = a
                    sp.wait_ge(scratch_free, scratch_after(("rot", b, n)))
                    for part in range(4):
                        heads = qk_d[b, n % 2, 8 * (n // 2):8 * (n // 2) + 8, part]
                        sp.dma_start(heads, hl[:, part, :].bitcast(F32)).then_inc(hl_stored, 16)
                elif kind == "xproj":
                    b, = a
                    emptied(sp, TASK["xproj", b])
                    sp.dma_start(bc_d[b], x_dbl[DR:DR + 2 * DS, :]).then_inc(bc_stored, 16)
                elif kind == "bcload":
                    b, half, k = a
                    sp.wait_ge(bc_stored, 16 * (b + 1))
                    n = 2 * b + half
                    if n:
                        sp.wait_ge(ch_done, 16 * (n - 1) + 12 + k + 1)
                    for tile, row in ((b_bc, 0), (c_bc, DS)):
                        r = row + 8 * half + 2 * k
                        src = bc_d[b, r:r + 2, :].rearrange("a n -> (a n)").partition_broadcast(P)
                        sp.dma_start(tile[:, 2 * k:2 * k + 2, :].rearrange("p a n -> p (a n)"), src)\
                            .then_inc(bc_in[k], 16)
                elif kind == "stack":
                    p, = a
                    b, sb_ = divmod(p, 8)
                    sp.wait_ge(hl_stored, 64 * (4 * b + 2 * (sb_ // 4) + 2))
                    if p >= 2:
                        sp.wait_ge(t_full, 5 * (p - 1))
                    for h in range(2):
                        head = 2 * sb_ + h
                        q = qk_d[b, 0, head].rearrange("s p n -> (s p) n")
                        k = qk_d[b, 1, head].rearrange("s p n -> (s p) n")
                        for dst, rows, src in ((q_st, (0, 64), q), (q_st, (64, 128), q), (k_st, (0, 64), k),
                                               (k_st, (64, 96), k[32:64]), (k_st, (96, 128), k[0:32])):
                            sp.dma_start(dst[rows[0]:rows[1], p % 2, h, :].bitcast(F32), src).then_inc(stack_in[p % 2], 16)
                elif kind == "resid":
                    b, = a
                    if b:
                        sp.wait_ge(x2_stored, 16 * b)
                    sp.dma_start(xr[:], t_in["x"][b].rearrange("t p n -> p t n")).then_inc(resid_in, 16)
                elif kind == "x2store":
                    b, = a
                    emptied(sp, TASK["yt", b, ET - 1])
                    sp.dma_start(x2_d[b].rearrange("t p n -> p t n"), xr[:]).then_inc(x2_stored, 16)

            sp.wait_ge(x2_stored, 16 * B)
            sp.wait_ge(y_done, SUBS * SLOTS)
            sp.wait_ge(p_ready, 5 * SLOTS)
            sp.wait_ge(norm_done, SLOTS // 2)
            sp.wait_ge(gated, B * ET)
            for n, w in enumerate(("w_fc", "w_pr")):
                sp.dma_start(stage[:, n, :], t_in[w]).then_inc(fw_in[n], 16)
            sp.wait_ge(tern_done, 16)
            for t in range(B * LT):
                if t >= XF:
                    sp.wait_ge(y_ready, t - XF + 1)
                sp.dma_start(xf[:, t % XF, :], x2_d[t // LT, t % LT]).then_inc(xf_in[t % XF], 16)
                if t >= XF:
                    d = t - XF
                    sp.dma_start(out[d // LT, d % LT], y_out[:, d % 2, :]).then_inc(y_stored[d % 2], 16)
            for t in range(B * LT - XF, B * LT):
                sp.wait_ge(y_ready, t + 1)
                sp.dma_start(out[t // LT, t % LT], y_out[:, t % 2, :]).then_inc(y_stored[t % 2], 16)
            for n in range(2):
                sp.wait_ge(y_stored[n], 16 * B * LT // 2)

        @block.gpsimd
        def _(pool):
            for ap, value in ((ones[:], 1.0), (neg_half[:], -0.5), (x_pad[:, 0:TAPS - 1], 0.0),
                              (da[:, :, :, 0:1], 0.0)):
                nc.gpsimd.memset(ap, value).then_inc(pool_set, 1)
            for ap in (ident_b, mask_qk, mask_kq):
                nc.gpsimd.memset(ap[:], 0.0).then_inc(pool_set, 1)
            pool.wait_ge(pool_set, 7)
            for ap, keep, fill, step in ((ident_b, ALU.not_equal, 1.0, -1), (mask_qk, ALU.is_ge, MASKED, -1),
                                         (mask_kq, ALU.is_ge, MASKED, 1)):
                nc.gpsimd.affine_select(out=ap[:], in_=ap[:], compare_op=keep, fill=fill, base=0,
                                        pattern=[[step, P]], channel_multiplier=-step).then_inc(pool_set, 1)

            for kind, *a in SCHEDULE:
                if kind == "dbu":
                    j, = a
                    b, half, et, k = sub(j)
                    pool.wait_ge(du_ready, ET * b + et + 1)
                    pool.wait_ge(bc_in[k], 32 * (2 * b + half + 1))
                    if j >= 3:
                        pool.wait_ge(y_done, j - 2)
                    nc.gpsimd.tensor_tensor(hb[:, j % 3], du[:, et, :].unsqueeze(1).to_broadcast([P, 2, L]),
                                            b_bc[:, 2 * k:2 * k + 2, :], ALU.mult).then_inc(dbu_ready, 1)
                elif kind == "ln1a":
                    b, t = a
                    i = LT * b + t
                    pool.wait_ge(ln1_var, i + 1)
                    nc.gpsimd.tensor_tensor(rstd[:, i % 2], mv[:, i % 2, 1:2], neg_half[:, 0:1], ALU.pow)\
                        .then_inc(ln1_rstd, 1)
                elif kind == "ln2a":
                    b, = a
                    pool.wait_ge(ln2_var, b + 1)
                    nc.gpsimd.tensor_tensor(rstd2[:], ve2[:], neg_half[:], ALU.pow).then_inc(ln2_rstd, 1)

            for t in range(B * LT):
                for n in range(2):
                    pool.wait_ge(fx_var, 2 * t + n + 1)
                    nc.gpsimd.tensor_tensor(fx[:, t % 2, 2 + n:3 + n], fx[:, t % 2, 4 + n:5 + n],
                                            neg_half[:, 0:1], ALU.pow).then_inc(fx_pow, 1)
                if t >= 1:
                    pool.wait_ge(fh_var, t)
                    nc.gpsimd.tensor_tensor(fh[:, (t - 1) % 2, 2:3], fh[:, (t - 1) % 2, 4:5],
                                            neg_half[:, 0:1], ALU.pow).then_inc(fh_pow, 1)
            t = B * LT - 1
            pool.wait_ge(fh_var, t + 1)
            nc.gpsimd.tensor_tensor(fh[:, t % 2, 2:3], fh[:, t % 2, 4:5], neg_half[:, 0:1], ALU.pow)\
                .then_inc(fh_pow, 1)

        @block.scalar
        def _(act):
            own = Own(act, act_own)
            act.wait_ge(consts_in, ALL_CONSTS)
            nc.scalar.activation(a_neg[:], a_log, ACT.Exp).then_inc(a_exp, 1)
            nc.scalar.activation(pick[:], pick_f[:], ACT.Copy).then_inc(pick_ready, 1)
            act.wait_ge(pool_set, 10)

            for kind, *a in SCHEDULE:
                if kind == "exp":
                    j, = a
                    b, half, et, k = sub(j)
                    act.wait_ge(a_ready, 1)
                    act.wait_ge(delta_ready, ET * b + et + 1)
                    if j >= 2:
                        act.wait_ge(scan_done, j - 1)
                    for m in range(2):
                        n = 8 * half + 2 * k + m
                        ins = nc.scalar.activation(da[:, j % 2, m, 1:L], delta[:, et, 1:L], ACT.Exp,
                                                   scale=a_neg[:, et, n:n + 1])
                    ins.then_inc(da_ready, 1)
                elif kind == "ln1b":
                    b, t = a
                    n = TASK[kind, b, t]
                    act.wait_ge(m_full, n + 1)
                    if b and t == 0:
                        act.wait_ge(m_full, TASK["v", b - 1, 1, 1] + 1)
                    nc.scalar.activation(xn_t[:, :, P * t:P * t + P], M[n % 2].rearrange("p (d k) -> p d k", d=KD),
                                         ACT.Copy).then_inc(m_free["act"], 1)
                elif kind == "inproj":
                    b, et = a
                    n = TASK[kind, b, et]
                    i = ET * b + et
                    act.wait_ge(m_full, n + 1)
                    if i:
                        act.wait_ge(conv_done, 3 * i)
                    if b:
                        act.wait_ge(yacc_done, 8 * (b - 1) + et + 1)
                        act.wait_ge(du_ready, ET * (b - 1) + et + 1)
                    nc.scalar.activation(u[:, et, :], M[n % 2], ACT.Identity, bias=conv_b[:, et, :],
                                         scale=conv_w[:, et, TAPS - 1:TAPS])
                    nc.scalar.activation(x_pad[:, TAPS - 1:TAPS - 1 + L], M[n % 2], ACT.Copy)\
                        .then_inc(m_free["act"], 1)
                    act.wait_ge(conv_done, 3 * (i + 1))
                    nc.scalar.activation(u[:, et, :], u[:, et, :], ACT.Silu).then_inc(u_ready, 1)
                elif kind == "xproj":
                    b, = a
                    n = TASK[kind, b]
                    act.wait_ge(m_full, n + 1)
                    if b:
                        act.wait_ge(bc_stored, 16 * b)
                        act.wait_ge(m_full, TASK["dt", b - 1, ET - 1] + 1)
                    nc.scalar.activation(x_dbl[:], M[n % 2][0:DR + 2 * DS, :], ACT.Copy).then_inc(m_free["act"], 1)
                elif kind == "dt":
                    b, et = a
                    n = TASK[kind, b, et]
                    act.wait_ge(m_full, n + 1)
                    act.wait_ge(scratch_free, SCRATCH["dt", b, et])
                    nc.scalar.activation(tmp[:, 0, :], M[n % 2], ACT.Identity, bias=dt_b[:, et, :])\
                        .then_inc(m_free["act"], 1)
                    act.wait_ge(m_free["act"], FREED[n][1])
                    own.done(nc.scalar.activation(tmp[:, 1, :], tmp[:, 0, :], ACT.Abs))
                    own.settle()
                    own.done(nc.scalar.activation(tmp[:, 1, :], tmp[:, 1, :], ACT.Exp, scale=-1.0))
                    own.settle()
                    nc.scalar.activation(tmp[:, 2, :], tmp[:, 1, :], ACT.Ln, bias=1.0).then_inc(sp_ready, 1)
                elif kind == "rot":
                    b, n, _ = a
                    i = 4 * b + n
                    act.wait_ge(rot_done, i + 1)
                    if i:
                        act.wait_ge(hl_stored, 64 * i)
                    nc.scalar.activation(hl[:, 0:2, :], tmp[:, 0:2, :], ACT.Copy).then_inc(hi_ready, 1)
                elif kind == "v":
                    b, c, tt, _ = a
                    n = TASK[kind, b, c, tt]
                    act.wait_ge(m_full, n + 1)
                    if b:
                        act.wait_ge(pv_done, 8 * (b - 1) + 4 * (c + 1))
                    nc.scalar.activation(v_sb[:, 2 * tt:2 * tt + 2, CH * c:CH * c + CH],
                                         M[n % 2].rearrange("p (t n) -> p t n", t=2), ACT.Copy)\
                        .then_inc(m_free["act"], 1)
                elif kind == "mt":
                    p, = a
                    act.wait_ge(s_full, 6 * p + 6)
                    if p:
                        act.wait_ge(t_full, 5 * p)
                    nc.scalar.activation(m_row[:], S_B[0:2, :], ACT.Copy).then_inc(m_row_ready, 1)
                elif kind == "t":
                    p, n = a
                    v = 5 * p + n
                    act.wait_ge(t_full, v + 1)
                    if p:
                        act.wait_ge(pv_done, p)
                    if n < 4:
                        dst = p_t[:, n // 2, 512 * (n % 2):512 * (n % 2) + 512]
                        src = T_B[v % 2]
                    else:
                        dst = p_t[:, :, P_AT[2]:P_AT[2] + 256]
                        src = T_B[v % 2].rearrange("p (h n) -> p h n", h=2)
                    nc.scalar.activation(dst, src, ACT.Exp, scale=SCALE).then_inc(p_ready, 1)
                elif kind == "gate":
                    b, et = a
                    act.wait_ge(ln2_ready, b + 1)
                    if b or et:
                        act.wait_ge(gated, ET * b + et)
                    nc.scalar.activation(gate[:], xr[:, et, :], ACT.Silu, bias=nmr2[:, et:et + 1],
                                         scale=rstd2[:, et:et + 1]).then_inc(gate_ready, 1)

            act.wait_ge(fw_in[1], 16)
            nc.scalar.activation(t_pr[:].rearrange("p a n -> p (a n)"), stage[:, 1, :], ACT.Abs,
                                 accum_out=w_sum[:, 1:2]).then_inc(wsum_act, 1)
            act.wait_ge(tern_done, 16)
            tr = 0

            def high(dst):
                nonlocal tr
                act.wait_ge(tr_full, tr + 1)
                nc.scalar.activation(dst, ps[:, 4 + tr % 2, :].rearrange("p (k n) -> p k n", n=P), ACT.Copy)\
                    .then_inc(tr_hi, 1)
                tr += 1

            def hidden(t):
                for n in range(4):
                    act.wait_ge(fc_full, 4 * t + n + 1)
                    if t >= 2:
                        act.wait_ge(tr_full, tr_count(t - 2))
                    nc.scalar.activation(h_sb[:, t % 2, 512 * n:512 * n + 512], ps[:, n, :], ACT.Gelu,
                                         scale=gam[:, 0:1]).then_inc(gelu_done, 1)
                act.wait_ge(fh_nmr, t + 1)
                nc.scalar.activation(h_sb[:, t % 2, :], h_sb[:, t % 2, :], ACT.Identity,
                                     bias=fh[:, t % 2, 3:4], scale=fh[:, t % 2, 2:3]).then_inc(hn_done, 1)

            for step, t in ffn_steps():
                if step == "xt":
                    if t >= 2:
                        act.wait_ge(fc_full, 4 * (t - 1))
                    high(xq_hi[:, t % 2])
                elif step == "fc":
                    hidden(t)
                elif step == "ht":
                    if t:
                        act.wait_ge(proj_full, t)
                    for n in range(4):
                        high(hq_hi[:, 4 * n:4 * n + 4])

        @block.tensor
        def _(pe):
            pe.wait_ge(consts_in, ALL_CONSTS)
            pe.wait_ge(pool_set, 10)

            def chunk_in(c):
                pe.wait_ge(w_in[c % 2], 16 * (c // 2 + 1))

            for kind, *a in SCHEDULE:
                if kind == "ln1b":
                    b, t = a
                    n, i = TASK[kind, b, t], LT * b + t
                    pe.wait_ge(ln1_done, i + 1)
                    freed(pe, n)
                    for d in range(KD):
                        mm = nc.tensor.transpose(M[n % 2][:, P * d:P * d + P], x_in[:, i % 2, P * d:P * d + P],
                                                 ident[:])
                    mm.then_inc(m_full, 1)
                elif kind == "inproj":
                    b, et = a
                    n = TASK[kind, b, et]
                    pe.wait_ge(ctx_in_s, 16 * (b + 1))
                    freed(pe, n)
                    for d in range(KC):
                        mm = nc.tensor.matmul(M[n % 2], in_w[:, d, P * et:P * et + P], ctx_in[:, d, :],
                                              start=(d == 0), stop=(d == KC - 1))
                    mm.then_inc(m_full, 1)
                elif kind == "xproj":
                    b, = a
                    n = TASK[kind, b]
                    pe.wait_ge(u_ready, ET * (b + 1))
                    freed(pe, n)
                    for et in range(ET):
                        mm = nc.tensor.matmul(M[n % 2][0:DR + 2 * DS, :], xp_w[:, et, :], u[:, et, :],
                                              start=(et == 0), stop=(et == ET - 1))
                    mm.then_inc(m_full, 1)
                elif kind == "dt":
                    b, et = a
                    n = TASK[kind, b, et]
                    emptied(pe, TASK["xproj", b])
                    freed(pe, n)
                    nc.tensor.matmul(M[n % 2], dt_w[:, P * et:P * et + P], x_dbl[0:DR, :], start=True, stop=True)\
                        .then_inc(m_full, 1)
                elif kind == "rot":
                    b, n, c = a
                    chunk_in(c)
                    emptied(pe, TASK["ln1b", b, LT - 1])
                    for half in range(2):
                        task = TASK[kind, b, n] + half
                        freed(pe, task)
                        for d in range(KD):
                            mm = nc.tensor.matmul(M[task % 2], w_ring[:, c % 2, d, P * half:P * half + P],
                                                  xn_t[:, d, :], start=(d == 0), stop=(d == KD - 1))
                        mm.then_inc(m_full, 1)
                elif kind == "v":
                    b, c, tt, wc = a
                    n = TASK[kind, b, c, tt]
                    chunk_in(wc)
                    emptied(pe, TASK["ln1b", b, LT - 1])
                    freed(pe, n)
                    for m in range(2):
                        t = 2 * tt + m
                        for d in range(KD):
                            mm = nc.tensor.matmul(M[n % 2][:, CH * m:CH * m + CH], xn_t[:, d, P * t:P * t + P],
                                                  w_ring[:, wc % 2, d, :], start=(d == 0), stop=(d == KD - 1))
                    mm.then_inc(m_full, 1)
                elif kind == "s":
                    p, n = a
                    pe.wait_ge(stack_in[p % 2], 160 * (p // 2 + 1))
                    if n:
                        pe.wait_ge(max_done, 5 * p + n)
                    elif p:
                        pe.wait_ge(m_row_ready, p)
                    for h, i, col in S_UNITS[n]:
                        w = P * (i + 1)
                        nc.tensor.matmul(S_B[:, col:col + w], q_st[:, p % 2, h, P * i:P * i + P],
                                         k_st[:, p % 2, h, 0:w], start=True, stop=False)
                        mm = nc.tensor.matmul(S_B[:, col + w - P:col + w], ident_b[:], mask_qk[:],
                                              start=False, stop=True)
                    mm.then_inc(s_full, 1)
                elif kind == "mt":
                    p, = a
                    pe.wait_ge(max_done, 5 * p + 5)
                    for i in range(LT):
                        mm = nc.tensor.transpose(S_B[0:2, P * i:P * i + P], m_col[:, i, :], ident[:])
                    mm.then_inc(s_full, 1)
                elif kind == "t":
                    p, n = a
                    v = 5 * p + n
                    pe.wait_ge(m_row_ready, p + 1)
                    pe.wait_ge(pick_ready, 1)
                    if v >= 2:
                        pe.wait_ge(p_ready, v - 1)
                    bank = T_B[v % 2]
                    for h, jt, col in T_UNITS[n]:
                        w = L - P * jt
                        nc.tensor.matmul(bank[:, col:col + w], k_st[:, p % 2, h, P * jt:P * jt + P],
                                         q_st[:, p % 2, h, P * jt:L], start=True, stop=False)
                        nc.tensor.matmul(bank[:, col:col + P], ident_b[:], mask_kq[:], start=False, stop=False)
                        mm = nc.tensor.matmul(bank[:, col:col + w], pick[:, h, :], m_row[:, P * jt:L],
                                              start=False, stop=True)
                    mm.then_inc(t_full, 1)
                elif kind == "pv":
                    p, = a
                    b, sb_ = divmod(p, 8)
                    pe.wait_ge(p_ready, 5 * (p + 1))
                    emptied(pe, TASK["v", b, sb_ // 4, 1])
                    if p % 2 == 0 and p:
                        pe.wait_ge(norm_done, p // 2)
                    for jt in range(LT):
                        for h in range(2):
                            head = 2 * sb_ + h
                            rhs = p_t[:, h, P_AT[jt]:P_AT[jt] + L - P * jt]
                            for lhs, bank, quad in ((v_sb[:, jt, HD * head:HD * head + HD], O_B, 2 * (p % 2) + h),
                                                    (ones[:, 0:HD], Z_B, (2 * (p % 2) + h + 2) % 4)):
                                mm = nc.tensor.matmul(bank[HD * quad:HD * quad + HD, P * jt:L], lhs, rhs,
                                                      start=(jt == 0), stop=(jt == LT - 1))
                    mm.then_inc(pv_done, 1)
                elif kind == "y":
                    j, = a
                    pe.wait_ge(ch_done, j + 1)
                    if j % 4 == 0 and j:
                        pe.wait_ge(yacc_done, j // 4)
                    for m in range(2):
                        mm = nc.tensor.matmul(Y_B, ident[:], hb[:, j % 3, m, :], start=(j % 4 == 0 and m == 0),
                                              stop=(j % 4 == 3 and m == 1))
                    mm.then_inc(y_done, 1)
                elif kind == "wo":
                    b, t, *wc = a
                    n = TASK[kind, b, t]
                    for c in wc:
                        chunk_in(c)
                    pe.wait_ge(norm_done, 4 * b + 4)
                    freed(pe, n)
                    for m, c in enumerate(wc):
                        for g in range(KD):
                            mm = nc.tensor.matmul(M[n % 2][:, CH * m:CH * m + CH], o_t[:, g, P * t:P * t + P],
                                                  w_ring[:, c % 2, g, :], start=(g == 0), stop=(g == KD - 1))
                    mm.then_inc(m_full, 1)
                elif kind == "yt":
                    b, et = a
                    n = TASK[kind, b, et]
                    pe.wait_ge(gated, ET * b + et + 1)
                    freed(pe, n)
                    for lt in range(LT):
                        mm = nc.tensor.transpose(M[n % 2][:, P * lt:P * lt + P],
                                                 y_acc[:, b % 2, et, P * lt:P * lt + P], ident[:])
                    mm.then_inc(m_full, 1)

            pe.wait_ge(wsum_ready, 1)
            pe.wait_ge(wsum_act, 1)
            nc.tensor.matmul(ps[:, 0, 0:2], ones[:], w_sum[:], start=True, stop=True).then_inc(wtot_full, 1)
            tr = 0

            def turn(src, n):
                nonlocal tr
                if tr >= 2:
                    pe.wait_ge(tr_free, tr - 1)
                for d in range(4):
                    mm = nc.tensor.transpose(ps[:, 4 + tr % 2, P * d:P * d + P], src[:, P * (4 * n + d):P * (4 * n + d + 1)],
                                             ident[:])
                mm.then_inc(tr_full, 1)
                tr += 1

            for step, t in ffn_steps():
                if step == "xt":
                    pe.wait_ge(xq_done, t + 1)
                    turn(xq[:, t % 2, :], 0)
                elif step == "fc":
                    pe.wait_ge(tr_free, tr_x(t))
                    for n in range(4):
                        if t:
                            pe.wait_ge(gelu_done, 4 * (t - 1) + n + 1)
                        for d in range(KD):
                            for m, part in enumerate((xq_hi, xq_lo)):
                                mm = nc.tensor.matmul(ps[:, n, :], part[:, t % 2, d, :], t_fc[:, d, 512 * n:512 * n + 512],
                                                      start=(d == 0 and m == 0), stop=(d == KD - 1 and m == 1))
                        mm.then_inc(fc_full, 1)
                elif step == "ht":
                    pe.wait_ge(hq_done, t + 1)
                    for n in range(4):
                        turn(h_sb[:, t % 2, :], n)
                elif step == "proj":
                    if t:
                        pe.wait_ge(y_ready, t)
                    pe.wait_ge(tr_free, tr_count(t))
                    for k in range(FT):
                        for m, part in enumerate((hq_hi, hq_lo)):
                            mm = nc.tensor.matmul(ps[:, 6, :], part[:, k, :], t_pr[:, k, :],
                                                  start=(k == 0 and m == 0), stop=(k == FT - 1 and m == 1))
                    mm.then_inc(proj_full, 1)

        @block.vector
        def _(dve):
            own = Own(dve, dve_own)
            v = nc.vector
            dve.wait_ge(consts_in, ALL_CONSTS)
            dve.wait_ge(pool_set, 10)
            dve.wait_ge(a_exp, 1)
            v.tensor_scalar(a_neg[:], a_neg[:], -1.0, None, ALU.mult).then_inc(a_ready, 1)

            for kind, *a in SCHEDULE:
                if kind == "scan":
                    j, = a
                    dve.wait_ge(da_ready, j + 1)
                    dve.wait_ge(dbu_ready, j + 1)
                    h = hb[:, j % 3].rearrange("p a n -> p (a n)")
                    v.tensor_tensor_scan(h, da[:, j % 2].rearrange("p a n -> p (a n)"), h, 0.0, ALU.mult, ALU.add)\
                        .then_inc(scan_done, 1)
                elif kind == "ch":
                    j, = a
                    k = j % 4
                    dve.wait_ge(scan_done, j + 1)
                    v.tensor_tensor(hb[:, j % 3], hb[:, j % 3], c_bc[:, 2 * k:2 * k + 2, :], ALU.mult)\
                        .then_inc(ch_done, 1)
                elif kind == "yacc":
                    n, = a
                    b, half, et = n // 8, n // 4 % 2, n % 4
                    dve.wait_ge(y_done, 4 * n + 4)
                    y = y_acc[:, b % 2, et, :]
                    if half == 0:
                        if b >= 2:
                            dve.wait_ge(m_full, TASK["yt", b - 2, et] + 1)
                        ins = v.scalar_tensor_tensor(out=y, in0=u[:, et, :], scalar=d_skip[:, et, :], in1=Y_B,
                                                     op0=ALU.mult, op1=ALU.add)
                    else:
                        dve.wait_ge(yacc_done, n - 3)
                        ins = v.tensor_tensor(y, y, Y_B, ALU.add)
                    ins.then_inc(yacc_done, 1)
                elif kind == "ln1a":
                    b, t = a
                    i = LT * b + t
                    dve.wait_ge(x_in_s[i % 2], 16 * (i // 2 + 1))
                    own.settle()
                    own.done(v.bn_stats(stats[:, i % 2], x_in[:, i % 2, :]))
                    own.settle()
                    own.done(v.bn_aggr(mv[:, i % 2], stats[:, i % 2]))
                    own.settle()
                    v.tensor_scalar(mv[:, i % 2, 1:2], mv[:, i % 2, 1:2], EPS, None, ALU.add).then_inc(ln1_var, 1)
                elif kind == "ln1b":
                    b, t = a
                    i = LT * b + t
                    dve.wait_ge(ln1_rstd, i + 1)
                    v.tensor_scalar(x_in[:, i % 2, :], x_in[:, i % 2, :], mv[:, i % 2, 0:1], rstd[:, i % 2],
                                    ALU.subtract, ALU.mult).then_inc(ln1_done, 1)
                elif kind == "inproj":
                    b, et = a
                    i = ET * b + et
                    emptied(dve, TASK[kind, b, et])
                    for tap in range(TAPS - 1):
                        if tap:
                            dve.wait_ge(conv_done, 3 * i + tap)
                        v.scalar_tensor_tensor(out=u[:, et, :], in0=x_pad[:, tap:tap + L],
                                               scalar=conv_w[:, et, tap:tap + 1], in1=u[:, et, :],
                                               op0=ALU.mult, op1=ALU.add).then_inc(conv_done, 1)
                elif kind == "delta":
                    b, et = a
                    i = ET * b + et
                    dve.wait_ge(sp_ready, i + 1)
                    if b:
                        dve.wait_ge(da_ready, 32 * (b - 1) + 16 + 4 * et + 4)
                        dve.wait_ge(dbu_ready, 32 * (b - 1) + 16 + 4 * et + 4)
                    d = delta[:, et, :]
                    own.done(v.tensor_scalar(d, tmp[:, 1, :], 1.0, 1.0, ALU.add, ALU.subtract))
                    own.settle()
                    own.done(v.tensor_tensor(d, tmp[:, 1, :], d, ALU.subtract))
                    own.settle()
                    own.done(v.tensor_tensor(d, d, tmp[:, 2, :], ALU.add))
                    own.settle()
                    own.done(v.scalar_tensor_tensor(out=d, in0=tmp[:, 0, :], scalar=0.0, in1=d,
                                                    op0=ALU.max, op1=ALU.add))
                    own.settle()
                    dve.wait_ge(u_ready, i + 1)
                    v.tensor_tensor(du[:, et, :], d, u[:, et, :], ALU.mult).then_inc(du_ready, 1)
                    v.tensor_scalar(tmp[:, 0, 0:1], d[:, 0:1], 1.0, None, ALU.mult).then_inc(delta_ready, 1)
                    dve.wait_ge(delta_ready, i + 1)
                    v.tensor_copy(tmp[:, 1, 0:1], tmp[:, 0, 0:1]).then_inc(scratch_free, 1)
                elif kind == "rot":
                    b, n, _ = a
                    i, task = 4 * b + n, TASK[kind, b, n]
                    first, second = M[task % 2], M[(task + 1) % 2]
                    dve.wait_ge(scratch_free, SCRATCH[kind, b, n])
                    dve.wait_ge(m_full, task + 1)
                    own.done(v.tensor_tensor(tmp[:, 0, :], first, cos[:], ALU.mult))
                    v.tensor_tensor(tmp[:, 2, :], first, sin[:], ALU.mult).then_inc(m_free["dve"], 1)
                    dve.wait_ge(m_full, task + 2)
                    own.done(v.tensor_tensor(tmp[:, 1, :], second, sin[:], ALU.mult))
                    own.settle()
                    own.done(v.tensor_tensor(tmp[:, 0, :], tmp[:, 0, :], tmp[:, 1, :], ALU.subtract))
                    own.settle()
                    v.tensor_tensor(tmp[:, 1, :], second, cos[:], ALU.mult).then_inc(m_free["dve"], 1)
                    dve.wait_ge(m_free["dve"], FREED[task + 1][1])
                    v.tensor_tensor(tmp[:, 1, :], tmp[:, 1, :], tmp[:, 2, :], ALU.add).then_inc(rot_done, 1)
                elif kind == "lo":
                    b, n = a
                    i = 4 * b + n
                    dve.wait_ge(hi_ready, i + 1)
                    v.tensor_tensor(hl[:, 2:4, :], tmp[:, 0:2, :], hl[:, 0:2, :].bitcast(F32), ALU.subtract)\
                        .then_inc(scratch_free, 1)
                elif kind == "s":
                    p, n = a
                    dve.wait_ge(s_full, 6 * p + n + 1)
                    if n == 4:
                        v.tensor_reduce(m_col[:, 1, :], S_B.rearrange("p (h n) -> p h n", h=2), AX.X, ALU.max,
                                        negate=True).then_inc(max_done, 1)
                    else:
                        for h, i, col in S_UNITS[n]:
                            ins = v.tensor_reduce(m_col[:, i, h:h + 1], S_B[:, col:col + P * (i + 1)], AX.X, ALU.max,
                                                  negate=True)
                        ins.then_inc(max_done, 1)
                elif kind == "norm":
                    n, = a
                    b, g = divmod(n, 4)
                    dve.wait_ge(pv_done, 2 * n + 2)
                    if b and g == 0:
                        dve.wait_ge(m_full, TASK["wo", b - 1, LT - 1] + 1)
                    own.done(v.reciprocal(o_t[0:64, g, :], Z_B[64:128, :]))
                    own.done(v.reciprocal(o_t[64:128, g, :], Z_B[0:64, :]))
                    own.settle()
                    v.tensor_tensor(o_t[:, g, :], O_B, o_t[:, g, :], ALU.mult).then_inc(norm_done, 1)
                elif kind == "wo":
                    b, t, *_ = a
                    n = TASK[kind, b, t]
                    dve.wait_ge(resid_in, 16 * (b + 1))
                    dve.wait_ge(m_full, n + 1)
                    v.tensor_tensor(xr[:, t, :], M[n % 2], xr[:, t, :], ALU.add).then_inc(m_free["dve"], 1)
                elif kind == "ln2a":
                    b, = a
                    emptied(dve, TASK["wo", b, LT - 1])
                    for t in range(LT):
                        own.done(v.bn_stats(stats2[:, t], xr[:, t, :]))
                    own.settle()
                    for t in range(LT):
                        own.done(v.bn_aggr(mv2[:, t], stats2[:, t]))
                    own.settle()
                    v.tensor_scalar(ve2[:], mv2[:, :, 1], EPS, None, ALU.add).then_inc(ln2_var, 1)
                elif kind == "ln2b":
                    b, = a
                    dve.wait_ge(ln2_rstd, b + 1)
                    v.scalar_tensor_tensor(out=nmr2[:], in0=mv2[:, :, 0], scalar=-1.0, in1=rstd2[:],
                                           op0=ALU.mult, op1=ALU.mult).then_inc(ln2_ready, 1)
                elif kind == "gate":
                    b, et = a
                    dve.wait_ge(gate_ready, ET * b + et + 1)
                    dve.wait_ge(yacc_done, 8 * b + 4 + et + 1)
                    y = y_acc[:, b % 2, et, :]
                    v.tensor_tensor(y, y, gate[:], ALU.mult).then_inc(gated, 1)
                elif kind == "yt":
                    b, et = a
                    n = TASK[kind, b, et]
                    dve.wait_ge(m_full, n + 1)
                    dst = xr[:, :, P * et:P * et + P]
                    v.tensor_tensor(dst, M[n % 2].rearrange("p (t n) -> p t n", t=LT), dst, ALU.add)\
                        .then_inc(m_free["dve"], 1)

            dve.wait_ge(fw_in[0], 16)
            v.tensor_reduce(w_sum[:, 0:1], stage[:, 0, :], AX.X, ALU.add, apply_absolute_value=True)\
                .then_inc(wsum_ready, 1)
            dve.wait_ge(wtot_full, 1)
            own.done(v.tensor_scalar(gam[:], ps[:, 0, 0:2], 1.0 / (DM * FF), None, ALU.mult))
            own.settle()
            own.done(v.tensor_scalar(thr[:], gam[:], EPS_Q, 0.5, ALU.add, ALU.mult))
            own.done(v.tensor_scalar(nthr[:], gam[:], EPS_Q, -0.5, ALU.add, ALU.mult))
            own.settle()
            dve.wait_ge(fw_in[1], 16)
            for n in range(8):
                w, c = divmod(n, 4)
                src = stage[:, w, FF * c:FF * c + FF]
                dst = t_fc[:, c, :] if w == 0 else t_pr[:, 4 * c:4 * c + 4, :].rearrange("p a n -> p (a n)")
                if n >= 2:
                    dve.wait_ge(tern_done, 2 * n - 2)
                v.tensor_scalar(low[:, n % 2, :], src, nthr[:, w:w + 1], None, ALU.is_lt).then_inc(tern_done, 1)
                dve.wait_ge(tern_done, 2 * n + 1)
                v.scalar_tensor_tensor(out=dst, in0=src, scalar=thr[:, w:w + 1], in1=low[:, n % 2, :],
                                       op0=ALU.is_gt, op1=ALU.subtract).then_inc(tern_done, 1)
            dve.wait_ge(tern_done, 16)
            tr = 0

            def low_part(dst, hi):
                nonlocal tr
                dve.wait_ge(tr_hi, tr + 1)
                v.tensor_tensor(dst, ps[:, 4 + tr % 2, :].rearrange("p (k n) -> p k n", n=P), hi.bitcast(F32),
                                ALU.subtract).then_inc(tr_free, 1)
                tr += 1

            def quantize(x, f, sig):
                own.done(v.tensor_reduce(f[:, 8:9], x, AX.X, ALU.max, apply_absolute_value=True))
                own.settle()
                own.done(v.reciprocal(f[:, 9:10], f[:, 8:9]))
                own.done(v.tensor_scalar(f[:, 11:12], f[:, 8:9], 1.0 / Q_B, None, ALU.mult))
                own.settle()
                own.done(v.tensor_scalar(f[:, 10:11], f[:, 9:10], Q_B, None, ALU.mult))
                own.settle()
                own.done(v.tensor_scalar(x, x, f[:, 10:11], Q_B, ALU.mult, ALU.min))
                own.settle()
                v.tensor_scalar(x, x, -Q_B, f[:, 11:12], ALU.max, ALU.mult).then_inc(sig, 1)

            def x_norm(t):
                f, x = fx[:, t % 2], xf[:, t % XF, :]
                dve.wait_ge(xf_in[t % XF], 16 * (t // XF + 1))
                own.settle()
                own.done(v.bn_stats(st_x[:, t % 2], x))
                own.settle()
                own.done(v.bn_aggr(f[:, 0:2], st_x[:, t % 2]))
                own.settle()
                v.tensor_scalar(f[:, 4:5], f[:, 1:2], EPS, None, ALU.add).then_inc(fx_var, 1)
                dve.wait_ge(fx_pow, 2 * t + 1)
                own.done(v.tensor_scalar(f[:, 6:7], f[:, 1:2], f[:, 2:3], f[:, 2:3], ALU.mult, ALU.mult))
                own.settle()
                v.tensor_scalar(f[:, 5:6], f[:, 6:7], EPS_Q, None, ALU.add).then_inc(fx_var, 1)
                dve.wait_ge(fx_pow, 2 * t + 2)
                own.done(v.tensor_scalar(f[:, 7:8], f[:, 2:3], f[:, 3:4], None, ALU.mult))
                own.settle()
                if t >= 2:
                    dve.wait_ge(tr_full, tr_xfull(t - 2))
                own.done(v.tensor_scalar(xq[:, t % 2, :], x, f[:, 0:1], f[:, 7:8], ALU.subtract, ALU.mult))
                own.settle()
                quantize(xq[:, t % 2, :], f, xq_done)

            x_norm(0)
            for step, t in ffn_steps():
                if step == "xt":
                    if t >= 2:
                        dve.wait_ge(fc_full, 4 * (t - 1))
                    low_part(xq_lo[:, t % 2], xq_hi[:, t % 2])
                    if t + 1 < B * LT:
                        x_norm(t + 1)
                elif step == "fc":
                    f = fh[:, t % 2]
                    for n in range(4):
                        dve.wait_ge(gelu_done, 4 * t + n + 1)
                        own.done(v.bn_stats(st_h[:, t % 2, n], h_sb[:, t % 2, 512 * n:512 * n + 512]))
                    own.settle()
                    own.done(v.bn_aggr(f[:, 0:2], st_h[:, t % 2]))
                    own.settle()
                    v.tensor_scalar(f[:, 4:5], f[:, 1:2], EPS_Q, None, ALU.add).then_inc(fh_var, 1)
                    dve.wait_ge(fh_pow, t + 1)
                    v.tensor_scalar(f[:, 3:4], f[:, 0:1], f[:, 2:3], -1.0, ALU.mult, ALU.mult).then_inc(fh_nmr, 1)
                    dve.wait_ge(hn_done, t + 1)
                    quantize(h_sb[:, t % 2, :], f, hq_done)
                elif step == "ht":
                    if t:
                        dve.wait_ge(proj_full, t)
                    for n in range(4):
                        low_part(hq_lo[:, 4 * n:4 * n + 4], hq_hi[:, 4 * n:4 * n + 4])
                elif step == "proj":
                    dve.wait_ge(proj_full, t + 1)
                    if t >= 2:
                        dve.wait_ge(y_stored[t % 2], 16 * (t // 2))
                    v.scalar_tensor_tensor(out=y_out[:, t % 2, :], in0=ps[:, 6, :], scalar=gam[:, 1:2],
                                           in1=xf[:, t % XF, :], op0=ALU.mult, op1=ALU.add).then_inc(y_ready, 1)


def ffn_steps():
    n = B * LT
    yield ("xt", 0)
    for t in range(n + 1):
        if t < n:
            yield ("fc", t)
            if t + 1 < n:
                yield ("xt", t + 1)
        if t:
            yield ("ht", t - 1)
            yield ("proj", t - 1)


def tr_order():
    n, at = 0, {}
    for step, t in ffn_steps():
        if step in ("xt", "ht"):
            n += 1 if step == "xt" else 4
            at[step, t] = n
    return at


TR = tr_order()


def tr_x(t):
    return TR["xt", t]


tr_xfull = tr_x


def tr_count(t):
    return TR["ht", t]


def constants():
    import numpy as np

    pos = np.arange(L, dtype=np.float32)
    inv = (1.0 / np.float32(10000.0) ** (np.arange(0, HD, 2, dtype=np.float32) / np.float32(HD))).astype(np.float32)
    angle = np.tile((inv[:, None] * pos[None, :]).astype(np.float32), (P // HALF, 1))
    pick = np.zeros((2, 2, P), np.float32)
    pick[0, 0] = pick[1, 1] = 1.0
    return {
        "cos": np.cos(angle).astype(np.float32), "sin": np.sin(angle).astype(np.float32),
        "ident": np.eye(P, dtype=np.float32), "pick": pick,
    }


def kernel(**inputs):
    import numpy as np
    import concourse.bacc as bacc
    from concourse.bass_utils import run_bass_kernel_spmd

    a = {k: np.ascontiguousarray(v) for k, v in inputs.items()}

    def rows(w):
        return w.reshape(w.shape[0] // P, P, w.shape[1]).transpose(1, 0, 2)

    w = a["L0_attn_w_qkv"].reshape(DM, 3, NH, 2, HALF)
    chunks = []
    for half in range(2):
        for which in range(2):
            part = w[:, which, 8 * half:8 * half + 8]
            chunks.append(rows(part.transpose(0, 2, 1, 3).reshape(DM, CH)))
    wv = a["L0_attn_w_qkv"][:, 2 * DM:]
    for m in (wv, a["L0_attn_w_o"]):
        for c in range(2):
            chunks.append(rows(m[:, CH * c:CH * c + CH]))

    def cols(m):
        return m.reshape(ET, P, -1).transpose(1, 0, 2)

    arrays = {
        "x": a["x"].reshape(B, LT, P, DM),
        "ctx": a["ctx_1024"].transpose(0, 2, 1).reshape(B, KC, P, L).transpose(0, 2, 1, 3),
        "w_attn": np.stack(chunks),
        "in_w": rows(a["L0_xattn_in_proj_w"].T),
        "xp_w": rows(a["L0_xattn_x_proj_w"].T),
        "dt_w": a["L0_xattn_dt_proj_w"].T,
        "small": np.concatenate([cols(a["L0_xattn_conv_w"]), cols(a["L0_xattn_conv_b"]),
                                 cols(a["L0_xattn_dt_proj_b"]), cols(a["L0_xattn_D"]),
                                 cols(a["L0_xattn_A_log"])], axis=2),
        "w_fc": rows(a["L0_ffn_w_fc"].T).reshape(P, KD * FF),
        "w_pr": rows(a["L0_ffn_w_proj"].T).reshape(P, FT * DM),
        **constants(),
    }
    arrays = {f"in_{k}": np.ascontiguousarray(v) for k, v in arrays.items()}
    nc = bacc.Bacc("TRN2", target_bir_lowering=False, num_devices=1)
    t_in = {k[3:]: nc.dram_tensor(k, v.shape, mybir.dt.from_np(v.dtype), kind="ExternalInput").ap()
            for k, v in arrays.items()}
    out = nc.dram_tensor("out_y", (B, LT, P, DM), F32, kind="ExternalOutput").ap()
    layer_kernel(nc, t_in, out)
    r = run_bass_kernel_spmd(nc, [arrays], core_ids=[0])
    return r.results[0]["out_y"].reshape(B, L, DM)
```

```python
from contextlib import ExitStack

import concourse.bass as bass
from concourse import mybir

F32 = mybir.dt.float32
F32R = mybir.dt.float32r
BF16 = mybir.dt.bfloat16
ALU = mybir.AluOpType
ACT = mybir.ActivationFunctionType
AX = mybir.AxisListType

P = 128
B, L, DM = 4, 512, 512
NH, HD = 16, 32
HALF = HD // 2
DC, DS, DR, TAPS = 256, 16, 16, 4
FF = 4 * DM
LT = L // P
ET = DM // P
KD = DM // P
KC = DC // P
FT = FF // P
SCALE = float(HD) ** -0.5
EPS = 1e-5
EPS_Q = 1e-6
Q_B = 128.0
MASKED = -1e30

SLOTS = B * 8
SUBS = 4
CH = 256
XF = 5

P_AT = [0, 512, 1024, 896]
P_W = 1280


TICKS = 12
POOL_CH = (1, 3)


def schedule():
    out = []

    def at(slot, tick, *items):
        out.extend((TICKS * slot + tick, item) for item in items)

    def mixer(s):
        if s < SLOTS:
            for k in range(SUBS):
                j = SUBS * s + k
                at(s, 3 * k - 3, ("exp", j), ("dbu", j))
                at(s, 3 * k, ("scan", j))
                at(s, 3 * k + 1, ("ch", j))
                at(s, 3 * k + 3.2, ("y", j))
            at(s, 13, ("yacc", s))
            if s:
                at(s, -12, ("stack", s))
            for n in range(5):
                at(s, n, ("s", s, n))
                at(s, 6.5 + n, ("t", s, n))
            at(s, 5.5, ("mt", s))
            at(s, 12.5, ("pv", s))
            if s % 2:
                n = s // 2
                at(s, 13.2, ("zt", n))
                at(s, 15.5, ("zb", n))
                at(s, 16.6, ("norm", n))

    def before(b):
        s = 8 * (b - 1)
        if b == 0:
            for t in range(LT):
                at(-8, 2 * t, ("xload", b, t), ("ln1a", b, t))
                at(-8, 2 * t + 2, ("ln1b", b, t))
            at(-8, 0, ("cload", b))
            for et in range(ET):
                at(-7, 3 * et, ("inproj", b, et))
                at(-6, et, ("silu", b, et))
            at(-6, 6, ("xproj", b))
            at(-6, 8, *[("bcload", b, 0, k) for k in range(SUBS)])
            times = {"rot": [(-5, 0), (-4, 0), (0, 2), (0, 7)], "dt": [(-4, -4), (-4, 9), (1, 3), (2, 0)],
                     "v": [(-2, 0), (-2, 3), (1, 6), (2, 3)]}
            at(-3, 3, ("stack", 0))
            gap = 3
        else:
            if b == 1:
                loads = [(0, 4), (0, 4.1), (2, 4.2), (2, 5.2)]
                sums = [(1, 8), (1, 9), (2, 4.5), (2, 5.5)]
                turns = [(2, 4), (2, 5), (2, 6), (2, 7)]
            else:
                loads = [(-1, 4), (-1, 4.1), (0, 10.6), (1, 1.6)]
                sums = [(0, 8 + 3 * t) for t in range(LT)]
                turns = [(0, 10 + 3 * t) for t in range(LT)]
            for t in range(LT):
                at(s + loads[t][0], loads[t][1], ("xload", b, t))
                at(s + sums[t][0], sums[t][1], ("ln1a", b, t))
                at(s + turns[t][0], turns[t][1], ("ln1b", b, t))
            at(s, 0, ("cload", b))
            for et in range(ET):
                slot, tick = ((1, 10), (2, 5), (3, 5), (4, 5))[et]
                at(s + slot, tick, ("inproj", b, et))
                at(s + 4, 9 + 0.5 * et, ("silu", b, et))
            at(s + 5, 0, ("xproj", b))
            for k in range(SUBS):
                at(s + 7, 3 * k + 3, ("bcload", b, 0, k))
            times = {"rot": [(2, 8), (3, 8), (4, 8), (6, 2)], "dt": [(5, 9), (6, 10), (7, 5), (8, 11)],
                     "v": [(7, 0), (7, 8), (8, 1), (8, 4)]}
            gap = 6
        for n, (slot, tick) in enumerate(times["rot"]):
            slot += s if b else 0
            second = tick + (gap if b == 0 else (6, 6, 8, 3)[n])
            at(slot, tick, ("rot", b, n, 0))
            at(slot, second, ("rot", b, n, 1))
            at(slot, second + 1.5, ("hi", b, n))
            at(slot, second + 2.2, ("lo", b, n))
        for et, (slot, tick) in enumerate(times["dt"]):
            slot += s if b else 0
            at(slot, tick, ("dt", b, et))
            at(slot, tick + 1.8, ("delta", b, et))
        for n, (slot, tick) in enumerate(times["v"]):
            at(slot + (s if b else 0), tick, ("v", b, n // 2, n % 2))
        for k in range(SUBS):
            at(8 * b + 3, 3 * k + 3, ("bcload", b, 1, k))

    def after(b):
        s = 8 * (b + 1)
        at(s, 0, ("resid", b))
        for n, (slot, tick) in enumerate(((0, 8), (1, 2), (1, 8), (2, 2))):
            at(s + slot, tick, ("wo", b, n // 2, n % 2))
        at(s + 2, 4, ("ln2a", b))
        at(s + 2, 6, ("ln2b", b))
        for et in range(ET):
            at(s + 4, 9.1 + 0.5 * et, ("gate", b, et))
            at(s + 5 + et // 2, (5.5, 10)[et % 2], ("yt", b, et))
        at(s + 7, 0, ("x2store", b))

    for s in range(SLOTS):
        mixer(s)
    for b in range(B):
        before(b)
        after(b)
    return out


LAG = {
    "pe": {"ln1b": 0.6, "zt": 0.6},
    "act": {"ln1b": 1.2, "inproj": 0.6, "xproj": 0.6, "dt": 0.6, "v": 0.8, "mt": 0.3, "t": 0.5, "zb": 0.6},
    "dve": {"s": 0.5, "inproj": 1.2, "rot": 0.8, "wo": 0.9, "gate": 0.5, "yt": 0.6, "zt": 1.2},
    "pool": {"ln1a": 0.1, "ln2a": 0.4},
    "sp": {"xproj": 1.0, "lo": 0.5},
}


def order(engine):
    lag = LAG[engine]
    return [item for _, item in sorted(((t + lag.get(i[0], 0), i) for t, i in schedule()), key=lambda x: x[0])]


ORDER = {engine: order(engine) for engine in LAG}


def chunk_uses():
    holds, number, last = [], {}, {}
    for item in ORDER["pe"]:
        kind, *a = item
        if kind not in ("rot", "v", "wo"):
            continue
        key = (kind, a[0], a[1])
        if key not in number:
            number[key] = len(holds)
            holds.append(a[1] + {"rot": 0, "v": 4, "wo": 6}[kind])
        last[number[key]] = item
    return holds, number, last


CHUNK, CHUNK_OF, LAST_USER = chunk_uses()
LOAD_AFTER = {item: c + 2 for c, item in LAST_USER.items() if c + 2 < len(CHUNK)}

EMPTIED_BY = {"ln1b": "act", "inproj": "act", "xproj": "act", "dt": "act", "v": "act", "zb": "act",
              "rot": "dve", "wo": "dve", "yt": "dve", "zt": "dve"}
TASK = {item: n for n, item in enumerate(x for x in ORDER["pe"] if x[0] in EMPTIED_BY)}
FREED = {}
for _who in ("act", "dve"):
    for _n, _item in enumerate(x for x in ORDER[_who] if EMPTIED_BY.get(x[0]) == _who):
        FREED[TASK[_item]] = (_who, _n + 1)
SCRATCH = {x[:3]: n for n, x in enumerate(x for x in ORDER["dve"] if x[0] in ("lo", "delta"))}
SCRATCH.update({("rot" if k[0] == "lo" else "dt", *k[1:]): n for k, n in list(SCRATCH.items())})


def scratch_after(item):
    return SCRATCH[item] + 1


def layer_kernel(nc, t_in, out):
    sems = {}
    with ExitStack() as ctx:
        base = [(nc.sbuf_base + 31) // 32 * 32]

        def sb(name, shape, dt=F32):
            size = 4 if dt in (F32, F32R) else 2
            n = size
            for d in shape[1:]:
                n *= d
            at = base[0]
            base[0] += (n + 31) // 32 * 32
            assert base[0] <= nc.sbuf_usable_end, (name, base[0], nc.sbuf_usable_end)
            return nc.alloc_sbuf_tensor_at(name, shape, dt, offset=at)

        def sem(name):
            sems[name] = ctx.enter_context(nc.semaphore(name))
            return sems[name]

        ident = sb("ident", [P, P])
        ones = sb("ones", [P, P])
        neg_half = sb("neg_half", [P, 4])
        phase_base = base[0]

        ident_b = sb("ident_b", [P, P], BF16)
        mask_qk = sb("mask_qk", [P, P], BF16)
        mask_kq = sb("mask_kq", [P, P], BF16)
        pick = sb("pick", [2, 2, P], F32R)
        pick_f = sb("pick_f", [2, 2, P])
        cos = sb("cos", [P, L])
        sin = sb("sin", [P, L])
        in_w = sb("in_w", [P, KC, DM])
        xp_w = sb("xp_w", [P, ET, DR + 2 * DS])
        dt_w = sb("dt_w", [DR, DM])
        small = sb("small", [P, ET, TAPS + 3 + DS])
        conv_w = small[:, :, 0:TAPS]
        conv_b = small[:, :, TAPS:TAPS + 1]
        dt_b = small[:, :, TAPS + 1:TAPS + 2]
        d_skip = small[:, :, TAPS + 2:TAPS + 3]
        a_log = small[:, :, TAPS + 3:]
        a_neg = sb("a_neg", [P, ET, DS])
        x_in = sb("x_in", [P, 2, DM])
        stats = sb("stats", [P, 2, 6])
        mv = sb("mv", [P, 2, 2])
        rstd = sb("rstd", [P, 2, 1])
        xn_t = sb("xn_t", [P, KD, L])
        w_ring = sb("w_ring", [P, 2, KD, CH])
        ctx_in = sb("ctx_in", [P, KC, L])
        x_pad = sb("x_pad", [P, 520])
        u = sb("u", [P, ET, L])
        delta = sb("delta", [P, ET, L])
        du = sb("du", [P, ET, L])
        b_bc = sb("b_bc", [P, 8, L])
        c_bc = sb("c_bc", [P, 8, L])
        da = sb("da", [P, 2, 2, L])
        hb = sb("hb", [P, 3, 2, L])
        y_acc = sb("y_acc", [P, 2, ET, L])
        x_dbl = sb("x_dbl", [DR + 2 * DS, L])
        tmp = sb("tmp", [P, 3, L])
        hl = sb("hl", [P, 4, L], F32R)
        v_sb = sb("v_sb", [P, LT, DM])
        q_st = sb("q_st", [P, 2, 2, L], F32R)
        k_st = sb("k_st", [P, 2, 2, L], F32R)
        p_t = sb("p_t", [P, 2, P_W])
        m_col = sb("m_col", [P, LT, 2])
        m_row = sb("m_row", [2, L], F32R)
        o_t = sb("o_t", [P, ET, L])
        z_sb = sb("z_sb", [P, L])
        z_rec = sb("z_rec", [P, LT, 4])
        xr = sb("xr", [P, LT, DM])
        stats2 = sb("stats2", [P, LT, 6])
        mv2 = sb("mv2", [P, LT, 2])
        ve2 = sb("ve2", [P, LT])
        rstd2 = sb("rstd2", [P, LT])
        nmr2 = sb("nmr2", [P, LT])
        gate = sb("gate", [P, L])

        base[0] = phase_base
        stage = sb("stage", [P, 2, KD * FF])
        low = sb("low", [P, 2, FF], BF16)
        t_fc = sb("t_fc", [P, KD, FF], F32R)
        t_pr = sb("t_pr", [P, FT, DM], F32R)
        w_sum = sb("w_sum", [P, 2])
        gam = sb("gam", [P, 2])
        thr = sb("thr", [P, 2])
        nthr = sb("nthr", [P, 2])
        base[0] -= 0
        act_base = phase_base
        end = base[0]
        base[0] = act_base
        xf = sb("xf", [P, XF, DM])
        xq = sb("xq", [P, 2, DM])
        fx = sb("fx", [P, 2, 16])
        st_x = sb("st_x", [P, 2, 6])
        xq_hi = sb("xq_hi", [P, 2, KD, P], F32R)
        xq_lo = sb("xq_lo", [P, 2, KD, P], F32R)
        h_sb = sb("h_sb", [P, 2, FF])
        fh = sb("fh", [P, 2, 16])
        st_h = sb("st_h", [P, 2, 4, 6])
        hq_hi = sb("hq_hi", [P, FT, P], F32R)
        hq_lo = sb("hq_lo", [P, FT, P], F32R)
        y_out = sb("y_out", [P, 2, DM])
        assert base[0] <= phase_base + 2 * KD * FF * 4

        ps = ctx.enter_context(nc.psum_tensor("ps", [P, 8, 512], F32))
        M = [ps[:, 0, :], ps[:, 1, :]]
        R = [ps[:, 2 + n, :] for n in range(3)]
        O_B, Z_B = ps[:, 5, :], ps[:, 6, :]
        Y_B = ps[:, 7, :]

        qk_d = nc.dram_tensor("qk_d", [B, 2, NH, 4, HALF, L], F32, kind="Internal").ap()
        bc_d = nc.dram_tensor("bc_d", [B, 2 * DS, L], F32, kind="Internal").ap()
        x2_d = nc.dram_tensor("x2_d", [B, LT, P, DM], F32, kind="Internal").ap()

        consts_in = sem("consts_in")
        w_in = [sem(f"w_in{i}") for i in range(2)]
        x_in_s = [sem(f"x_in{i}") for i in range(2)]
        ctx_in_s = sem("ctx_in_s")
        stack_in = [sem(f"stack_in{i}") for i in range(2)]
        bc_in = [sem(f"bc_in{i}") for i in range(SUBS)]
        resid_in = sem("resid_in")
        hl_stored = sem("hl_stored")
        bc_stored = sem("bc_stored")
        x2_stored = sem("x2_stored")
        pool_set = sem("pool_set")
        a_exp = sem("a_exp")
        a_ready = sem("a_ready")
        pick_ready = sem("pick_ready")
        m_full = sem("m_full")
        m_free = {"act": sem("m_free_act"), "dve": sem("m_free_dve")}
        ln1_var = sem("ln1_var")
        ln1_rstd = sem("ln1_rstd")
        ln1_done = sem("ln1_done")
        conv_done = sem("conv_done")
        u_ready = sem("u_ready")
        sp_ready = sem("sp_ready")
        delta_ready = sem("delta_ready")
        du_ready = sem("du_ready")
        scratch_free = sem("scratch_free")
        rot_done = sem("rot_done")
        hi_ready = sem("hi_ready")
        da_ready = sem("da_ready")
        dbu_ready = sem("dbu_ready")
        scan_done = sem("scan_done")
        ch_done = {"dve": sem("ch_done_dve"), "pool": sem("ch_done_pool")}
        y_done = sem("y_done")
        yacc_done = sem("yacc_done")
        s_full = sem("s_full")
        max_done = sem("max_done")
        m_row_ready = sem("m_row_ready")
        t_full = sem("t_full")
        p_ready = sem("p_ready")
        pv_done = sem("pv_done")
        z_copied = sem("z_copied")
        norm_done = sem("norm_done")
        ln2_var = sem("ln2_var")
        ln2_rstd = sem("ln2_rstd")
        ln2_ready = sem("ln2_ready")
        gate_ready = sem("gate_ready")
        gated = sem("gated")
        act_own = sem("act_own")
        dve_own = sem("dve_own")
        fw_in = [sem("fw_in0"), sem("fw_in1")]
        wsum_ready = sem("wsum_ready")
        wsum_act = sem("wsum_act")
        wtot_full = sem("wtot_full")
        tern_done = sem("tern_done")
        xf_in = [sem(f"xf_in{i}") for i in range(XF)]
        fx_var = sem("fx_var")
        fx_pow = sem("fx_pow")
        xq_done = sem("xq_done")
        tr_full = sem("tr_full")
        tr_hi = sem("tr_hi")
        tr_free = sem("tr_free")
        fc_full = sem("fc_full")
        gelu_done = sem("gelu_done")
        fh_var = sem("fh_var")
        fh_pow = sem("fh_pow")
        fh_nmr = sem("fh_nmr")
        hn_done = sem("hn_done")
        hq_done = sem("hq_done")
        proj_full = sem("proj_full")
        y_ready = sem("y_ready")
        y_stored = [sem("y_stored0"), sem("y_stored1")]

        CONSTS = [
            (ident, t_in["ident"]), (pick_f, t_in["pick"]), (in_w, t_in["in_w"]), (small, t_in["small"]),
            (xp_w, t_in["xp_w"]), (dt_w, t_in["dt_w"]), (cos, t_in["cos"]), (sin, t_in["sin"]),
        ]
        ALL_CONSTS = 16 * len(CONSTS)

        def sub(j):
            return j // 32, j // 16 % 2, j // 4 % 4, j % 4

        def freed(eng, n):
            if n >= 2:
                who, count = FREED[n - 2]
                eng.wait_ge(m_free[who], count)

        def emptied(eng, n):
            who, count = FREED[n]
            eng.wait_ge(m_free[who], count)

        def wait_ch(eng, j):
            mine = "pool" if j % SUBS in POOL_CH else "dve"
            eng.wait_ge(ch_done[mine], sum((i % SUBS in POOL_CH) == (mine == "pool") for i in range(j + 1)))

        def ring_free(r):
            if r >= 3:
                p, n = divmod(r - 3, 11)
                if n < 5:
                    nc.tensor.wait_ge(max_done, 5 * p + n + 1)
                elif n == 5:
                    nc.tensor.wait_ge(m_row_ready, p + 1)
                else:
                    nc.tensor.wait_ge(p_ready, 5 * p + n - 5)

        class Own:

            def __init__(self, eng, s):
                self.eng, self.s, self.n = eng, s, 0

            def done(self, ins):
                ins.then_inc(self.s, 1)
                self.n += 1

            def settle(self):
                self.eng.wait_ge(self.s, self.n)

        S_UNITS = [[(0, 3, 0)], [(0, 2, 0), (0, 0, 384)], [(1, 3, 0)], [(1, 2, 0), (1, 0, 384)],
                   [(0, 1, 0), (1, 1, 256)]]
        T_UNITS = [[(0, 0, 0)], [(0, 1, 0), (0, 3, 384)], [(1, 0, 0)], [(1, 1, 0), (1, 3, 384)],
                   [(0, 2, 0), (1, 2, 256)]]

        block = ctx.enter_context(nc.Block())

        @block.sync
        def _(sp):
            for dst, src in CONSTS:
                sp.dma_start(dst[:], src).then_inc(consts_in, 16)

            def load_chunk(c):
                sp.dma_start(w_ring[:, c % 2], t_in["w_attn"][CHUNK[c]]).then_inc(w_in[c % 2], 16)

            load_chunk(0)
            load_chunk(1)
            for item in ORDER["sp"]:
                kind, *a = item
                if item in LOAD_AFTER:
                    sp.wait_ge(m_full, TASK[item] + 1)
                    load_chunk(LOAD_AFTER[item])
                if kind == "xload":
                    b, t = a
                    i = LT * b + t
                    if i >= 2:
                        sp.wait_ge(m_full, TASK["ln1b", (i - 2) // LT, (i - 2) % LT] + 1)
                    sp.dma_start(x_in[:, i % 2], t_in["x"][b, t]).then_inc(x_in_s[i % 2], 16)
                elif kind == "cload":
                    b, = a
                    if b:
                        sp.wait_ge(m_full, TASK["inproj", b - 1, ET - 1] + 1)
                    sp.dma_start(ctx_in[:], t_in["ctx"][b]).then_inc(ctx_in_s, 16)
                elif kind == "lo":
                    b, n = a
                    sp.wait_ge(scratch_free, scratch_after(("rot", b, n)))
                    for part in range(4):
                        heads = qk_d[b, n % 2, 8 * (n // 2):8 * (n // 2) + 8, part]
                        sp.dma_start(heads, hl[:, part, :].bitcast(F32)).then_inc(hl_stored, 16)
                elif kind == "xproj":
                    b, = a
                    emptied(sp, TASK["xproj", b])
                    sp.dma_start(bc_d[b], x_dbl[DR:DR + 2 * DS, :]).then_inc(bc_stored, 16)
                elif kind == "bcload":
                    b, half, k = a
                    sp.wait_ge(bc_stored, 16 * (b + 1))
                    n = 2 * b + half
                    if n:
                        wait_ch(sp, 16 * (n - 1) + 12 + k)
                    for tile, row in ((b_bc, 0), (c_bc, DS)):
                        r = row + 8 * half + 2 * k
                        src = bc_d[b, r:r + 2, :].rearrange("a n -> (a n)").partition_broadcast(P)
                        sp.dma_start(tile[:, 2 * k:2 * k + 2, :].rearrange("p a n -> p (a n)"), src)\
                            .then_inc(bc_in[k], 16)
                elif kind == "stack":
                    p, = a
                    b, sb_ = divmod(p, 8)
                    sp.wait_ge(hl_stored, 64 * (4 * b + 2 * (sb_ // 4) + 2))
                    if p >= 2:
                        sp.wait_ge(t_full, 5 * (p - 1))
                    for h in range(2):
                        head = 2 * sb_ + h
                        q = qk_d[b, 0, head].rearrange("s p n -> (s p) n")
                        k = qk_d[b, 1, head].rearrange("s p n -> (s p) n")
                        for dst, rows, src in ((q_st, (0, 64), q), (q_st, (64, 128), q), (k_st, (0, 64), k),
                                               (k_st, (64, 96), k[32:64]), (k_st, (96, 128), k[0:32])):
                            sp.dma_start(dst[rows[0]:rows[1], p % 2, h, :].bitcast(F32), src).then_inc(stack_in[p % 2], 16)
                elif kind == "resid":
                    b, = a
                    if b:
                        sp.wait_ge(x2_stored, 16 * b)
                    sp.dma_start(xr[:], t_in["x"][b].rearrange("t p n -> p t n")).then_inc(resid_in, 16)
                elif kind == "x2store":
                    b, = a
                    emptied(sp, TASK["yt", b, ET - 1])
                    sp.dma_start(x2_d[b].rearrange("t p n -> p t n"), xr[:]).then_inc(x2_stored, 16)

            sp.wait_ge(x2_stored, 16 * B)
            sp.wait_ge(y_done, SUBS * SLOTS)
            sp.wait_ge(p_ready, 5 * SLOTS)
            sp.wait_ge(norm_done, SLOTS // 2)
            sp.wait_ge(gated, B * ET)
            for n, w in enumerate(("w_fc", "w_pr")):
                sp.dma_start(stage[:, n, :], t_in[w]).then_inc(fw_in[n], 16)
            sp.wait_ge(tern_done, 16)
            for t in range(B * LT):
                if t >= XF:
                    sp.wait_ge(y_ready, t - XF + 1)
                sp.dma_start(xf[:, t % XF, :], x2_d[t // LT, t % LT]).then_inc(xf_in[t % XF], 16)
                if t >= XF:
                    d = t - XF
                    sp.dma_start(out[d // LT, d % LT], y_out[:, d % 2, :]).then_inc(y_stored[d % 2], 16)
            for t in range(B * LT - XF, B * LT):
                sp.wait_ge(y_ready, t + 1)
                sp.dma_start(out[t // LT, t % LT], y_out[:, t % 2, :]).then_inc(y_stored[t % 2], 16)
            for n in range(2):
                sp.wait_ge(y_stored[n], 16 * B * LT // 2)

        @block.gpsimd
        def _(pool):
            for ap, value in ((ones[:], 1.0), (neg_half[:], -0.5), (x_pad[:, 0:TAPS - 1], 0.0),
                              (da[:, :, :, 0:1], 0.0)):
                nc.gpsimd.memset(ap, value).then_inc(pool_set, 1)
            for ap in (ident_b, mask_qk, mask_kq):
                nc.gpsimd.memset(ap[:], 0.0).then_inc(pool_set, 1)
            pool.wait_ge(pool_set, 7)
            for ap, keep, fill, step in ((ident_b, ALU.not_equal, 1.0, -1), (mask_qk, ALU.is_ge, MASKED, -1),
                                         (mask_kq, ALU.is_ge, MASKED, 1)):
                nc.gpsimd.affine_select(out=ap[:], in_=ap[:], compare_op=keep, fill=fill, base=0,
                                        pattern=[[step, P]], channel_multiplier=-step).then_inc(pool_set, 1)

            for kind, *a in ORDER["pool"]:
                if kind == "dbu":
                    j, = a
                    b, half, et, k = sub(j)
                    pool.wait_ge(du_ready, ET * b + et + 1)
                    pool.wait_ge(bc_in[k], 32 * (2 * b + half + 1))
                    if j >= 3:
                        pool.wait_ge(y_done, j - 2)
                    nc.gpsimd.tensor_tensor(hb[:, j % 3], du[:, et, :].unsqueeze(1).to_broadcast([P, 2, L]),
                                            b_bc[:, 2 * k:2 * k + 2, :], ALU.mult).then_inc(dbu_ready, 1)
                elif kind == "ch" and a[0] % SUBS in POOL_CH:
                    j, = a
                    k = j % SUBS
                    pool.wait_ge(scan_done, j + 1)
                    nc.gpsimd.tensor_tensor(hb[:, j % 3], hb[:, j % 3], c_bc[:, 2 * k:2 * k + 2, :], ALU.mult)\
                        .then_inc(ch_done["pool"], 1)
                elif kind == "ln1a":
                    b, t = a
                    i = LT * b + t
                    pool.wait_ge(ln1_var, i + 1)
                    nc.gpsimd.tensor_tensor(rstd[:, i % 2], mv[:, i % 2, 1:2], neg_half[:, 0:1], ALU.pow)\
                        .then_inc(ln1_rstd, 1)
                elif kind == "ln2a":
                    b, = a
                    pool.wait_ge(ln2_var, b + 1)
                    nc.gpsimd.tensor_tensor(rstd2[:], ve2[:], neg_half[:], ALU.pow).then_inc(ln2_rstd, 1)

            for t in range(B * LT):
                for n in range(2):
                    pool.wait_ge(fx_var, 2 * t + n + 1)
                    nc.gpsimd.tensor_tensor(fx[:, t % 2, 2 + n:3 + n], fx[:, t % 2, 4 + n:5 + n],
                                            neg_half[:, 0:1], ALU.pow).then_inc(fx_pow, 1)
                if t >= 1:
                    pool.wait_ge(fh_var, t)
                    nc.gpsimd.tensor_tensor(fh[:, (t - 1) % 2, 2:3], fh[:, (t - 1) % 2, 4:5],
                                            neg_half[:, 0:1], ALU.pow).then_inc(fh_pow, 1)
            t = B * LT - 1
            pool.wait_ge(fh_var, t + 1)
            nc.gpsimd.tensor_tensor(fh[:, t % 2, 2:3], fh[:, t % 2, 4:5], neg_half[:, 0:1], ALU.pow)\
                .then_inc(fh_pow, 1)

        @block.scalar
        def _(act):
            own = Own(act, act_own)
            act.wait_ge(consts_in, ALL_CONSTS)
            nc.scalar.activation(a_neg[:], a_log, ACT.Exp).then_inc(a_exp, 1)
            nc.scalar.activation(pick[:], pick_f[:], ACT.Copy).then_inc(pick_ready, 1)
            act.wait_ge(pool_set, 10)

            for kind, *a in ORDER["act"]:
                if kind == "exp":
                    j, = a
                    b, half, et, k = sub(j)
                    act.wait_ge(a_ready, 1)
                    act.wait_ge(delta_ready, ET * b + et + 1)
                    if j >= 2:
                        act.wait_ge(scan_done, j - 1)
                    for m in range(2):
                        n = 8 * half + 2 * k + m
                        ins = nc.scalar.activation(da[:, j % 2, m, 1:L], delta[:, et, 1:L], ACT.Exp,
                                                   scale=a_neg[:, et, n:n + 1])
                    ins.then_inc(da_ready, 1)
                elif kind == "ln1b":
                    b, t = a
                    n = TASK[kind, b, t]
                    act.wait_ge(m_full, n + 1)
                    if b and t == 0:
                        act.wait_ge(m_full, TASK["v", b - 1, 1, 1] + 1)
                    nc.scalar.activation(xn_t[:, :, P * t:P * t + P], M[n % 2].rearrange("p (d k) -> p d k", d=KD),
                                         ACT.Copy).then_inc(m_free["act"], 1)
                elif kind == "inproj":
                    b, et = a
                    n = TASK[kind, b, et]
                    i = ET * b + et
                    act.wait_ge(m_full, n + 1)
                    if i:
                        act.wait_ge(conv_done, 3 * i)
                    if b:
                        act.wait_ge(yacc_done, 8 * (b - 1) + et + 1)
                        act.wait_ge(du_ready, ET * (b - 1) + et + 1)
                    nc.scalar.activation(u[:, et, :], M[n % 2], ACT.Identity, bias=conv_b[:, et, :],
                                         scale=conv_w[:, et, TAPS - 1:TAPS])
                    nc.scalar.activation(x_pad[:, TAPS - 1:TAPS - 1 + L], M[n % 2], ACT.Copy)\
                        .then_inc(m_free["act"], 1)
                elif kind == "silu":
                    b, et = a
                    act.wait_ge(conv_done, 3 * (ET * b + et + 1))
                    nc.scalar.activation(u[:, et, :], u[:, et, :], ACT.Silu).then_inc(u_ready, 1)
                elif kind == "xproj":
                    b, = a
                    n = TASK[kind, b]
                    act.wait_ge(m_full, n + 1)
                    if b:
                        act.wait_ge(bc_stored, 16 * b)
                        act.wait_ge(m_full, TASK["dt", b - 1, ET - 1] + 1)
                    nc.scalar.activation(x_dbl[:], M[n % 2][0:DR + 2 * DS, :], ACT.Copy).then_inc(m_free["act"], 1)
                elif kind == "dt":
                    b, et = a
                    n = TASK[kind, b, et]
                    act.wait_ge(m_full, n + 1)
                    act.wait_ge(scratch_free, SCRATCH["dt", b, et])
                    nc.scalar.activation(tmp[:, 0, :], M[n % 2], ACT.Identity, bias=dt_b[:, et, :])\
                        .then_inc(m_free["act"], 1)
                    act.wait_ge(m_free["act"], FREED[n][1])
                    own.done(nc.scalar.activation(tmp[:, 1, :], tmp[:, 0, :], ACT.Abs))
                    own.settle()
                    own.done(nc.scalar.activation(tmp[:, 1, :], tmp[:, 1, :], ACT.Exp, scale=-1.0))
                    own.settle()
                    nc.scalar.activation(tmp[:, 2, :], tmp[:, 1, :], ACT.Ln, bias=1.0).then_inc(sp_ready, 1)
                elif kind == "hi":
                    b, n = a
                    i = 4 * b + n
                    act.wait_ge(rot_done, i + 1)
                    if i:
                        act.wait_ge(hl_stored, 64 * i)
                    nc.scalar.activation(hl[:, 0:2, :], tmp[:, 0:2, :], ACT.Copy).then_inc(hi_ready, 1)
                elif kind == "v":
                    b, c, tt = a
                    n = TASK[kind, b, c, tt]
                    act.wait_ge(m_full, n + 1)
                    if b:
                        act.wait_ge(pv_done, 8 * (b - 1) + 4 * (c + 1))
                    nc.scalar.activation(v_sb[:, 2 * tt:2 * tt + 2, CH * c:CH * c + CH],
                                         M[n % 2].rearrange("p (t n) -> p t n", t=2), ACT.Copy)\
                        .then_inc(m_free["act"], 1)
                elif kind == "mt":
                    p, = a
                    act.wait_ge(s_full, 6 * p + 6)
                    if p:
                        act.wait_ge(t_full, 5 * p)
                    nc.scalar.activation(m_row[:], R[(11 * p + 5) % 3][0:2, :], ACT.Copy).then_inc(m_row_ready, 1)
                elif kind == "t":
                    p, n = a
                    bank = R[(11 * p + 6 + n) % 3]
                    act.wait_ge(t_full, 5 * p + n + 1)
                    if p:
                        act.wait_ge(pv_done, p)
                    if n < 4:
                        dst = p_t[:, n // 2, 512 * (n % 2):512 * (n % 2) + 512]
                        src = bank
                    else:
                        dst = p_t[:, :, P_AT[2]:P_AT[2] + 256]
                        src = bank.rearrange("p (h n) -> p h n", h=2)
                    nc.scalar.activation(dst, src, ACT.Exp, scale=SCALE).then_inc(p_ready, 1)
                elif kind == "zt":
                    g, = a
                    act.wait_ge(pv_done, 2 * g + 2)
                    if g:
                        act.wait_ge(m_full, TASK[kind, g - 1] + 1)
                    nc.scalar.activation(z_sb[:], Z_B, ACT.Copy).then_inc(z_copied, 1)
                elif kind == "zb":
                    g, = a
                    n = TASK[kind, g]
                    act.wait_ge(m_full, n + 1)
                    if g % 4 == 0 and g:
                        act.wait_ge(m_full, TASK["wo", g // 4 - 1, 1, 1] + 1)
                    nc.scalar.activation(o_t[:, g % 4, :], M[n % 2], ACT.Copy).then_inc(m_free["act"], 1)
                elif kind == "gate":
                    b, et = a
                    act.wait_ge(ln2_ready, b + 1)
                    if b or et:
                        act.wait_ge(gated, ET * b + et)
                    nc.scalar.activation(gate[:], xr[:, et, :], ACT.Silu, bias=nmr2[:, et:et + 1],
                                         scale=rstd2[:, et:et + 1]).then_inc(gate_ready, 1)

            act.wait_ge(fw_in[1], 16)
            nc.scalar.activation(t_pr[:].rearrange("p a n -> p (a n)"), stage[:, 1, :], ACT.Abs,
                                 accum_out=w_sum[:, 1:2]).then_inc(wsum_act, 1)
            act.wait_ge(tern_done, 16)
            tr = 0

            def high(dst):
                nonlocal tr
                act.wait_ge(tr_full, tr + 1)
                nc.scalar.activation(dst, ps[:, 4 + tr % 2, :].rearrange("p (k n) -> p k n", n=P), ACT.Copy)\
                    .then_inc(tr_hi, 1)
                tr += 1

            def hidden(t):
                for n in range(4):
                    act.wait_ge(fc_full, 4 * t + n + 1)
                    if t >= 2:
                        act.wait_ge(tr_full, tr_count(t - 2))
                    nc.scalar.activation(h_sb[:, t % 2, 512 * n:512 * n + 512], ps[:, n, :], ACT.Gelu,
                                         scale=gam[:, 0:1]).then_inc(gelu_done, 1)
                act.wait_ge(fh_nmr, t + 1)
                nc.scalar.activation(h_sb[:, t % 2, :], h_sb[:, t % 2, :], ACT.Identity,
                                     bias=fh[:, t % 2, 3:4], scale=fh[:, t % 2, 2:3]).then_inc(hn_done, 1)

            for step, t in ffn_steps():
                if step == "xt":
                    if t >= 2:
                        act.wait_ge(fc_full, 4 * (t - 1))
                    high(xq_hi[:, t % 2])
                elif step == "fc":
                    hidden(t)
                elif step == "ht":
                    if t:
                        act.wait_ge(proj_full, t)
                    for n in range(4):
                        high(hq_hi[:, 4 * n:4 * n + 4])

        @block.tensor
        def _(pe):
            pe.wait_ge(consts_in, ALL_CONSTS)
            pe.wait_ge(pool_set, 10)

            def chunk_in(c):
                pe.wait_ge(w_in[c % 2], 16 * (c // 2 + 1))

            for kind, *a in ORDER["pe"]:
                if kind == "ln1b":
                    b, t = a
                    n, i = TASK[kind, b, t], LT * b + t
                    pe.wait_ge(ln1_done, i + 1)
                    freed(pe, n)
                    for d in range(KD):
                        mm = nc.tensor.transpose(M[n % 2][:, P * d:P * d + P], x_in[:, i % 2, P * d:P * d + P],
                                                 ident[:])
                    mm.then_inc(m_full, 1)
                elif kind == "inproj":
                    b, et = a
                    n = TASK[kind, b, et]
                    pe.wait_ge(ctx_in_s, 16 * (b + 1))
                    freed(pe, n)
                    for d in range(KC):
                        mm = nc.tensor.matmul(M[n % 2], in_w[:, d, P * et:P * et + P], ctx_in[:, d, :],
                                              start=(d == 0), stop=(d == KC - 1))
                    mm.then_inc(m_full, 1)
                elif kind == "xproj":
                    b, = a
                    n = TASK[kind, b]
                    pe.wait_ge(u_ready, ET * (b + 1))
                    freed(pe, n)
                    for et in range(ET):
                        mm = nc.tensor.matmul(M[n % 2][0:DR + 2 * DS, :], xp_w[:, et, :], u[:, et, :],
                                              start=(et == 0), stop=(et == ET - 1))
                    mm.then_inc(m_full, 1)
                elif kind == "dt":
                    b, et = a
                    n = TASK[kind, b, et]
                    emptied(pe, TASK["xproj", b])
                    freed(pe, n)
                    nc.tensor.matmul(M[n % 2], dt_w[:, P * et:P * et + P], x_dbl[0:DR, :], start=True, stop=True)\
                        .then_inc(m_full, 1)
                elif kind == "rot":
                    b, n, half = a
                    c = CHUNK_OF[kind, b, n]
                    task = TASK[(kind, *a)]
                    chunk_in(c)
                    emptied(pe, TASK["ln1b", b, LT - 1])
                    freed(pe, task)
                    for d in range(KD):
                        mm = nc.tensor.matmul(M[task % 2], w_ring[:, c % 2, d, P * half:P * half + P],
                                              xn_t[:, d, :], start=(d == 0), stop=(d == KD - 1))
                    mm.then_inc(m_full, 1)
                elif kind == "v":
                    b, c, tt = a
                    wc = CHUNK_OF[kind, b, c]
                    n = TASK[kind, b, c, tt]
                    chunk_in(wc)
                    emptied(pe, TASK["ln1b", b, LT - 1])
                    freed(pe, n)
                    for m in range(2):
                        t = 2 * tt + m
                        for d in range(KD):
                            mm = nc.tensor.matmul(M[n % 2][:, CH * m:CH * m + CH], xn_t[:, d, P * t:P * t + P],
                                                  w_ring[:, wc % 2, d, :], start=(d == 0), stop=(d == KD - 1))
                    mm.then_inc(m_full, 1)
                elif kind == "s":
                    p, n = a
                    pe.wait_ge(stack_in[p % 2], 160 * (p // 2 + 1))
                    ring_free(11 * p + n)
                    bank = R[(11 * p + n) % 3]
                    for h, i, col in S_UNITS[n]:
                        w = P * (i + 1)
                        nc.tensor.matmul(bank[:, col:col + w], q_st[:, p % 2, h, P * i:P * i + P],
                                         k_st[:, p % 2, h, 0:w], start=True, stop=False)
                        mm = nc.tensor.matmul(bank[:, col + w - P:col + w], ident_b[:], mask_qk[:],
                                              start=False, stop=True)
                    mm.then_inc(s_full, 1)
                elif kind == "mt":
                    p, = a
                    pe.wait_ge(max_done, 5 * p + 5)
                    ring_free(11 * p + 5)
                    for i in range(LT):
                        mm = nc.tensor.transpose(R[(11 * p + 5) % 3][0:2, P * i:P * i + P], m_col[:, i, :], ident[:])
                    mm.then_inc(s_full, 1)
                elif kind == "t":
                    p, n = a
                    pe.wait_ge(m_row_ready, p + 1)
                    pe.wait_ge(pick_ready, 1)
                    ring_free(11 * p + 6 + n)
                    bank = R[(11 * p + 6 + n) % 3]
                    for h, jt, col in T_UNITS[n]:
                        w = L - P * jt
                        nc.tensor.matmul(bank[:, col:col + w], k_st[:, p % 2, h, P * jt:P * jt + P],
                                         q_st[:, p % 2, h, P * jt:L], start=True, stop=False)
                        nc.tensor.matmul(bank[:, col:col + P], ident_b[:], mask_kq[:], start=False, stop=False)
                        mm = nc.tensor.matmul(bank[:, col:col + w], pick[:, h, :], m_row[:, P * jt:L],
                                              start=False, stop=True)
                    mm.then_inc(t_full, 1)
                elif kind == "pv":
                    p, = a
                    b, sb_ = divmod(p, 8)
                    pe.wait_ge(p_ready, 5 * (p + 1))
                    emptied(pe, TASK["v", b, sb_ // 4, 1])
                    if p % 2 == 0 and p:
                        pe.wait_ge(norm_done, p // 2)
                    for jt in range(LT):
                        for h in range(2):
                            head = 2 * sb_ + h
                            rhs = p_t[:, h, P_AT[jt]:P_AT[jt] + L - P * jt]
                            for lhs, bank, quad in ((v_sb[:, jt, HD * head:HD * head + HD], O_B, 2 * (p % 2) + h),
                                                    (ones[:, 0:HD], Z_B, (2 * (p % 2) + h + 2) % 4)):
                                mm = nc.tensor.matmul(bank[HD * quad:HD * quad + HD, P * jt:L], lhs, rhs,
                                                      start=(jt == 0), stop=(jt == LT - 1))
                    mm.then_inc(pv_done, 1)
                elif kind == "y":
                    j, = a
                    wait_ch(pe, j)
                    if j % 4 == 0 and j:
                        pe.wait_ge(yacc_done, j // 4)
                    for m in range(2):
                        mm = nc.tensor.matmul(Y_B, ident[:], hb[:, j % 3, m, :], start=(j % 4 == 0 and m == 0),
                                              stop=(j % 4 == 3 and m == 1))
                    mm.then_inc(y_done, 1)
                elif kind == "wo":
                    b, c, tt = a
                    wc, n = CHUNK_OF[kind, b, c], TASK[(kind, *a)]
                    chunk_in(wc)
                    pe.wait_ge(norm_done, 4 * b + 4)
                    freed(pe, n)
                    for m in range(2):
                        t = 2 * tt + m
                        for g in range(KD):
                            mm = nc.tensor.matmul(M[n % 2][:, CH * m:CH * m + CH], o_t[:, g, P * t:P * t + P],
                                                  w_ring[:, wc % 2, g, :], start=(g == 0), stop=(g == KD - 1))
                    mm.then_inc(m_full, 1)
                elif kind == "zt":
                    g, = a
                    n = TASK[kind, g]
                    pe.wait_ge(z_copied, g + 1)
                    freed(pe, n)
                    for i in range(LT):
                        mm = nc.tensor.transpose(M[n % 2][:, P * i:P * i + P], z_sb[:, P * i:P * i + P], ident[:])
                    mm.then_inc(m_full, 1)
                elif kind == "zb":
                    g, = a
                    n = TASK[kind, g]
                    emptied(pe, TASK["zt", g])
                    freed(pe, n)
                    for i in range(LT):
                        for q in range(4):
                            mm = nc.tensor.matmul(M[n % 2][HD * q:HD * q + HD, P * i:P * i + P],
                                                  z_rec[:, i, q:q + 1].to_broadcast([P, HD]), ident[:],
                                                  start=True, stop=True)
                    mm.then_inc(m_full, 1)
                elif kind == "yt":
                    b, et = a
                    n = TASK[kind, b, et]
                    pe.wait_ge(gated, ET * b + et + 1)
                    freed(pe, n)
                    for lt in range(LT):
                        mm = nc.tensor.transpose(M[n % 2][:, P * lt:P * lt + P],
                                                 y_acc[:, b % 2, et, P * lt:P * lt + P], ident[:])
                    mm.then_inc(m_full, 1)

            pe.wait_ge(wsum_ready, 1)
            pe.wait_ge(wsum_act, 1)
            nc.tensor.matmul(ps[:, 0, 0:2], ones[:], w_sum[:], start=True, stop=True).then_inc(wtot_full, 1)
            tr = 0

            def turn(src, n):
                nonlocal tr
                if tr >= 2:
                    pe.wait_ge(tr_free, tr - 1)
                for d in range(4):
                    mm = nc.tensor.transpose(ps[:, 4 + tr % 2, P * d:P * d + P], src[:, P * (4 * n + d):P * (4 * n + d + 1)],
                                             ident[:])
                mm.then_inc(tr_full, 1)
                tr += 1

            for step, t in ffn_steps():
                if step == "xt":
                    pe.wait_ge(xq_done, t + 1)
                    turn(xq[:, t % 2, :], 0)
                elif step == "fc":
                    pe.wait_ge(tr_free, tr_x(t))
                    for n in range(4):
                        if t:
                            pe.wait_ge(gelu_done, 4 * (t - 1) + n + 1)
                        for d in range(KD):
                            for m, part in enumerate((xq_hi, xq_lo)):
                                mm = nc.tensor.matmul(ps[:, n, :], part[:, t % 2, d, :], t_fc[:, d, 512 * n:512 * n + 512],
                                                      start=(d == 0 and m == 0), stop=(d == KD - 1 and m == 1))
                        mm.then_inc(fc_full, 1)
                elif step == "ht":
                    pe.wait_ge(hq_done, t + 1)
                    for n in range(4):
                        turn(h_sb[:, t % 2, :], n)
                elif step == "proj":
                    if t:
                        pe.wait_ge(y_ready, t)
                    pe.wait_ge(tr_free, tr_count(t))
                    for k in range(FT):
                        for m, part in enumerate((hq_hi, hq_lo)):
                            mm = nc.tensor.matmul(ps[:, 6, :], part[:, k, :], t_pr[:, k, :],
                                                  start=(k == 0 and m == 0), stop=(k == FT - 1 and m == 1))
                    mm.then_inc(proj_full, 1)

        @block.vector
        def _(dve):
            own = Own(dve, dve_own)
            v = nc.vector
            dve.wait_ge(consts_in, ALL_CONSTS)
            dve.wait_ge(pool_set, 10)
            dve.wait_ge(a_exp, 1)
            v.tensor_scalar(a_neg[:], a_neg[:], -1.0, None, ALU.mult).then_inc(a_ready, 1)

            for kind, *a in ORDER["dve"]:
                if kind == "scan":
                    j, = a
                    dve.wait_ge(da_ready, j + 1)
                    dve.wait_ge(dbu_ready, j + 1)
                    h = hb[:, j % 3].rearrange("p a n -> p (a n)")
                    v.tensor_tensor_scan(h, da[:, j % 2].rearrange("p a n -> p (a n)"), h, 0.0, ALU.mult, ALU.add)\
                        .then_inc(scan_done, 1)
                elif kind == "ch":
                    j, = a
                    k = j % 4
                    if k in POOL_CH:
                        continue
                    dve.wait_ge(scan_done, j + 1)
                    v.tensor_tensor(hb[:, j % 3], hb[:, j % 3], c_bc[:, 2 * k:2 * k + 2, :], ALU.mult)\
                        .then_inc(ch_done["dve"], 1)
                elif kind == "yacc":
                    n, = a
                    b, half, et = n // 8, n // 4 % 2, n % 4
                    dve.wait_ge(y_done, 4 * n + 4)
                    y = y_acc[:, b % 2, et, :]
                    if half == 0:
                        if b >= 2:
                            dve.wait_ge(m_full, TASK["yt", b - 2, et] + 1)
                        ins = v.scalar_tensor_tensor(out=y, in0=u[:, et, :], scalar=d_skip[:, et, :], in1=Y_B,
                                                     op0=ALU.mult, op1=ALU.add)
                    else:
                        dve.wait_ge(yacc_done, n - 3)
                        ins = v.tensor_tensor(y, y, Y_B, ALU.add)
                    ins.then_inc(yacc_done, 1)
                elif kind == "ln1a":
                    b, t = a
                    i = LT * b + t
                    dve.wait_ge(x_in_s[i % 2], 16 * (i // 2 + 1))
                    own.settle()
                    own.done(v.bn_stats(stats[:, i % 2], x_in[:, i % 2, :]))
                    own.settle()
                    own.done(v.bn_aggr(mv[:, i % 2], stats[:, i % 2]))
                    own.settle()
                    v.tensor_scalar(mv[:, i % 2, 1:2], mv[:, i % 2, 1:2], EPS, None, ALU.add).then_inc(ln1_var, 1)
                elif kind == "ln1b":
                    b, t = a
                    i = LT * b + t
                    dve.wait_ge(ln1_rstd, i + 1)
                    v.tensor_scalar(x_in[:, i % 2, :], x_in[:, i % 2, :], mv[:, i % 2, 0:1], rstd[:, i % 2],
                                    ALU.subtract, ALU.mult).then_inc(ln1_done, 1)
                elif kind == "inproj":
                    b, et = a
                    i = ET * b + et
                    emptied(dve, TASK[kind, b, et])
                    for tap in range(TAPS - 1):
                        if tap:
                            dve.wait_ge(conv_done, 3 * i + tap)
                        v.scalar_tensor_tensor(out=u[:, et, :], in0=x_pad[:, tap:tap + L],
                                               scalar=conv_w[:, et, tap:tap + 1], in1=u[:, et, :],
                                               op0=ALU.mult, op1=ALU.add).then_inc(conv_done, 1)
                elif kind == "delta":
                    b, et = a
                    i = ET * b + et
                    dve.wait_ge(sp_ready, i + 1)
                    if b:
                        dve.wait_ge(da_ready, 32 * (b - 1) + 16 + 4 * et + 4)
                        dve.wait_ge(dbu_ready, 32 * (b - 1) + 16 + 4 * et + 4)
                    d = delta[:, et, :]
                    own.done(v.tensor_scalar(d, tmp[:, 1, :], 1.0, 1.0, ALU.add, ALU.subtract))
                    own.settle()
                    own.done(v.tensor_tensor(d, tmp[:, 1, :], d, ALU.subtract))
                    own.settle()
                    own.done(v.tensor_tensor(d, d, tmp[:, 2, :], ALU.add))
                    own.settle()
                    own.done(v.scalar_tensor_tensor(out=d, in0=tmp[:, 0, :], scalar=0.0, in1=d,
                                                    op0=ALU.max, op1=ALU.add))
                    own.settle()
                    dve.wait_ge(u_ready, i + 1)
                    v.tensor_tensor(du[:, et, :], d, u[:, et, :], ALU.mult).then_inc(du_ready, 1)
                    v.tensor_scalar(tmp[:, 0, 0:1], d[:, 0:1], 1.0, None, ALU.mult).then_inc(delta_ready, 1)
                    dve.wait_ge(delta_ready, i + 1)
                    v.tensor_copy(tmp[:, 1, 0:1], tmp[:, 0, 0:1]).then_inc(scratch_free, 1)
                elif kind == "rot" and a[2] == 0:
                    b, n, _ = a
                    task = TASK[(kind, *a)]
                    bank = M[task % 2]
                    dve.wait_ge(scratch_free, SCRATCH[kind, b, n])
                    dve.wait_ge(m_full, task + 1)
                    own.done(v.tensor_tensor(tmp[:, 0, :], bank, cos[:], ALU.mult))
                    v.tensor_tensor(tmp[:, 2, :], bank, sin[:], ALU.mult).then_inc(m_free["dve"], 1)
                elif kind == "rot":
                    b, n, _ = a
                    task = TASK[(kind, *a)]
                    bank = M[task % 2]
                    dve.wait_ge(m_full, task + 1)
                    own.done(v.tensor_tensor(tmp[:, 1, :], bank, sin[:], ALU.mult))
                    own.settle()
                    own.done(v.tensor_tensor(tmp[:, 0, :], tmp[:, 0, :], tmp[:, 1, :], ALU.subtract))
                    own.settle()
                    v.tensor_tensor(tmp[:, 1, :], bank, cos[:], ALU.mult).then_inc(m_free["dve"], 1)
                    dve.wait_ge(m_free["dve"], FREED[task][1])
                    v.tensor_tensor(tmp[:, 1, :], tmp[:, 1, :], tmp[:, 2, :], ALU.add).then_inc(rot_done, 1)
                elif kind == "lo":
                    b, n = a
                    i = 4 * b + n
                    dve.wait_ge(hi_ready, i + 1)
                    v.tensor_tensor(hl[:, 2:4, :], tmp[:, 0:2, :], hl[:, 0:2, :].bitcast(F32), ALU.subtract)\
                        .then_inc(scratch_free, 1)
                elif kind == "s":
                    p, n = a
                    bank = R[(11 * p + n) % 3]
                    dve.wait_ge(s_full, 6 * p + n + 1)
                    if n == 4:
                        v.tensor_reduce(m_col[:, 1, :], bank.rearrange("p (h n) -> p h n", h=2), AX.X, ALU.max,
                                        negate=True).then_inc(max_done, 1)
                    else:
                        for h, i, col in S_UNITS[n]:
                            ins = v.tensor_reduce(m_col[:, i, h:h + 1], bank[:, col:col + P * (i + 1)], AX.X, ALU.max,
                                                  negate=True)
                        ins.then_inc(max_done, 1)
                elif kind == "zt":
                    g, = a
                    n = TASK[kind, g]
                    dve.wait_ge(m_full, n + 1)
                    if g:
                        dve.wait_ge(m_full, TASK["zb", g - 1] + 1)
                    sums = M[n % 2].rearrange("p (t h c) -> p t h c", t=LT, h=4)
                    own.done(v.reciprocal(z_rec[:, :, 0:2], sums[:, :, 2:4, 0]))
                    own.settle()
                    v.reciprocal(z_rec[:, :, 2:4], sums[:, :, 0:2, 0]).then_inc(m_free["dve"], 1)
                elif kind == "norm":
                    n, = a
                    b, g = divmod(n, 4)
                    emptied(dve, TASK["zb", n])
                    v.tensor_tensor(o_t[:, g, :], O_B, o_t[:, g, :], ALU.mult).then_inc(norm_done, 1)
                elif kind == "wo":
                    b, c, tt = a
                    n = TASK[(kind, *a)]
                    dve.wait_ge(resid_in, 16 * (b + 1))
                    dve.wait_ge(m_full, n + 1)
                    dst = xr[:, 2 * tt:2 * tt + 2, CH * c:CH * c + CH]
                    v.tensor_tensor(dst, M[n % 2].rearrange("p (t n) -> p t n", t=2), dst, ALU.add)\
                        .then_inc(m_free["dve"], 1)
                elif kind == "ln2a":
                    b, = a
                    emptied(dve, TASK["wo", b, 1, 1])
                    for t in range(LT):
                        own.done(v.bn_stats(stats2[:, t], xr[:, t, :]))
                    own.settle()
                    for t in range(LT):
                        own.done(v.bn_aggr(mv2[:, t], stats2[:, t]))
                    own.settle()
                    v.tensor_scalar(ve2[:], mv2[:, :, 1], EPS, None, ALU.add).then_inc(ln2_var, 1)
                elif kind == "ln2b":
                    b, = a
                    dve.wait_ge(ln2_rstd, b + 1)
                    v.scalar_tensor_tensor(out=nmr2[:], in0=mv2[:, :, 0], scalar=-1.0, in1=rstd2[:],
                                           op0=ALU.mult, op1=ALU.mult).then_inc(ln2_ready, 1)
                elif kind == "gate":
                    b, et = a
                    dve.wait_ge(gate_ready, ET * b + et + 1)
                    dve.wait_ge(yacc_done, 8 * b + 4 + et + 1)
                    y = y_acc[:, b % 2, et, :]
                    v.tensor_tensor(y, y, gate[:], ALU.mult).then_inc(gated, 1)
                elif kind == "yt":
                    b, et = a
                    n = TASK[kind, b, et]
                    dve.wait_ge(m_full, n + 1)
                    dst = xr[:, :, P * et:P * et + P]
                    v.tensor_tensor(dst, M[n % 2].rearrange("p (t n) -> p t n", t=LT), dst, ALU.add)\
                        .then_inc(m_free["dve"], 1)

            dve.wait_ge(fw_in[0], 16)
            v.tensor_reduce(w_sum[:, 0:1], stage[:, 0, :], AX.X, ALU.add, apply_absolute_value=True)\
                .then_inc(wsum_ready, 1)
            dve.wait_ge(wtot_full, 1)
            own.done(v.tensor_scalar(gam[:], ps[:, 0, 0:2], 1.0 / (DM * FF), None, ALU.mult))
            own.settle()
            own.done(v.tensor_scalar(thr[:], gam[:], EPS_Q, 0.5, ALU.add, ALU.mult))
            own.done(v.tensor_scalar(nthr[:], gam[:], EPS_Q, -0.5, ALU.add, ALU.mult))
            own.settle()
            dve.wait_ge(fw_in[1], 16)
            for n in range(8):
                w, c = divmod(n, 4)
                src = stage[:, w, FF * c:FF * c + FF]
                dst = t_fc[:, c, :] if w == 0 else t_pr[:, 4 * c:4 * c + 4, :].rearrange("p a n -> p (a n)")
                if n >= 2:
                    dve.wait_ge(tern_done, 2 * n - 2)
                v.tensor_scalar(low[:, n % 2, :], src, nthr[:, w:w + 1], None, ALU.is_lt).then_inc(tern_done, 1)
                dve.wait_ge(tern_done, 2 * n + 1)
                v.scalar_tensor_tensor(out=dst, in0=src, scalar=thr[:, w:w + 1], in1=low[:, n % 2, :],
                                       op0=ALU.is_gt, op1=ALU.subtract).then_inc(tern_done, 1)
            dve.wait_ge(tern_done, 16)
            tr = 0

            def low_part(dst, hi):
                nonlocal tr
                dve.wait_ge(tr_hi, tr + 1)
                v.tensor_tensor(dst, ps[:, 4 + tr % 2, :].rearrange("p (k n) -> p k n", n=P), hi.bitcast(F32),
                                ALU.subtract).then_inc(tr_free, 1)
                tr += 1

            def quantize(x, f, sig):
                own.done(v.tensor_reduce(f[:, 8:9], x, AX.X, ALU.max, apply_absolute_value=True))
                own.settle()
                own.done(v.reciprocal(f[:, 9:10], f[:, 8:9]))
                own.done(v.tensor_scalar(f[:, 11:12], f[:, 8:9], 1.0 / Q_B, None, ALU.mult))
                own.settle()
                own.done(v.tensor_scalar(f[:, 10:11], f[:, 9:10], Q_B, None, ALU.mult))
                own.settle()
                own.done(v.tensor_scalar(x, x, f[:, 10:11], Q_B, ALU.mult, ALU.min))
                own.settle()
                v.tensor_scalar(x, x, -Q_B, f[:, 11:12], ALU.max, ALU.mult).then_inc(sig, 1)

            def x_norm(t):
                f, x = fx[:, t % 2], xf[:, t % XF, :]
                dve.wait_ge(xf_in[t % XF], 16 * (t // XF + 1))
                own.settle()
                own.done(v.bn_stats(st_x[:, t % 2], x))
                own.settle()
                own.done(v.bn_aggr(f[:, 0:2], st_x[:, t % 2]))
                own.settle()
                v.tensor_scalar(f[:, 4:5], f[:, 1:2], EPS, None, ALU.add).then_inc(fx_var, 1)
                dve.wait_ge(fx_pow, 2 * t + 1)
                own.done(v.tensor_scalar(f[:, 6:7], f[:, 1:2], f[:, 2:3], f[:, 2:3], ALU.mult, ALU.mult))
                own.settle()
                v.tensor_scalar(f[:, 5:6], f[:, 6:7], EPS_Q, None, ALU.add).then_inc(fx_var, 1)
                dve.wait_ge(fx_pow, 2 * t + 2)
                own.done(v.tensor_scalar(f[:, 7:8], f[:, 2:3], f[:, 3:4], None, ALU.mult))
                own.settle()
                if t >= 2:
                    dve.wait_ge(tr_full, tr_xfull(t - 2))
                own.done(v.tensor_scalar(xq[:, t % 2, :], x, f[:, 0:1], f[:, 7:8], ALU.subtract, ALU.mult))
                own.settle()
                quantize(xq[:, t % 2, :], f, xq_done)

            x_norm(0)
            for step, t in ffn_steps():
                if step == "xt":
                    if t >= 2:
                        dve.wait_ge(fc_full, 4 * (t - 1))
                    low_part(xq_lo[:, t % 2], xq_hi[:, t % 2])
                    if t + 1 < B * LT:
                        x_norm(t + 1)
                elif step == "fc":
                    f = fh[:, t % 2]
                    for n in range(4):
                        dve.wait_ge(gelu_done, 4 * t + n + 1)
                        own.done(v.bn_stats(st_h[:, t % 2, n], h_sb[:, t % 2, 512 * n:512 * n + 512]))
                    own.settle()
                    own.done(v.bn_aggr(f[:, 0:2], st_h[:, t % 2]))
                    own.settle()
                    v.tensor_scalar(f[:, 4:5], f[:, 1:2], EPS_Q, None, ALU.add).then_inc(fh_var, 1)
                    dve.wait_ge(fh_pow, t + 1)
                    v.tensor_scalar(f[:, 3:4], f[:, 0:1], f[:, 2:3], -1.0, ALU.mult, ALU.mult).then_inc(fh_nmr, 1)
                    dve.wait_ge(hn_done, t + 1)
                    quantize(h_sb[:, t % 2, :], f, hq_done)
                elif step == "ht":
                    if t:
                        dve.wait_ge(proj_full, t)
                    for n in range(4):
                        low_part(hq_lo[:, 4 * n:4 * n + 4], hq_hi[:, 4 * n:4 * n + 4])
                elif step == "proj":
                    dve.wait_ge(proj_full, t + 1)
                    if t >= 2:
                        dve.wait_ge(y_stored[t % 2], 16 * (t // 2))
                    v.scalar_tensor_tensor(out=y_out[:, t % 2, :], in0=ps[:, 6, :], scalar=gam[:, 1:2],
                                           in1=xf[:, t % XF, :], op0=ALU.mult, op1=ALU.add).then_inc(y_ready, 1)


def ffn_steps():
    n = B * LT
    yield ("xt", 0)
    for t in range(n + 1):
        if t < n:
            yield ("fc", t)
            if t + 1 < n:
                yield ("xt", t + 1)
        if t:
            yield ("ht", t - 1)
            yield ("proj", t - 1)


def tr_order():
    n, at = 0, {}
    for step, t in ffn_steps():
        if step in ("xt", "ht"):
            n += 1 if step == "xt" else 4
            at[step, t] = n
    return at


TR = tr_order()


def tr_x(t):
    return TR["xt", t]


tr_xfull = tr_x


def tr_count(t):
    return TR["ht", t]


def constants():
    import numpy as np

    pos = np.arange(L, dtype=np.float32)
    inv = (1.0 / np.float32(10000.0) ** (np.arange(0, HD, 2, dtype=np.float32) / np.float32(HD))).astype(np.float32)
    angle = np.tile((inv[:, None] * pos[None, :]).astype(np.float32), (P // HALF, 1))
    pick = np.zeros((2, 2, P), np.float32)
    pick[0, 0] = pick[1, 1] = 1.0
    return {
        "cos": np.cos(angle).astype(np.float32), "sin": np.sin(angle).astype(np.float32),
        "ident": np.eye(P, dtype=np.float32), "pick": pick,
    }


def kernel(**inputs):
    import numpy as np
    import concourse.bacc as bacc
    from concourse.bass_utils import run_bass_kernel_spmd

    a = {k: np.ascontiguousarray(v) for k, v in inputs.items()}

    def rows(w):
        return w.reshape(w.shape[0] // P, P, w.shape[1]).transpose(1, 0, 2)

    w = a["L0_attn_w_qkv"].reshape(DM, 3, NH, 2, HALF)
    chunks = []
    for half in range(2):
        for which in range(2):
            part = w[:, which, 8 * half:8 * half + 8]
            chunks.append(rows(part.transpose(0, 2, 1, 3).reshape(DM, CH)))
    wv = a["L0_attn_w_qkv"][:, 2 * DM:]
    for m in (wv, a["L0_attn_w_o"]):
        for c in range(2):
            chunks.append(rows(m[:, CH * c:CH * c + CH]))

    def cols(m):
        return m.reshape(ET, P, -1).transpose(1, 0, 2)

    arrays = {
        "x": a["x"].reshape(B, LT, P, DM),
        "ctx": a["ctx_1024"].transpose(0, 2, 1).reshape(B, KC, P, L).transpose(0, 2, 1, 3),
        "w_attn": np.stack(chunks),
        "in_w": rows(a["L0_xattn_in_proj_w"].T),
        "xp_w": rows(a["L0_xattn_x_proj_w"].T),
        "dt_w": a["L0_xattn_dt_proj_w"].T,
        "small": np.concatenate([cols(a["L0_xattn_conv_w"]), cols(a["L0_xattn_conv_b"]),
                                 cols(a["L0_xattn_dt_proj_b"]), cols(a["L0_xattn_D"]),
                                 cols(a["L0_xattn_A_log"])], axis=2),
        "w_fc": rows(a["L0_ffn_w_fc"].T).reshape(P, KD * FF),
        "w_pr": rows(a["L0_ffn_w_proj"].T).reshape(P, FT * DM),
        **constants(),
    }
    arrays = {f"in_{k}": np.ascontiguousarray(v) for k, v in arrays.items()}
    nc = bacc.Bacc("TRN2", target_bir_lowering=False, num_devices=1)
    t_in = {k[3:]: nc.dram_tensor(k, v.shape, mybir.dt.from_np(v.dtype), kind="ExternalInput").ap()
            for k, v in arrays.items()}
    out = nc.dram_tensor("out_y", (B, LT, P, DM), F32, kind="ExternalOutput").ap()
    layer_kernel(nc, t_in, out)
    r = run_bass_kernel_spmd(nc, [arrays], core_ids=[0])
    return r.results[0]["out_y"].reshape(B, L, DM)
```

```python
from contextlib import ExitStack

import concourse.bass as bass
from concourse import mybir

F32 = mybir.dt.float32
F32R = mybir.dt.float32r
BF16 = mybir.dt.bfloat16
ALU = mybir.AluOpType
ACT = mybir.ActivationFunctionType
AX = mybir.AxisListType

P = 128
B, L, DM = 4, 512, 512
NH, HD = 16, 32
HALF = HD // 2
DC, DS, DR, TAPS = 256, 16, 16, 4
FF = 4 * DM
LT = L // P
ET = DM // P
KD = DM // P
KC = DC // P
FT = FF // P
SCALE = float(HD) ** -0.5
EPS = 1e-5
EPS_Q = 1e-6
Q_B = 128.0
MASKED = -1e30

SLOTS = B * 8
SUBS = 4
CH = 256
DA_RING, HB_RING = 2, 4
XF = 7

P_AT = [0, 512, 1024, 896]
P_W = 1280


TICKS = 12
POOL_CH = (1, 3), (1, 3)
PAIRED = (0, 1, 2, 3), ()


def is_last(j):
    return j >= SUBS * SLOTS * (B - 1) // B


def on_pool(j):
    return j % SUBS in POOL_CH[is_last(j)]


def is_paired(j):
    return j % SUBS in PAIRED[is_last(j)]


MIXER = [{
    "exp": [-3.9, -1, 1.9, 6.2], "dbu": [-1.1, 0.5, 2.5, 4.9], "scan": [-3.6, 1.9, 4.9, 7.9], "ch": [1.2, 4.1, 7.3, 9.4],
    "pair": [2.2, 5.5, 8.3, 11.3], "y": [4.8, 7.8, 10.9, 13.7], "yacc": [14],
    "stack": [-14.6], "s": [0, 1, 1.4, 3, 4], "mt": [5.5], "t": [6.6, 7.5, 8.5, 9.6, 10.5], "pv": [15],
}, {
    "exp": [-3.9, -1, 2.9, 6.2], "dbu": [-3.3, -0.1, 2.2, 5.6], "scan": [-3.7, 1.8, 4.8, 7.8], "ch": [1, 3.1, 5.9, 11.3],
    "pair": [2.2, 5.5, 7.1, 10.7], "y": [4.8, 7.8, 10.8, 13.7], "yacc": [14.1],
    "stack": [-13.5], "s": [0, 1, 1.4, 3.1, 4], "mt": [5.1], "t": [6.2, 7.5, 8.5, 9.6, 10.5], "pv": [12.5],
}, {
    "exp": [-3.9, -1, 1.9, 6.2], "dbu": [-4.5, -0.6, 1.5, 4.6], "scan": [-3, 1.3, 5.4, 7.4], "ch": [-0.5, 3.2, 6.6, 9.4],
    "pair": [2.7, 3.2, 7.1, 12.3], "y": [5.2, 7.8, 10.6, 13.4], "yacc": [13.8],
    "stack": [-12.2], "s": [-0.1, 0.4, 0.9, 2.4, 3.3], "mt": [5.3], "t": [5.9, 7.5, 8.5, 8.9, 10.2], "pv": [12.4],
}]
QUOTIENT = {"zt": [13.2], "zb": [16], "norm": [17.7]}
BEFORE = [{
    "xload": [-93.7, -93.5, -92, -90.6], "ln1a": [-94.5, -94.4, -91.9, -89.1], "ln1b": [-93, -92.9, -90.2, -87.4],
    "cload": [-94.7], "inproj": [-86, -82.9, -78.6, -74.6], "silu": [-81.2, -80, -75.7, -72.3], "xproj": [-69.4],
    "bcload": [-72.9, -65.8, -64.2, -61.6], "rot": [-79.7, -75.9, -72.6, -65.7, 10.9, 12, 21.5, 23.6],
    "hi": [-74.8, -65.2, 13.2, 24.1], "lo": [-72.6, -64.5, 14.2, 25], "dt": [-62, -58.8, 16.4, 28],
    "delta": [-63, -56.1, 15.7, 29.3], "du": [-59.4, -54.2, 18.7, 32.6], "v": [-63, -60.6, 18, 25.3], "stack": [-61.2],
}, {
    "xload": [-91.3, -89, -66.7, -65.8], "ln1a": [-79, -77.9, -68.2, -66.2], "ln1b": [-69.2, -67.5, -65.9, -65.5],
    "cload": [-105.7], "inproj": [-73.2, -67.3, -57.2, -43.2], "silu": [-46.2, -43.5, -42.7, -42.1], "xproj": [-35.6],
    "bcload": [-15.5, -13, -9.4, -9.4], "rot": [-63.8, -59.1, -53.4, -45.5, -39.4, -32.1, -22, -18.9],
    "hi": [-54.8, -42.9, -28.6, -15.4], "lo": [-53, -40.7, -25.5, -14.6], "dt": [-27.2, -14, -6.7, 10.9],
    "delta": [-26.2, -11, -4.9, 13.5], "du": [-17.9, -13.9, -5.8, 20.3], "v": [-11.7, -5.1, 1.1, 3.1],
}, {
    "xload": [-100.9, -98.4, -83.5, -81.4], "ln1a": [-86.3, -85.4, -82.1, -79.3], "ln1b": [-83.2, -82.6, -80.6, -76.6],
    "cload": [-114.8], "inproj": [-74.2, -67.5, -56, -43.2], "silu": [-43.6, -43.2, -43.2, -42.2], "xproj": [-32.2],
    "bcload": [-23.9, -8.6, -8.3, -7.8], "rot": [-63.8, -58, -52, -46.1, -41, -32, -23.6, -19.1],
    "hi": [-55.4, -43.6, -28.6, -17.1], "lo": [-50.8, -43, -26.6, -14.5], "dt": [-26.3, -16.2, -8.5, 10.5],
    "delta": [-23.6, -12.2, -4.2, 13.1], "du": [-19.4, -5.1, 3.1, 14.6], "v": [-12.2, -5, -0.7, 4.9],
}]
AFTER = {
    "resid": [3.5], "wo": [8.9, 14.1, 17.9, 26], "ln2a": [28.8], "ln2b": [33.6], "gate": [58.9, 58.9, 59.3, 60.4],
    "yt": [67.1, 71.6, 78.5, 83.6], "x2store": [84.6],
}
WEIGHTS = [
    {"fwload": [-0.1], "wsum": [9.4, 13.9, 16.5, 26.5], "wtot": [32.4], "tern": [35.5, 44.7, 48.5, 54.8]},
    {"fwload": [84.9], "wsum": [92.5, 94.5, 96.9, 97.8], "wtot": [98.6], "tern": [100.4, 104, 104.9, 108.1]},
]
TILE = {
    "fxload": [-32.6], "xa": [-19.5], "xb": [-19.3], "xc": [-17.4], "xt": [-1.6], "fc": [2.2, 4.9, 6.3, 8],
    "hstat": [12.3], "hnmr": [13.5], "hn": [12.9, 13.5], "hscale": [15.1], "hq": [15.5, 16.4],
    "ht": [16.2, 16.7, 18.7, 20.6], "proj": [23],
}
FIRST_TILE = {"xa": [-13], "xb": [-9.8], "xc": [-6.8]}


def schedule():
    out = []

    def add(start, times, name=lambda kind, n: (kind, n)):
        for kind, at in times.items():
            out.extend((start + t, (kind, *name(kind, n))) for n, t in enumerate(at))

    for s in range(SLOTS):
        start = TICKS * s
        per_sub = ("exp", "dbu", "scan", "ch", "pair", "y")
        add(start, {k: v for k, v in MIXER[2 if is_last(SUBS * s) else s % 2].items() if s or k != "stack"},
            lambda kind, n: (SUBS * s + n,) if kind in per_sub else (s, n) if kind in ("s", "t") else (s,))
        if s % 2:
            add(start, QUOTIENT, lambda kind, n: (s // 2,))
    for b in range(B):
        start = 8 * TICKS * b
        args = {
            "cload": lambda n: (b,), "xproj": lambda n: (b,), "stack": lambda n: (0,),
            "rot": lambda n: (b, n // 2, n % 2), "v": lambda n: (b, n // 2, n % 2),
            "bcload": lambda n: (b, 0, n), "resid": lambda n: (b,), "ln2a": lambda n: (b,),
            "ln2b": lambda n: (b,), "x2store": lambda n: (b,), "wo": lambda n: (b, n // 2, n % 2),
        }
        add(start, BEFORE[min(b, 2)], lambda kind, n: args.get(kind, lambda n: (b, n))(n))
        add(start + 8 * TICKS, AFTER, lambda kind, n: args.get(kind, lambda n: (b, n))(n))
        out += [(start + 3 * TICKS + 3 * k + 3, ("bcload", b, 1, k)) for k in range(SUBS)]
    for w in range(2):
        add(TICKS * (SLOTS - 7), WEIGHTS[w], lambda kind, n: (w, n) if kind in ("wsum", "tern") else (w,))
    for t in range(B * LT):
        times = {**TILE, **FIRST_TILE} if t == 0 else TILE
        add(TICKS * (SLOTS + 1 + t), {**times, "fxload": [max(times["fxload"][0], -TICKS * (t + 1))]},
            lambda kind, n: (t, n) if kind in ("fc", "ht", "hn", "hq") else (t,))
    return out


LAG = {
    "pe": {"first": -0.05, "ln1b": -0.4, "zt": 0.6, "inproj": 0, "xproj": 0.7, "dt": 0.1, "rot": 0, "v": -1, "wo": 0.2, "zb": 0.7, "yt": 0.7,
           "s": -0.2, "t": 0.2, "mt": 0.3, "xt": 3.1, "fc": 0.7, "ht": -0.9, "wtot": 1.9, "proj": 3.2},
    "act": {"ln1b": 0.4, "inproj": 0.9, "xproj": -0.4, "dt": 0.5, "v": -0.1, "mt": 0.2, "t": 0.5, "zb": 1.1,
            "xt": 1.3, "fc": 2.4, "ht": -1, "zt": -0.5, "gate": 1.3, "hn": -0.6},
    "dve": {"s": 0.5, "ln1b": -0.4, "inproj": 2.1, "rot": 0.8, "wo": 1.1, "gate": 21.6, "yt": 1.4, "zt": 0.9,
            "wtot": 1.1, "xt": 0.7, "fc": 3.6, "ht": 0.7, "hn": 0.6, "proj": 5.9, "ln1a": -0.1, "ln2a": -0.9,
            "xa": -1, "xb": 0.4, "hstat": 0.1},
    "pool": {"ln1a": -0.2, "ln2a": 1, "xa": 0.2, "xb": 1.3, "hstat": -3.4, "ch": 0, "gate": 2, "lo": -0.4, "dbu": 0.1},
    "sp": {"xproj": -8.9, "lo": -0.8, "proj": 2.5},
}


IN_PARTS = ("rot", "v", "wo")


def order(engine):
    lag = LAG[engine]
    placed = [(t + lag.get(item[0], 0), item) for t, item in schedule()]
    if engine == "pe":
        placed += [(t + lag["first"], ("first", item)) for t, item in placed if item[0] in IN_PARTS]
    return [item for _, item in sorted(placed, key=lambda x: x[0])]


ORDER = {engine: order(engine) for engine in LAG}


def check_order():
    for items in ORDER.values():
        at = {item: n for n, item in enumerate(items)}
        for kind in {item[0] for item in items}:
            mine = [item for item in items if item[0] == kind]
            assert kind == "first" or mine == sorted(mine), kind
        if items is ORDER["dve"] or items is ORDER["pool"]:
            for t in range(B * LT):
                assert at["xa", t] < at["xb", t] and (t == 0 or at["xb", t - 1] < at["xa", t])
        if items is ORDER["dve"]:
            for t in range(B * LT):
                assert at["xb", t] < at["xc", t]
                assert at["fc", t, 3] < at["hstat", t] < at["hnmr", t] < at["hn", t, 1] < at["hscale", t] < at["hq", t, 0]
            for w in range(2):
                assert at["wtot", w] < at["tern", w, 0]
            for b in range(B):
                for n in range(4):
                    assert at["rot", b, n, 0] < at["rot", b, n, 1]
        if items is ORDER["pe"]:
            for p in range(SLOTS):
                assert at["s", p, 4] < at["mt", p] < at["t", p, 0] and (p == 0 or at["t", p - 1, 4] < at["s", p, 0])


check_order()


def chunk_uses():
    holds, number, last = [], {}, {}
    for item in ORDER["pe"]:
        kind, *a = item
        if kind not in ("rot", "v", "wo"):
            continue
        key = (kind, a[0], a[1])
        if key not in number:
            number[key] = len(holds)
            holds.append(a[1] + {"rot": 0, "v": 4, "wo": 6}[kind])
        last[number[key]] = item
    return holds, number, last


CHUNK, CHUNK_OF, LAST_USER = chunk_uses()
LOAD_AFTER = {item: c + 2 for c, item in LAST_USER.items() if c + 2 < len(CHUNK)}

EMPTIED_BY = {"ln1b": "act", "inproj": "act", "xproj": "act", "dt": "act", "v": "act", "zb": "act",
              "rot": "dve", "wo": "dve", "yt": "dve", "zt": "dve", "wtot": "dve"}
TASK = {item: n for n, item in enumerate(x for x in ORDER["pe"] if x[0] in EMPTIED_BY)}
FREED = {}
for _who in ("act", "dve"):
    for _n, _item in enumerate(x for x in ORDER[_who] if EMPTIED_BY.get(x[0]) == _who):
        FREED[TASK[_item]] = (_who, _n + 1)
TURNS = [x for x in ORDER["pe"] if x[0] in ("xt", "ht")]
assert all([x for x in ORDER[e] if x[0] in ("xt", "ht")] == TURNS for e in ("act", "dve"))
TURN = {item: n for n, item in enumerate(TURNS)}
SCRATCH = [x[:3] for x in ORDER["pe"] if x[0] == "dt" or (x[0] == "rot" and x[3] == 0)]


def earlier(engine, kind, item):
    items = ORDER[engine]
    return sum(x[0] == kind for x in items[:items.index(item)])


def layer_kernel(nc, t_in, out):
    sems = {}
    with ExitStack() as ctx:
        base = [(nc.sbuf_base + 31) // 32 * 32]

        def sb(name, shape, dt=F32):
            size = 4 if dt in (F32, F32R) else 2
            n = size
            for d in shape[1:]:
                n *= d
            at = base[0]
            base[0] += (n + 31) // 32 * 32
            assert base[0] <= nc.sbuf_usable_end, (name, base[0], nc.sbuf_usable_end)
            return nc.alloc_sbuf_tensor_at(name, shape, dt, offset=at)

        def sem(name):
            sems[name] = ctx.enter_context(nc.semaphore(name))
            return sems[name]

        ident = sb("ident", [P, P])
        ones = sb("ones", [P, P])
        neg_half = sb("neg_half", [P, 4])
        phase_base = base[0]

        ident_b = sb("ident_b", [P, P], BF16)
        mask_qk = sb("mask_qk", [P, P], BF16)
        mask_kq = sb("mask_kq", [P, P], BF16)
        pick = sb("pick", [2, 2, P], F32R)
        xp_w = sb("xp_w", [P, ET, DR + 2 * DS])
        dt_w = sb("dt_w", [DR, DM])
        small = sb("small", [P, ET, TAPS + 3 + DS])
        conv_w = small[:, :, 0:TAPS]
        conv_b = small[:, :, TAPS:TAPS + 1]
        dt_b = small[:, :, TAPS + 1:TAPS + 2]
        d_skip = small[:, :, TAPS + 2:TAPS + 3]
        a_log = small[:, :, TAPS + 3:]
        a_neg = sb("a_neg", [P, ET, DS])
        stats = sb("stats", [P, 2, 6])
        mv = sb("mv", [P, 2, 2])
        rstd = sb("rstd", [P, 2, 1])
        w_ring = sb("w_ring", [P, 2, KD, CH])
        y_acc = sb("y_acc", [P, 2, ET, L])
        x_dbl = sb("x_dbl", [DR + 2 * DS, L])
        m_col = sb("m_col", [P, LT, 2])
        m_row = sb("m_row", [2, L], F32R)
        pick_f = sb("pick_f", [2, 2, P])
        base[0] -= 4 * 2 * P
        o_t = sb("o_t", [P, ET, L])
        z_sb = sb("z_sb", [P, L])
        z_rec = sb("z_rec", [P, LT, 4])
        xr = sb("xr", [P, LT, DM])
        stats2 = sb("stats2", [P, LT, 6])
        mv2 = sb("mv2", [P, LT, 2])
        ve2 = sb("ve2", [P, LT])
        rstd2 = sb("rstd2", [P, LT])
        nmr2 = sb("nmr2", [P, LT])
        gate = z_sb
        w_sum = sb("w_sum", [P, 2, 4])
        gam = sb("gam", [P, 2])
        gam_q = sb("gam_q", [P, 2])
        thr = sb("thr", [P, 2])
        nthr = sb("nthr", [P, 2])
        fx = sb("fx", [P, 4, 16])
        st_x = sb("st_x", [P, 2, 6])
        fh = sb("fh", [P, 4, 16])
        st_h = sb("st_h", [P, 2, 4, 6])

        early = base[0]
        in_w = sb("in_w", [P, KC, DM])
        cos = sb("cos", [P, L])
        sin = sb("sin", [P, L])
        x_in = sb("x_in", [P, 2, DM])
        xn_t = sb("xn_t", [P, KD, L])
        ctx_in = sb("ctx_in", [P, KC, L])
        x_pad = sb("x_pad", [P, 520])
        tmp = sb("tmp", [P, 3, L])
        hl = sb("hl", [P, 4, L], F32R)
        late = base[0]
        base[0] = early
        raw = [sb("raw_fc", [P, 4, FF])]
        base[0] = early
        t_fc = sb("t_fc", [P, KD, FF], F32R)
        low = sb("low", [P, FF], BF16)
        assert base[0] <= late

        base[0] = late
        b_bc = sb("b_bc", [P, 8, L])
        c_bc = sb("c_bc", [P, 8, L])
        q_st = sb("q_st", [P, 2, 2, L], F32R)
        k_st = sb("k_st", [P, 2, 2, L], F32R)
        u = sb("u", [P, ET, L])
        delta = sb("delta", [P, ET, L])
        du = sb("du", [P, ET, L])
        da = sb("da", [P, DA_RING, 2, L])
        hb = sb("hb", [P, HB_RING, 2, L])
        v_sb = sb("v_sb", [P, LT, DM])
        p_t = sb("p_t", [P, 2, P_W])
        base[0] = late
        raw.append(sb("raw_pr", [P, 4, FF]))
        base[0] = late
        t_pr = sb("t_pr", [P, FT, DM], F32R)
        xf = sb("xf", [P, XF, DM])
        xq = sb("xq", [P, 2, DM])
        xq_hi = sb("xq_hi", [P, 2, KD, P], F32R)
        xq_lo = sb("xq_lo", [P, 2, KD, P], F32R)
        h_sb = sb("h_sb", [P, 2, FF])
        hq_hi = sb("hq_hi", [P, FT, P], F32R)
        hq_lo = sb("hq_lo", [P, FT, P], F32R)
        y_out = sb("y_out", [P, 2, DM])

        ps = ctx.enter_context(nc.psum_tensor("ps", [P, 8, 512], F32))
        M = [ps[:, 0, :], ps[:, 1, :]]
        R = [ps[:, 2 + n, :] for n in range(3)]
        O_B, Z_B = ps[:, 5, :], ps[:, 6, :]
        Y_B = ps[:, 7, :]
        UP = [ps[:, 2, :], ps[:, 3, :]]
        TR = [ps[:, 4, :], ps[:, 7, :]]
        DOWN = [ps[:, 5, :], ps[:, 6, :]]

        qk_d = nc.dram_tensor("qk_d", [B, 2, NH, 4, HALF, L], F32, kind="Internal").ap()
        bc_d = nc.dram_tensor("bc_d", [B, 2 * DS, L], F32, kind="Internal").ap()
        x2_d = nc.dram_tensor("x2_d", [B, LT, P, DM], F32, kind="Internal").ap()

        const_in = {group: sem(f"const_in_{group}") for group in ("basic", "inproj", "rotary", "scan")}
        w_in = [sem(f"w_in{i}") for i in range(2)]
        x_in_s = [sem(f"x_in{i}") for i in range(2)]
        ctx_in_s = sem("ctx_in_s")
        stack_in = [sem(f"stack_in{i}") for i in range(2)]
        bc_in = [sem(f"bc_in{i}") for i in range(SUBS)]
        resid_in = sem("resid_in")
        hl_stored = sem("hl_stored")
        bc_stored = sem("bc_stored")
        x2_stored = sem("x2_stored")
        pool_set = sem("pool_set")
        a_exp = sem("a_exp")
        a_ready = sem("a_ready")
        pick_ready = sem("pick_ready")
        m_full = sem("m_full")
        m_free = {"act": sem("m_free_act"), "dve": sem("m_free_dve")}
        ln1_var = sem("ln1_var")
        ln1_rstd = sem("ln1_rstd")
        ln1_done = sem("ln1_done")
        conv_done = sem("conv_done")
        u_ready = sem("u_ready")
        sp_ready = sem("sp_ready")
        delta_ready = sem("delta_ready")
        du_ready = sem("du_ready")
        lo_ready = sem("lo_ready")
        rot_done = sem("rot_done")
        hi_ready = sem("hi_ready")
        da_ready = sem("da_ready")
        dbu_ready = sem("dbu_ready")
        scan_done = sem("scan_done")
        ch_done = {"dve": sem("ch_done_dve"), "pool": sem("ch_done_pool")}
        pair_done = sem("pair_done")
        y_done = sem("y_done")
        yacc_done = sem("yacc_done")
        s_full = sem("s_full")
        max_done = sem("max_done")
        m_row_ready = sem("m_row_ready")
        t_full = sem("t_full")
        p_ready = sem("p_ready")
        pv_done = sem("pv_done")
        z_copied = sem("z_copied")
        norm_done = sem("norm_done")
        ln2_var = sem("ln2_var")
        ln2_rstd = sem("ln2_rstd")
        ln2_ready = sem("ln2_ready")
        gate_ready = sem("gate_ready")
        gated = sem("gated")
        act_own = sem("act_own")
        dve_own = sem("dve_own")
        fw_in = [sem("fw_in0"), sem("fw_in1")]
        wsum_ready = sem("wsum_ready")
        tern_done = sem("tern_done")
        xf_in = [sem(f"xf_in{i}") for i in range(XF)]
        fx_var = sem("fx_var")
        fx_pow = sem("fx_pow")
        xq_done = sem("xq_done")
        tr_full = sem("tr_full")
        tr_hi = sem("tr_hi")
        tr_free = sem("tr_free")
        fc_full = sem("fc_full")
        gelu_done = sem("gelu_done")
        fh_var = sem("fh_var")
        fh_pow = sem("fh_pow")
        fh_nmr = sem("fh_nmr")
        hn_done = sem("hn_done")
        hq_done = sem("hq_done")
        proj_full = sem("proj_full")
        y_ready = sem("y_ready")
        y_stored = [sem("y_stored0"), sem("y_stored1")]

        CONSTS = {
            "basic": [(ident, t_in["ident"]), (small, t_in["small"]), (pick_f, t_in["pick"])],
            "inproj": [(in_w, t_in["in_w"])],
            "rotary": [(cos, t_in["cos"]), (sin, t_in["sin"])],
            "scan": [(xp_w, t_in["xp_w"]), (dt_w, t_in["dt_w"])],
        }

        def consts(eng, *groups):
            for group in groups:
                eng.wait_ge(const_in[group], 16 * len(CONSTS[group]))

        def sub(j):
            return j // 32, j // 16 % 2, j // 4 % 4, j % 4

        def freed(eng, n):
            if n >= 2:
                who, count = FREED[n - 2]
                eng.wait_ge(m_free[who], count)

        def emptied(eng, n):
            who, count = FREED[n]
            eng.wait_ge(m_free[who], count)

        def scratch_free(eng, item):
            n = SCRATCH.index(item)
            if n:
                kind = SCRATCH[n - 1][0]
                eng.wait_ge(lo_ready if kind == "rot" else delta_ready, sum(x[0] == kind for x in SCRATCH[:n]))

        def wait_ch(eng, j):
            mine = "pool" if on_pool(j) else "dve"
            eng.wait_ge(ch_done[mine], sum(on_pool(i) == on_pool(j) for i in range(j + 1)))

        def ring_free(r):
            if r >= 3:
                p, n = divmod(r - 3, 11)
                if n < 5:
                    nc.tensor.wait_ge(max_done, 5 * p + n + 1)
                elif n == 5:
                    nc.tensor.wait_ge(m_row_ready, p + 1)
                else:
                    nc.tensor.wait_ge(p_ready, 5 * p + n - 5)

        def slots_over(eng):
            eng.wait_ge(t_full, 5 * SLOTS)
            eng.wait_ge(pv_done, SLOTS)
            eng.wait_ge(y_done, SUBS * SLOTS)
            eng.wait_ge(yacc_done, SLOTS)

        class Own:

            def __init__(self, eng, s):
                self.eng, self.s, self.n = eng, s, 0

            def done(self, ins):
                ins.then_inc(self.s, 1)
                self.n += 1

            def settle(self):
                self.eng.wait_ge(self.s, self.n)

        S_UNITS = [[(0, 3, 0)], [(0, 2, 0), (0, 0, 384)], [(1, 3, 0)], [(1, 2, 0), (1, 0, 384)],
                   [(0, 1, 0), (1, 1, 256)]]
        T_UNITS = [[(0, 0, 0)], [(0, 1, 0), (0, 3, 384)], [(1, 0, 0)], [(1, 1, 0), (1, 3, 384)],
                   [(0, 2, 0), (1, 2, 256)]]

        block = ctx.enter_context(nc.Block())

        @block.sync
        def _(sp):
            def load_chunk(c):
                sp.dma_start(w_ring[:, c % 2], t_in["w_attn"][CHUNK[c]]).then_inc(w_in[c % 2], 16)

            def load_consts(group):
                for dst, src in CONSTS[group]:
                    sp.dma_start(dst[:], src).then_inc(const_in[group], 16)

            for item in ORDER["sp"]:
                kind, *a = item
                if item in LOAD_AFTER:
                    sp.wait_ge(m_full, TASK[item] + 1)
                    load_chunk(LOAD_AFTER[item])
                if kind == "xload":
                    b, t = a
                    i = LT * b + t
                    if i >= 2:
                        sp.wait_ge(m_full, TASK["ln1b", (i - 2) // LT, (i - 2) % LT] + 1)
                    sp.dma_start(x_in[:, i % 2], t_in["x"][b, t]).then_inc(x_in_s[i % 2], 16)
                    if i == 1:
                        load_consts("basic")
                    if i == 3:
                        load_chunk(0)
                        load_consts("rotary")
                        load_chunk(1)
                        load_consts("scan")
                elif kind == "cload":
                    b, = a
                    if b:
                        sp.wait_ge(m_full, TASK["inproj", b - 1, ET - 1] + 1)
                    sp.dma_start(ctx_in[:], t_in["ctx"][b]).then_inc(ctx_in_s, 16)
                    if b == 0:
                        load_consts("inproj")
                elif kind == "lo":
                    b, n = a
                    sp.wait_ge(lo_ready, 4 * b + n + 1)
                    for part in range(4):
                        heads = qk_d[b, n % 2, 8 * (n // 2):8 * (n // 2) + 8, part]
                        sp.dma_start(heads, hl[:, part, :].bitcast(F32)).then_inc(hl_stored, 16)
                elif kind == "xproj":
                    b, = a
                    emptied(sp, TASK["xproj", b])
                    sp.dma_start(bc_d[b], x_dbl[DR:DR + 2 * DS, :]).then_inc(bc_stored, 16)
                elif kind == "bcload":
                    b, half, k = a
                    sp.wait_ge(bc_stored, 16 * (b + 1))
                    n = 2 * b + half
                    if n:
                        wait_ch(sp, 16 * (n - 1) + 12 + k)
                    for tile, row in ((b_bc, 0), (c_bc, DS)):
                        r = row + 8 * half + 2 * k
                        src = bc_d[b, r:r + 2, :].rearrange("a n -> (a n)").partition_broadcast(P)
                        sp.dma_start(tile[:, 2 * k:2 * k + 2, :].rearrange("p a n -> p (a n)"), src)\
                            .then_inc(bc_in[k], 16)
                elif kind == "stack":
                    p, = a
                    b, sb_ = divmod(p, 8)
                    sp.wait_ge(hl_stored, 64 * (4 * b + 2 * (sb_ // 4) + 2))
                    if p >= 2:
                        sp.wait_ge(t_full, 5 * (p - 1))
                    for h in range(2):
                        head = 2 * sb_ + h
                        q = qk_d[b, 0, head].rearrange("s p n -> (s p) n")
                        k = qk_d[b, 1, head].rearrange("s p n -> (s p) n")
                        for dst, rows, src in ((q_st, (0, 64), q), (q_st, (64, 128), q), (k_st, (0, 64), k),
                                               (k_st, (64, 96), k[32:64]), (k_st, (96, 128), k[0:32])):
                            sp.dma_start(dst[rows[0]:rows[1], p % 2, h, :].bitcast(F32), src).then_inc(stack_in[p % 2], 16)
                elif kind == "resid":
                    b, = a
                    if b:
                        sp.wait_ge(x2_stored, 16 * b)
                    sp.dma_start(xr[:], t_in["x"][b].rearrange("t p n -> p t n")).then_inc(resid_in, 16)
                elif kind == "x2store":
                    b, = a
                    emptied(sp, TASK["yt", b, ET - 1])
                    sp.dma_start(x2_d[b].rearrange("t p n -> p t n"), xr[:]).then_inc(x2_stored, 16)

                elif kind == "fwload":
                    w, = a
                    if w == 0:
                        sp.wait_ge(m_full, TASK["v", B - 1, 1, 1] + 1)
                        sp.wait_ge(lo_ready, 4 * B)
                        sp.wait_ge(delta_ready, ET * B)
                        sp.wait_ge(hl_stored, 64 * 4 * B)
                        sp.wait_ge(conv_done, 3 * ET * B)
                    else:
                        sp.wait_ge(dbu_ready, SUBS * SLOTS)
                        for k in range(2):
                            wait_ch(sp, SUBS * SLOTS - 1 - k)
                    for c in range(4):
                        sp.dma_start(raw[w][:, c, :], t_in[("w_fc", "w_pr")[w]][:, FF * c:FF * c + FF]).then_inc(fw_in[w], 16)
                elif kind == "fxload":
                    t, = a
                    sp.wait_ge(x2_stored, 16 * (t // LT + 1))
                    if t >= XF:
                        sp.wait_ge(y_ready, t - XF + 1)
                    else:
                        sp.wait_ge(t_full, 5 * SLOTS)
                    sp.dma_start(xf[:, t % XF, :], x2_d[t // LT, t % LT]).then_inc(xf_in[t % XF], 16)
                elif kind == "proj":
                    t, = a
                    sp.wait_ge(y_ready, t + 1)
                    sp.dma_start(out[t // LT, t % LT], y_out[:, t % 2, :]).then_inc(y_stored[t % 2], 16)

            for n in range(2):
                sp.wait_ge(y_stored[n], 16 * B * LT // 2)

        @block.gpsimd
        def _(pool):
            for ap, value in ((ones[:], 1.0), (neg_half[:], -0.5), (x_pad[:, 0:TAPS - 1], 0.0),
                              (da[:, :, :, 0:1], 0.0)):
                nc.gpsimd.memset(ap, value).then_inc(pool_set, 1)
            for ap in (ident_b, mask_qk, mask_kq):
                nc.gpsimd.memset(ap[:], 0.0).then_inc(pool_set, 1)
            pool.wait_ge(pool_set, 7)
            for ap, keep, fill, step in ((ident_b, ALU.not_equal, 1.0, -1), (mask_qk, ALU.is_ge, MASKED, -1),
                                         (mask_kq, ALU.is_ge, MASKED, 1)):
                nc.gpsimd.affine_select(out=ap[:], in_=ap[:], compare_op=keep, fill=fill, base=0,
                                        pattern=[[step, P]], channel_multiplier=-step).then_inc(pool_set, 1)

            for kind, *a in ORDER["pool"]:
                if kind == "dbu":
                    j, = a
                    b, half, et, k = sub(j)
                    pool.wait_ge(du_ready, ET * b + et + 1)
                    pool.wait_ge(bc_in[k], 32 * (2 * b + half + 1))
                    if j >= HB_RING:
                        pool.wait_ge(y_done, j - HB_RING + 1)
                    nc.gpsimd.tensor_tensor(hb[:, j % HB_RING], du[:, et, :].unsqueeze(1).to_broadcast([P, 2, L]),
                                            b_bc[:, 2 * k:2 * k + 2, :], ALU.mult).then_inc(dbu_ready, 1)
                elif kind == "ch" and on_pool(a[0]):
                    j, = a
                    k = j % SUBS
                    pool.wait_ge(scan_done, j + 1)
                    nc.gpsimd.tensor_tensor(hb[:, j % HB_RING], hb[:, j % HB_RING], c_bc[:, 2 * k:2 * k + 2, :], ALU.mult)\
                        .then_inc(ch_done["pool"], 1)
                elif kind == "du":
                    b, et = a
                    i = ET * b + et
                    pool.wait_ge(delta_ready, i + 1)
                    pool.wait_ge(u_ready, i + 1)
                    if b:
                        pool.wait_ge(dbu_ready, 32 * (b - 1) + 16 + 4 * et + 4)
                    nc.gpsimd.tensor_tensor(du[:, et, :], delta[:, et, :], u[:, et, :], ALU.mult).then_inc(du_ready, 1)
                elif kind == "lo":
                    b, n = a
                    pool.wait_ge(hi_ready, 4 * b + n + 1)
                    nc.gpsimd.tensor_tensor(hl[:, 2:4, :], tmp[:, 0:2, :], hl[:, 0:2, :].bitcast(F32), ALU.subtract)\
                        .then_inc(lo_ready, 1)
                elif kind == "gate":
                    b, et = a
                    pool.wait_ge(gate_ready, ET * b + et + 1)
                    pool.wait_ge(yacc_done, 8 * b + 4 + et + 1)
                    y = y_acc[:, b % 2, et, :]
                    nc.gpsimd.tensor_tensor(y, y, gate[:], ALU.mult).then_inc(gated, 1)
                elif kind == "ln1a":
                    b, t = a
                    i = LT * b + t
                    pool.wait_ge(ln1_var, i + 1)
                    nc.gpsimd.tensor_tensor(rstd[:, i % 2], mv[:, i % 2, 1:2], neg_half[:, 0:1], ALU.pow)\
                        .then_inc(ln1_rstd, 1)
                elif kind == "ln2a":
                    b, = a
                    pool.wait_ge(ln2_var, b + 1)
                    nc.gpsimd.tensor_tensor(rstd2[:], ve2[:], neg_half[:], ALU.pow).then_inc(ln2_rstd, 1)

                elif kind in ("xa", "xb"):
                    t, = a
                    n = (kind == "xb")
                    pool.wait_ge(fx_var, 2 * t + n + 1)
                    nc.gpsimd.tensor_tensor(fx[:, t % 4, 2 + n:3 + n], fx[:, t % 4, 4 + n:5 + n],
                                            neg_half[:, 0:1], ALU.pow).then_inc(fx_pow, 1)
                elif kind == "hstat":
                    t, = a
                    pool.wait_ge(fh_var, t + 1)
                    nc.gpsimd.tensor_tensor(fh[:, t % 4, 2:3], fh[:, t % 4, 4:5], neg_half[:, 0:1], ALU.pow)\
                        .then_inc(fh_pow, 1)

        @block.scalar
        def _(act):
            own = Own(act, act_own)
            consts(act, "basic")
            nc.scalar.activation(a_neg[:], a_log, ACT.Exp).then_inc(a_exp, 1)
            nc.scalar.activation(pick[:], pick_f[:], ACT.Copy).then_inc(pick_ready, 1)
            act.wait_ge(pool_set, 10)

            for kind, *a in ORDER["act"]:
                if kind == "exp":
                    j, = a
                    b, half, et, k = sub(j)
                    act.wait_ge(a_ready, 1)
                    act.wait_ge(delta_ready, ET * b + et + 1)
                    if j >= DA_RING:
                        act.wait_ge(scan_done, j - DA_RING + 1)
                    for m in range(2):
                        n = 8 * half + 2 * k + m
                        ins = nc.scalar.activation(da[:, j % DA_RING, m, 1:L], delta[:, et, 1:L], ACT.Exp,
                                                   scale=a_neg[:, et, n:n + 1])
                    ins.then_inc(da_ready, 1)
                elif kind == "ln1b":
                    b, t = a
                    n = TASK[kind, b, t]
                    act.wait_ge(m_full, n + 1)
                    if b and t == 0:
                        act.wait_ge(m_full, TASK["v", b - 1, 1, 1] + 1)
                    nc.scalar.activation(xn_t[:, :, P * t:P * t + P], M[n % 2].rearrange("p (d k) -> p d k", d=KD),
                                         ACT.Copy).then_inc(m_free["act"], 1)
                elif kind == "inproj":
                    b, et = a
                    n = TASK[kind, b, et]
                    i = ET * b + et
                    act.wait_ge(m_full, n + 1)
                    if i:
                        act.wait_ge(conv_done, 3 * i)
                    if b:
                        act.wait_ge(yacc_done, 8 * (b - 1) + et + 1)
                        act.wait_ge(du_ready, ET * (b - 1) + et + 1)
                    nc.scalar.activation(u[:, et, :], M[n % 2], ACT.Identity, bias=conv_b[:, et, :],
                                         scale=conv_w[:, et, TAPS - 1:TAPS])
                    nc.scalar.activation(x_pad[:, TAPS - 1:TAPS - 1 + L], M[n % 2], ACT.Copy)\
                        .then_inc(m_free["act"], 1)
                elif kind == "silu":
                    b, et = a
                    act.wait_ge(conv_done, 3 * (ET * b + et + 1))
                    nc.scalar.activation(u[:, et, :], u[:, et, :], ACT.Silu).then_inc(u_ready, 1)
                elif kind == "xproj":
                    b, = a
                    n = TASK[kind, b]
                    act.wait_ge(m_full, n + 1)
                    if b:
                        act.wait_ge(bc_stored, 16 * b)
                        act.wait_ge(m_full, TASK["dt", b - 1, ET - 1] + 1)
                    nc.scalar.activation(x_dbl[:], M[n % 2][0:DR + 2 * DS, :], ACT.Copy).then_inc(m_free["act"], 1)
                elif kind == "dt":
                    b, et = a
                    n = TASK[kind, b, et]
                    act.wait_ge(m_full, n + 1)
                    scratch_free(act, ("dt", b, et))
                    nc.scalar.activation(tmp[:, 0, :], M[n % 2], ACT.Identity, bias=dt_b[:, et, :])\
                        .then_inc(m_free["act"], 1)
                    act.wait_ge(m_free["act"], FREED[n][1])
                    own.done(nc.scalar.activation(tmp[:, 1, :], tmp[:, 0, :], ACT.Abs))
                    own.settle()
                    own.done(nc.scalar.activation(tmp[:, 1, :], tmp[:, 1, :], ACT.Exp, scale=-1.0))
                    own.settle()
                    nc.scalar.activation(tmp[:, 2, :], tmp[:, 1, :], ACT.Ln, bias=1.0).then_inc(sp_ready, 1)
                elif kind == "hi":
                    b, n = a
                    i = 4 * b + n
                    act.wait_ge(rot_done, i + 1)
                    if i:
                        act.wait_ge(hl_stored, 64 * i)
                    nc.scalar.activation(hl[:, 0:2, :], tmp[:, 0:2, :], ACT.Copy).then_inc(hi_ready, 1)
                elif kind == "v":
                    b, c, tt = a
                    n = TASK[kind, b, c, tt]
                    act.wait_ge(m_full, n + 1)
                    if b:
                        act.wait_ge(pv_done, 8 * (b - 1) + 4 * (c + 1))
                    nc.scalar.activation(v_sb[:, 2 * tt:2 * tt + 2, CH * c:CH * c + CH],
                                         M[n % 2].rearrange("p (t n) -> p t n", t=2), ACT.Copy)\
                        .then_inc(m_free["act"], 1)
                elif kind == "mt":
                    p, = a
                    act.wait_ge(s_full, 6 * p + 6)
                    if p:
                        act.wait_ge(t_full, 5 * p)
                    nc.scalar.activation(m_row[:], R[(11 * p + 5) % 3][0:2, :], ACT.Copy).then_inc(m_row_ready, 1)
                elif kind == "t":
                    p, n = a
                    bank = R[(11 * p + 6 + n) % 3]
                    act.wait_ge(t_full, 5 * p + n + 1)
                    if p:
                        act.wait_ge(pv_done, p)
                    if n < 4:
                        dst = p_t[:, n // 2, 512 * (n % 2):512 * (n % 2) + 512]
                        src = bank
                    else:
                        dst = p_t[:, :, P_AT[2]:P_AT[2] + 256]
                        src = bank.rearrange("p (h n) -> p h n", h=2)
                    nc.scalar.activation(dst, src, ACT.Exp, scale=SCALE).then_inc(p_ready, 1)
                elif kind == "zt":
                    g, = a
                    act.wait_ge(pv_done, 2 * g + 2)
                    if g:
                        act.wait_ge(m_full, TASK[kind, g - 1] + 1)
                    if earlier("act", "gate", (kind, g)):
                        act.wait_ge(gated, earlier("act", "gate", (kind, g)))
                    nc.scalar.activation(z_sb[:], Z_B, ACT.Copy).then_inc(z_copied, 1)
                elif kind == "zb":
                    g, = a
                    n = TASK[kind, g]
                    act.wait_ge(m_full, n + 1)
                    if g % 4 == 0 and g:
                        act.wait_ge(m_full, TASK["wo", g // 4 - 1, 1, 1] + 1)
                    nc.scalar.activation(o_t[:, g % 4, :], M[n % 2], ACT.Copy).then_inc(m_free["act"], 1)
                elif kind == "gate":
                    b, et = a
                    act.wait_ge(ln2_ready, b + 1)
                    if b or et:
                        act.wait_ge(gated, ET * b + et)
                    act.wait_ge(m_full, TASK["zt", earlier("act", "zt", (kind, b, et)) - 1] + 1)
                    nc.scalar.activation(gate[:], xr[:, et, :], ACT.Silu, bias=nmr2[:, et:et + 1],
                                         scale=rstd2[:, et:et + 1]).then_inc(gate_ready, 1)

                elif kind in ("xt", "ht"):
                    t = a[0]
                    tr = TURN[(kind, *a)]
                    if kind == "xt":
                        dst = xq_hi[:, t % 2]
                        if t >= 2:
                            act.wait_ge(fc_full, 4 * (t - 1))
                        else:
                            slots_over(act)
                    else:
                        dst = hq_hi[:, 4 * a[1]:4 * a[1] + 4]
                        if t:
                            act.wait_ge(proj_full, t)
                    act.wait_ge(tr_full, tr + 1)
                    nc.scalar.activation(dst, TR[tr % 2].rearrange("p (k n) -> p k n", n=P), ACT.Copy)\
                        .then_inc(tr_hi, 1)
                elif kind == "fc":
                    t, n = a
                    act.wait_ge(fc_full, 4 * t + n + 1)
                    if t >= 2:
                        act.wait_ge(tr_full, TURN["ht", t - 2, 3] + 1)
                    nc.scalar.activation(h_sb[:, t % 2, 512 * n:512 * n + 512], UP[n % 2], ACT.Gelu,
                                         scale=fx[:, t % 4, 12:13]).then_inc(gelu_done, 1)
                elif kind == "wsum":
                    w, c = a
                    act.wait_ge(fw_in[w], 64)
                    if w or c:
                        act.wait_ge(wsum_ready, 4 * w + c)
                    if w:
                        act.wait_ge(tern_done, 8)
                    nc.scalar.activation(low[:], raw[w][:, c, :], ACT.Abs, accum_out=w_sum[:, w, c:c + 1])\
                        .then_inc(wsum_ready, 1)
                elif kind == "hn":
                    t, h = a
                    act.wait_ge(fh_nmr, t + 1)
                    half = h_sb[:, t % 2, FF // 2 * h:FF // 2 * (h + 1)]
                    nc.scalar.activation(half, half, ACT.Identity, bias=fh[:, t % 4, 3:4],
                                         scale=fh[:, t % 4, 2:3]).then_inc(hn_done, 1)

        @block.tensor
        def _(pe):
            consts(pe, "basic")
            pe.wait_ge(pool_set, 10)

            def chunk_in(c):
                pe.wait_ge(w_in[c % 2], 16 * (c // 2 + 1))

            for kind, *a in ORDER["pe"]:
                first = kind == "first"
                if first:
                    kind, *a = a[0]
                if kind == "ln1b":
                    b, t = a
                    n, i = TASK[kind, b, t], LT * b + t
                    pe.wait_ge(ln1_done, i + 1)
                    freed(pe, n)
                    for d in range(KD):
                        mm = nc.tensor.transpose(M[n % 2][:, P * d:P * d + P], x_in[:, i % 2, P * d:P * d + P],
                                                 ident[:])
                    mm.then_inc(m_full, 1)
                elif kind == "inproj":
                    b, et = a
                    n = TASK[kind, b, et]
                    pe.wait_ge(ctx_in_s, 16 * (b + 1))
                    consts(pe, "inproj")
                    freed(pe, n)
                    for d in range(KC):
                        mm = nc.tensor.matmul(M[n % 2], in_w[:, d, P * et:P * et + P], ctx_in[:, d, :],
                                              start=(d == 0), stop=(d == KC - 1))
                    mm.then_inc(m_full, 1)
                elif kind == "xproj":
                    b, = a
                    n = TASK[kind, b]
                    pe.wait_ge(u_ready, ET * (b + 1))
                    consts(pe, "scan")
                    freed(pe, n)
                    for et in range(ET):
                        mm = nc.tensor.matmul(M[n % 2][0:DR + 2 * DS, :], xp_w[:, et, :], u[:, et, :],
                                              start=(et == 0), stop=(et == ET - 1))
                    mm.then_inc(m_full, 1)
                elif kind == "dt":
                    b, et = a
                    n = TASK[kind, b, et]
                    emptied(pe, TASK["xproj", b])
                    freed(pe, n)
                    nc.tensor.matmul(M[n % 2], dt_w[:, P * et:P * et + P], x_dbl[0:DR, :], start=True, stop=True)\
                        .then_inc(m_full, 1)
                elif kind == "rot":
                    b, n, half = a
                    c = CHUNK_OF[kind, b, n]
                    task = TASK[(kind, *a)]
                    chunk_in(c)
                    emptied(pe, TASK["ln1b", b, LT - 1])
                    freed(pe, task)
                    for d in (range(KD // 2) if first else range(KD // 2, KD)):
                        mm = nc.tensor.matmul(M[task % 2], w_ring[:, c % 2, d, P * half:P * half + P],
                                              xn_t[:, d, :], start=(d == 0), stop=(d == KD - 1))
                    if not first:
                        mm.then_inc(m_full, 1)
                elif kind == "v":
                    b, c, tt = a
                    wc = CHUNK_OF[kind, b, c]
                    n = TASK[kind, b, c, tt]
                    chunk_in(wc)
                    emptied(pe, TASK["ln1b", b, LT - 1])
                    freed(pe, n)
                    m = 0 if first else 1
                    t = 2 * tt + m
                    for d in range(KD):
                        mm = nc.tensor.matmul(M[n % 2][:, CH * m:CH * m + CH], xn_t[:, d, P * t:P * t + P],
                                              w_ring[:, wc % 2, d, :], start=(d == 0), stop=(d == KD - 1))
                    if not first:
                        mm.then_inc(m_full, 1)
                elif kind == "s":
                    p, n = a
                    pe.wait_ge(stack_in[p % 2], 160 * (p // 2 + 1))
                    ring_free(11 * p + n)
                    bank = R[(11 * p + n) % 3]
                    for h, i, col in S_UNITS[n]:
                        w = P * (i + 1)
                        nc.tensor.matmul(bank[:, col:col + w], q_st[:, p % 2, h, P * i:P * i + P],
                                         k_st[:, p % 2, h, 0:w], start=True, stop=False)
                        mm = nc.tensor.matmul(bank[:, col + w - P:col + w], ident_b[:], mask_qk[:],
                                              start=False, stop=True)
                    mm.then_inc(s_full, 1)
                elif kind == "mt":
                    p, = a
                    pe.wait_ge(max_done, 5 * p + 5)
                    ring_free(11 * p + 5)
                    for i in range(LT):
                        mm = nc.tensor.transpose(R[(11 * p + 5) % 3][0:2, P * i:P * i + P], m_col[:, i, :], ident[:])
                    mm.then_inc(s_full, 1)
                elif kind == "t":
                    p, n = a
                    pe.wait_ge(m_row_ready, p + 1)
                    pe.wait_ge(pick_ready, 1)
                    ring_free(11 * p + 6 + n)
                    bank = R[(11 * p + 6 + n) % 3]
                    for h, jt, col in T_UNITS[n]:
                        w = L - P * jt
                        nc.tensor.matmul(bank[:, col:col + w], k_st[:, p % 2, h, P * jt:P * jt + P],
                                         q_st[:, p % 2, h, P * jt:L], start=True, stop=False)
                        nc.tensor.matmul(bank[:, col:col + P], ident_b[:], mask_kq[:], start=False, stop=False)
                        mm = nc.tensor.matmul(bank[:, col:col + w], pick[:, h, :], m_row[:, P * jt:L],
                                              start=False, stop=True)
                    mm.then_inc(t_full, 1)
                elif kind == "pv":
                    p, = a
                    b, sb_ = divmod(p, 8)
                    pe.wait_ge(p_ready, 5 * (p + 1))
                    emptied(pe, TASK["v", b, sb_ // 4, 1])
                    if p % 2 == 0 and p:
                        pe.wait_ge(norm_done, p // 2)
                    for jt in range(LT):
                        for h in range(2):
                            head = 2 * sb_ + h
                            rhs = p_t[:, h, P_AT[jt]:P_AT[jt] + L - P * jt]
                            for lhs, bank, quad in ((v_sb[:, jt, HD * head:HD * head + HD], O_B, 2 * (p % 2) + h),
                                                    (ones[:, 0:HD], Z_B, (2 * (p % 2) + h + 2) % 4)):
                                mm = nc.tensor.matmul(bank[HD * quad:HD * quad + HD, P * jt:L], lhs, rhs,
                                                      start=(jt == 0), stop=(jt == LT - 1))
                    mm.then_inc(pv_done, 1)
                elif kind == "y":
                    j, = a
                    paired = is_paired(j)
                    if paired:
                        pe.wait_ge(pair_done, sum(is_paired(i) for i in range(j + 1)))
                    else:
                        wait_ch(pe, j)
                    if j % 4 == 0 and j:
                        pe.wait_ge(yacc_done, j // 4)
                    for m in range(1 if paired else 2):
                        mm = nc.tensor.matmul(Y_B, ident[:], hb[:, j % HB_RING, m, :], start=(j % 4 == 0 and m == 0),
                                              stop=(j % 4 == 3 and (paired or m == 1)))
                    mm.then_inc(y_done, 1)
                elif kind == "wo":
                    b, c, tt = a
                    wc, n = CHUNK_OF[kind, b, c], TASK[(kind, *a)]
                    chunk_in(wc)
                    pe.wait_ge(norm_done, 4 * b + 4)
                    freed(pe, n)
                    m = 0 if first else 1
                    t = 2 * tt + m
                    for g in range(KD):
                        mm = nc.tensor.matmul(M[n % 2][:, CH * m:CH * m + CH], o_t[:, g, P * t:P * t + P],
                                              w_ring[:, wc % 2, g, :], start=(g == 0), stop=(g == KD - 1))
                    if not first:
                        mm.then_inc(m_full, 1)
                elif kind == "zt":
                    g, = a
                    n = TASK[kind, g]
                    pe.wait_ge(z_copied, g + 1)
                    freed(pe, n)
                    for i in range(LT):
                        mm = nc.tensor.transpose(M[n % 2][:, P * i:P * i + P], z_sb[:, P * i:P * i + P], ident[:])
                    mm.then_inc(m_full, 1)
                elif kind == "zb":
                    g, = a
                    n = TASK[kind, g]
                    emptied(pe, TASK["zt", g])
                    freed(pe, n)
                    for i in range(LT):
                        for q in range(4):
                            mm = nc.tensor.matmul(M[n % 2][HD * q:HD * q + HD, P * i:P * i + P],
                                                  z_rec[:, i, q:q + 1].to_broadcast([P, HD]), ident[:],
                                                  start=True, stop=True)
                    mm.then_inc(m_full, 1)
                elif kind == "yt":
                    b, et = a
                    n = TASK[kind, b, et]
                    pe.wait_ge(gated, ET * b + et + 1)
                    freed(pe, n)
                    for lt in range(LT):
                        mm = nc.tensor.transpose(M[n % 2][:, P * lt:P * lt + P],
                                                 y_acc[:, b % 2, et, P * lt:P * lt + P], ident[:])
                    mm.then_inc(m_full, 1)

                elif kind == "wtot":
                    w, = a
                    n = TASK[kind, w]
                    pe.wait_ge(wsum_ready, 4 * (w + 1))
                    freed(pe, n)
                    nc.tensor.matmul(M[n % 2][:, 0:4], ones[:], w_sum[:, w, :], start=True, stop=True)\
                        .then_inc(m_full, 1)
                elif kind in ("xt", "ht"):
                    t = a[0]
                    tr = TURN[(kind, *a)]
                    if kind == "xt":
                        pe.wait_ge(xq_done, t + 1)
                        src = xq[:, t % 2, :]
                    else:
                        pe.wait_ge(hq_done, 2 * t + a[1] // 2 + 1)
                        src = h_sb[:, t % 2, 512 * a[1]:512 * a[1] + 512]
                    if tr >= 2:
                        pe.wait_ge(tr_free, tr - 1)
                    else:
                        pe.wait_ge(p_ready, 5 * SLOTS)
                        pe.wait_ge(yacc_done, SLOTS)
                    for d in range(4):
                        mm = nc.tensor.transpose(TR[tr % 2][:, P * d:P * d + P], src[:, P * d:P * d + P], ident[:])
                    mm.then_inc(tr_full, 1)
                elif kind == "fc":
                    t, n = a
                    pe.wait_ge(tr_free, TURN["xt", t] + 1)
                    pe.wait_ge(tern_done, 8)
                    if t or n >= 2:
                        pe.wait_ge(gelu_done, 4 * t + n - 1)
                    for d in range(KD):
                        for m, part in enumerate((xq_hi, xq_lo)):
                            mm = nc.tensor.matmul(UP[n % 2], part[:, t % 2, d, :], t_fc[:, d, 512 * n:512 * n + 512],
                                                  start=(d == 0 and m == 0), stop=(d == KD - 1 and m == 1))
                    mm.then_inc(fc_full, 1)
                elif kind == "proj":
                    t, = a
                    if t >= 2:
                        pe.wait_ge(y_ready, t - 1)
                    else:
                        pe.wait_ge(norm_done, SLOTS // 2)
                    pe.wait_ge(tern_done, 16)
                    pe.wait_ge(tr_free, TURN["ht", t, 3] + 1)
                    for k in range(FT):
                        for m, part in enumerate((hq_hi, hq_lo)):
                            mm = nc.tensor.matmul(DOWN[t % 2], part[:, k, :], t_pr[:, k, :],
                                                  start=(k == 0 and m == 0), stop=(k == FT - 1 and m == 1))
                    mm.then_inc(proj_full, 1)

        @block.vector
        def _(dve):
            own = Own(dve, dve_own)
            v = nc.vector
            dve.wait_ge(pool_set, 10)

            def scales(f, w):
                own.done(v.reciprocal(f[:, 9:10], f[:, 8:9]))
                own.done(v.tensor_scalar(f[:, 12:13], f[:, 8:9], gam_q[:, w:w + 1], None, ALU.mult))
                own.settle()
                own.done(v.tensor_scalar(f[:, 10:11], f[:, 9:10], Q_B, None, ALU.mult))
                own.settle()

            for kind, *a in ORDER["dve"]:
                if kind == "scan":
                    j, = a
                    dve.wait_ge(da_ready, j + 1)
                    dve.wait_ge(dbu_ready, j + 1)
                    h = hb[:, j % HB_RING].rearrange("p a n -> p (a n)")
                    v.tensor_tensor_scan(h, da[:, j % DA_RING].rearrange("p a n -> p (a n)"), h, 0.0, ALU.mult, ALU.add)\
                        .then_inc(scan_done, 1)
                elif kind == "ch":
                    j, = a
                    k = j % 4
                    if on_pool(j):
                        continue
                    dve.wait_ge(scan_done, j + 1)
                    v.tensor_tensor(hb[:, j % HB_RING], hb[:, j % HB_RING], c_bc[:, 2 * k:2 * k + 2, :], ALU.mult)\
                        .then_inc(ch_done["dve"], 1)
                elif kind == "pair":
                    j, = a
                    if not is_paired(j):
                        continue
                    wait_ch(dve, j)
                    v.tensor_tensor(hb[:, j % HB_RING, 0, :], hb[:, j % HB_RING, 0, :], hb[:, j % HB_RING, 1, :], ALU.add)\
                        .then_inc(pair_done, 1)
                elif kind == "yacc":
                    n, = a
                    b, half, et = n // 8, n // 4 % 2, n % 4
                    dve.wait_ge(y_done, 4 * n + 4)
                    y = y_acc[:, b % 2, et, :]
                    if half == 0:
                        if b >= 2:
                            dve.wait_ge(m_full, TASK["yt", b - 2, et] + 1)
                        ins = v.scalar_tensor_tensor(out=y, in0=u[:, et, :], scalar=d_skip[:, et, :], in1=Y_B,
                                                     op0=ALU.mult, op1=ALU.add)
                    else:
                        dve.wait_ge(yacc_done, n - 3)
                        ins = v.tensor_tensor(y, y, Y_B, ALU.add)
                    ins.then_inc(yacc_done, 1)
                elif kind == "ln1a":
                    b, t = a
                    i = LT * b + t
                    dve.wait_ge(x_in_s[i % 2], 16 * (i // 2 + 1))
                    own.settle()
                    own.done(v.bn_stats(stats[:, i % 2], x_in[:, i % 2, :]))
                    own.settle()
                    own.done(v.bn_aggr(mv[:, i % 2], stats[:, i % 2]))
                    own.settle()
                    v.tensor_scalar(mv[:, i % 2, 1:2], mv[:, i % 2, 1:2], EPS, None, ALU.add).then_inc(ln1_var, 1)
                elif kind == "ln1b":
                    b, t = a
                    i = LT * b + t
                    dve.wait_ge(ln1_rstd, i + 1)
                    v.tensor_scalar(x_in[:, i % 2, :], x_in[:, i % 2, :], mv[:, i % 2, 0:1], rstd[:, i % 2],
                                    ALU.subtract, ALU.mult).then_inc(ln1_done, 1)
                elif kind == "inproj":
                    b, et = a
                    if b == 0 and et == 0:
                        consts(dve, "basic")
                        dve.wait_ge(a_exp, 1)
                        v.tensor_scalar(a_neg[:], a_neg[:], -1.0, None, ALU.mult).then_inc(a_ready, 1)
                    i = ET * b + et
                    emptied(dve, TASK[kind, b, et])
                    for tap in range(TAPS - 1):
                        if tap:
                            dve.wait_ge(conv_done, 3 * i + tap)
                        v.scalar_tensor_tensor(out=u[:, et, :], in0=x_pad[:, tap:tap + L],
                                               scalar=conv_w[:, et, tap:tap + 1], in1=u[:, et, :],
                                               op0=ALU.mult, op1=ALU.add).then_inc(conv_done, 1)
                elif kind == "delta":
                    b, et = a
                    i = ET * b + et
                    dve.wait_ge(sp_ready, i + 1)
                    if b:
                        dve.wait_ge(da_ready, 32 * (b - 1) + 16 + 4 * et + 4)
                        dve.wait_ge(du_ready, ET * (b - 1) + et + 1)
                    d = delta[:, et, :]
                    own.done(v.tensor_scalar(d, tmp[:, 1, :], 1.0, 1.0, ALU.add, ALU.subtract))
                    own.settle()
                    own.done(v.tensor_tensor(d, tmp[:, 1, :], d, ALU.subtract))
                    own.settle()
                    own.done(v.tensor_tensor(d, d, tmp[:, 2, :], ALU.add))
                    own.settle()
                    v.scalar_tensor_tensor(out=d, in0=tmp[:, 0, :], scalar=0.0, in1=d, op0=ALU.max, op1=ALU.add)\
                        .then_inc(delta_ready, 1)
                elif kind == "rot" and a[2] == 0:
                    b, n, _ = a
                    task = TASK[(kind, *a)]
                    bank = M[task % 2]
                    consts(dve, "rotary")
                    scratch_free(dve, (kind, b, n))
                    dve.wait_ge(m_full, task + 1)
                    own.done(v.tensor_tensor(tmp[:, 0, :], bank, cos[:], ALU.mult))
                    v.tensor_tensor(tmp[:, 2, :], bank, sin[:], ALU.mult).then_inc(m_free["dve"], 1)
                elif kind == "rot":
                    b, n, _ = a
                    task = TASK[(kind, *a)]
                    bank = M[task % 2]
                    dve.wait_ge(m_full, task + 1)
                    own.done(v.tensor_tensor(tmp[:, 1, :], bank, sin[:], ALU.mult))
                    own.settle()
                    own.done(v.tensor_tensor(tmp[:, 0, :], tmp[:, 0, :], tmp[:, 1, :], ALU.subtract))
                    own.settle()
                    v.tensor_tensor(tmp[:, 1, :], bank, cos[:], ALU.mult).then_inc(m_free["dve"], 1)
                    dve.wait_ge(m_free["dve"], FREED[task][1])
                    v.tensor_tensor(tmp[:, 1, :], tmp[:, 1, :], tmp[:, 2, :], ALU.add).then_inc(rot_done, 1)
                elif kind == "s":
                    p, n = a
                    bank = R[(11 * p + n) % 3]
                    dve.wait_ge(s_full, 6 * p + n + 1)
                    if n == 4:
                        v.tensor_reduce(m_col[:, 1, :], bank.rearrange("p (h n) -> p h n", h=2), AX.X, ALU.max,
                                        negate=True).then_inc(max_done, 1)
                    else:
                        for h, i, col in S_UNITS[n]:
                            ins = v.tensor_reduce(m_col[:, i, h:h + 1], bank[:, col:col + P * (i + 1)], AX.X, ALU.max,
                                                  negate=True)
                        ins.then_inc(max_done, 1)
                elif kind == "zt":
                    g, = a
                    n = TASK[kind, g]
                    dve.wait_ge(m_full, n + 1)
                    if g:
                        dve.wait_ge(m_full, TASK["zb", g - 1] + 1)
                    sums = M[n % 2].rearrange("p (t h c) -> p t h c", t=LT, h=4)
                    own.done(v.reciprocal(z_rec[:, :, 0:2], sums[:, :, 2:4, 0]))
                    own.settle()
                    v.reciprocal(z_rec[:, :, 2:4], sums[:, :, 0:2, 0]).then_inc(m_free["dve"], 1)
                elif kind == "norm":
                    n, = a
                    b, g = divmod(n, 4)
                    emptied(dve, TASK["zb", n])
                    v.tensor_tensor(o_t[:, g, :], O_B, o_t[:, g, :], ALU.mult).then_inc(norm_done, 1)
                elif kind == "wo":
                    b, c, tt = a
                    n = TASK[(kind, *a)]
                    dve.wait_ge(resid_in, 16 * (b + 1))
                    dve.wait_ge(m_full, n + 1)
                    dst = xr[:, 2 * tt:2 * tt + 2, CH * c:CH * c + CH]
                    v.tensor_tensor(dst, M[n % 2].rearrange("p (t n) -> p t n", t=2), dst, ALU.add)\
                        .then_inc(m_free["dve"], 1)
                elif kind == "ln2a":
                    b, = a
                    emptied(dve, TASK["wo", b, 1, 1])
                    for t in range(LT):
                        own.done(v.bn_stats(stats2[:, t], xr[:, t, :]))
                    own.settle()
                    for t in range(LT):
                        own.done(v.bn_aggr(mv2[:, t], stats2[:, t]))
                    own.settle()
                    v.tensor_scalar(ve2[:], mv2[:, :, 1], EPS, None, ALU.add).then_inc(ln2_var, 1)
                elif kind == "ln2b":
                    b, = a
                    dve.wait_ge(ln2_rstd, b + 1)
                    v.scalar_tensor_tensor(out=nmr2[:], in0=mv2[:, :, 0], scalar=-1.0, in1=rstd2[:],
                                           op0=ALU.mult, op1=ALU.mult).then_inc(ln2_ready, 1)
                elif kind == "yt":
                    b, et = a
                    n = TASK[kind, b, et]
                    dve.wait_ge(m_full, n + 1)
                    dst = xr[:, :, P * et:P * et + P]
                    v.tensor_tensor(dst, M[n % 2].rearrange("p (t n) -> p t n", t=LT), dst, ALU.add)\
                        .then_inc(m_free["dve"], 1)

                elif kind == "wtot":
                    w, = a
                    n = TASK[kind, w]
                    g = gam[:, w:w + 1]
                    dve.wait_ge(m_full, n + 1)
                    v.tensor_reduce(g, M[n % 2][:, 0:4], AX.X, ALU.add).then_inc(m_free["dve"], 1)
                    emptied(dve, n)
                    own.done(v.tensor_scalar(g, g, 1.0 / (DM * FF), None, ALU.mult))
                    own.settle()
                    own.done(v.tensor_scalar(thr[:, w:w + 1], g, EPS_Q, 0.5, ALU.add, ALU.mult))
                    own.done(v.tensor_scalar(nthr[:, w:w + 1], g, EPS_Q, -0.5, ALU.add, ALU.mult))
                    own.done(v.tensor_scalar(gam_q[:, w:w + 1], g, 1.0 / Q_B, None, ALU.mult))
                    own.settle()
                elif kind == "tern":
                    w, c = a
                    n = 4 * w + c
                    dst = (t_fc[:, c, :], t_pr[:, 4 * c:4 * c + 4, :].rearrange("p a n -> p (a n)"))[w]
                    if n:
                        dve.wait_ge(tern_done, 2 * n)
                    v.tensor_scalar(low[:], raw[w][:, c, :], nthr[:, w:w + 1], None, ALU.is_lt).then_inc(tern_done, 1)
                    dve.wait_ge(tern_done, 2 * n + 1)
                    v.scalar_tensor_tensor(out=dst, in0=raw[w][:, c, :], scalar=thr[:, w:w + 1], in1=low[:],
                                           op0=ALU.is_gt, op1=ALU.subtract).then_inc(tern_done, 1)
                elif kind == "xa":
                    t, = a
                    f = fx[:, t % 4]
                    dve.wait_ge(xf_in[t % XF], 16 * (t // XF + 1))
                    own.settle()
                    own.done(v.bn_stats(st_x[:, t % 2], xf[:, t % XF, :]))
                    own.settle()
                    own.done(v.bn_aggr(f[:, 0:2], st_x[:, t % 2]))
                    own.settle()
                    v.tensor_scalar(f[:, 4:5], f[:, 1:2], EPS, None, ALU.add).then_inc(fx_var, 1)
                elif kind == "xb":
                    t, = a
                    f = fx[:, t % 4]
                    dve.wait_ge(fx_pow, 2 * t + 1)
                    own.done(v.tensor_scalar(f[:, 6:7], f[:, 1:2], f[:, 2:3], f[:, 2:3], ALU.mult, ALU.mult))
                    own.settle()
                    v.tensor_scalar(f[:, 5:6], f[:, 6:7], EPS_Q, None, ALU.add).then_inc(fx_var, 1)
                elif kind == "xc":
                    t, = a
                    f, x = fx[:, t % 4], xq[:, t % 2, :]
                    dve.wait_ge(fx_pow, 2 * t + 2)
                    own.done(v.tensor_scalar(f[:, 7:8], f[:, 2:3], f[:, 3:4], None, ALU.mult))
                    own.settle()
                    if t >= 2:
                        dve.wait_ge(tr_full, TURN["xt", t - 2] + 1)
                    else:
                        slots_over(dve)
                    own.done(v.tensor_scalar(x, xf[:, t % XF, :], f[:, 0:1], f[:, 7:8], ALU.subtract, ALU.mult))
                    own.settle()
                    own.done(v.tensor_reduce(f[:, 8:9], x, AX.X, ALU.max, apply_absolute_value=True))
                    own.settle()
                    scales(f, 0)
                    v.tensor_scalar(x, x, f[:, 10:11], Q_B, ALU.mult, ALU.min).then_inc(xq_done, 1)
                elif kind in ("xt", "ht"):
                    t = a[0]
                    tr = TURN[(kind, *a)]
                    if kind == "xt":
                        hi, dst = xq_hi[:, t % 2], xq_lo[:, t % 2]
                        if t >= 2:
                            dve.wait_ge(fc_full, 4 * (t - 1))
                    else:
                        part = slice(4 * a[1], 4 * a[1] + 4)
                        hi, dst = hq_hi[:, part], hq_lo[:, part]
                        if t:
                            dve.wait_ge(proj_full, t)
                    dve.wait_ge(tr_hi, tr + 1)
                    v.scalar_tensor_tensor(out=dst, in0=TR[tr % 2].rearrange("p (k n) -> p k n", n=P), scalar=-Q_B,
                                           in1=hi.bitcast(F32), op0=ALU.max, op1=ALU.subtract).then_inc(tr_free, 1)
                elif kind == "fc":
                    t, n = a
                    dve.wait_ge(gelu_done, 4 * t + n + 1)
                    own.done(v.bn_stats(st_h[:, t % 2, n], h_sb[:, t % 2, 512 * n:512 * n + 512]))
                elif kind == "hstat":
                    t, = a
                    f = fh[:, t % 4]
                    own.settle()
                    own.done(v.bn_aggr(f[:, 0:2], st_h[:, t % 2]))
                    own.settle()
                    v.tensor_scalar(f[:, 4:5], f[:, 1:2], EPS_Q, None, ALU.add).then_inc(fh_var, 1)
                elif kind == "hnmr":
                    t, = a
                    f = fh[:, t % 4]
                    dve.wait_ge(fh_pow, t + 1)
                    v.tensor_scalar(f[:, 3:4], f[:, 0:1], f[:, 2:3], -1.0, ALU.mult, ALU.mult).then_inc(fh_nmr, 1)
                elif kind == "hn":
                    t, h = a
                    dve.wait_ge(hn_done, 2 * t + h + 1)
                    own.done(v.tensor_reduce(fh[:, t % 4, 14 + h:15 + h], h_sb[:, t % 2, FF // 2 * h:FF // 2 * (h + 1)],
                                             AX.X, ALU.max, apply_absolute_value=True))
                elif kind == "hscale":
                    t, = a
                    f = fh[:, t % 4]
                    own.settle()
                    own.done(v.tensor_scalar(f[:, 8:9], f[:, 14:15], f[:, 15:16], None, ALU.max))
                    own.settle()
                    scales(f, 1)
                elif kind == "hq":
                    t, h = a
                    half = h_sb[:, t % 2, FF // 2 * h:FF // 2 * (h + 1)]
                    v.tensor_scalar(half, half, fh[:, t % 4, 10:11], Q_B, ALU.mult, ALU.min).then_inc(hq_done, 1)
                elif kind == "proj":
                    t, = a
                    dve.wait_ge(proj_full, t + 1)
                    if t >= 2:
                        dve.wait_ge(y_stored[t % 2], 16 * (t // 2))
                    v.scalar_tensor_tensor(out=y_out[:, t % 2, :], in0=DOWN[t % 2], scalar=fh[:, t % 4, 12:13],
                                           in1=xf[:, t % XF, :], op0=ALU.mult, op1=ALU.add).then_inc(y_ready, 1)


def constants():
    import numpy as np

    pos = np.arange(L, dtype=np.float32)
    inv = (1.0 / np.float32(10000.0) ** (np.arange(0, HD, 2, dtype=np.float32) / np.float32(HD))).astype(np.float32)
    angle = np.tile((inv[:, None] * pos[None, :]).astype(np.float32), (P // HALF, 1))
    pick = np.zeros((2, 2, P), np.float32)
    pick[0, 0] = pick[1, 1] = 1.0
    return {
        "cos": np.cos(angle).astype(np.float32), "sin": np.sin(angle).astype(np.float32),
        "ident": np.eye(P, dtype=np.float32), "pick": pick,
    }


def kernel(**inputs):
    import numpy as np
    import concourse.bacc as bacc
    from concourse.bass_utils import run_bass_kernel_spmd

    a = {k: np.ascontiguousarray(v) for k, v in inputs.items()}

    def rows(w):
        return w.reshape(w.shape[0] // P, P, w.shape[1]).transpose(1, 0, 2)

    w = a["L0_attn_w_qkv"].reshape(DM, 3, NH, 2, HALF)
    chunks = []
    for half in range(2):
        for which in range(2):
            part = w[:, which, 8 * half:8 * half + 8]
            chunks.append(rows(part.transpose(0, 2, 1, 3).reshape(DM, CH)))
    wv = a["L0_attn_w_qkv"][:, 2 * DM:]
    for m in (wv, a["L0_attn_w_o"]):
        for c in range(2):
            chunks.append(rows(m[:, CH * c:CH * c + CH]))

    def cols(m):
        return m.reshape(ET, P, -1).transpose(1, 0, 2)

    arrays = {
        "x": a["x"].reshape(B, LT, P, DM),
        "ctx": a["ctx_1024"].transpose(0, 2, 1).reshape(B, KC, P, L).transpose(0, 2, 1, 3),
        "w_attn": np.stack(chunks),
        "in_w": rows(a["L0_xattn_in_proj_w"].T),
        "xp_w": rows(a["L0_xattn_x_proj_w"].T),
        "dt_w": a["L0_xattn_dt_proj_w"].T,
        "small": np.concatenate([cols(a["L0_xattn_conv_w"]), cols(a["L0_xattn_conv_b"]),
                                 cols(a["L0_xattn_dt_proj_b"]), cols(a["L0_xattn_D"]),
                                 cols(a["L0_xattn_A_log"])], axis=2),
        "w_fc": rows(a["L0_ffn_w_fc"].T).reshape(P, KD * FF),
        "w_pr": rows(a["L0_ffn_w_proj"].T).reshape(P, FT * DM),
        **constants(),
    }
    arrays = {f"in_{k}": np.ascontiguousarray(v) for k, v in arrays.items()}
    nc = bacc.Bacc("TRN2", target_bir_lowering=False, num_devices=1)
    t_in = {k[3:]: nc.dram_tensor(k, v.shape, mybir.dt.from_np(v.dtype), kind="ExternalInput").ap()
            for k, v in arrays.items()}
    out = nc.dram_tensor("out_y", (B, LT, P, DM), F32, kind="ExternalOutput").ap()
    layer_kernel(nc, t_in, out)
    r = run_bass_kernel_spmd(nc, [arrays], core_ids=[0])
    return r.results[0]["out_y"].reshape(B, L, DM)
```
